# Optimizing a Trainium2 kernel written in Bass

```python
import numpy as np
import jax
import jax.numpy as jnp

def _softmax(x, axis=-1):
    return jax.nn.softmax(x, axis=axis)

def _gelu(x):
    return jax.nn.gelu(x, approximate=True)

def _silu(x):
    return jax.nn.silu(x)

def _sigmoid(x):
    return jax.nn.sigmoid(x)

def _layernorm(x, axis=-1, eps=1e-05):
    m = jnp.mean(x, axis=axis, keepdims=True)
    v = jnp.var(x, axis=axis, keepdims=True)
    return (x - m) / jnp.sqrt(v + eps)

def _scatter_add(tgt, idx, src, axis=0):
    return tgt.at[idx].add(src)

def _segment_sum(src, seg, n):
    return jax.ops.segment_sum(src, seg, n)
kernel_name = 'mk_metaformer_d1_conv_nchw768_r4_93a065'

def setup_inputs(seed: int=0):
    np.random.seed(seed)
    _w = jnp.asarray

    def _rec_inputs():
        import jax
        import jax.numpy as jnp
        _gk = jax.random.key(seed)
        x = -0.0002221 + 1 * jax.random.normal(jax.random.fold_in(_gk, 1), (8, 192, 16, 16), jnp.float32)
        return x
    x = _rec_inputs()

    def _L0_conv_setup():
        import jax, jax.numpy as jnp
        import numpy as np
        CHUNK = 16

        def l2norm(x, eps=1e-06):
            return x * jax.lax.rsqrt(jnp.sum(x * x, axis=-1, keepdims=True) + eps)

        def delta_rule_chunked(q, k, v, beta):
            B, H, L, D = q.shape
            n = L // CHUNK

            def to_chunks(t):
                return jnp.moveaxis(t.reshape(B, H, n, CHUNK, *(t.shape[4:] if t.ndim > 4 else ())) if False else t.reshape(B, H, n, CHUNK, -1) if t.ndim == 4 else t.reshape(B, H, n, CHUNK), 2, 0)
            qc = jnp.moveaxis(q.reshape(B, H, n, CHUNK, D), 2, 0)
            kc = jnp.moveaxis(k.reshape(B, H, n, CHUNK, D), 2, 0)
            vc = jnp.moveaxis(v.reshape(B, H, n, CHUNK, D), 2, 0)
            bc = jnp.moveaxis(beta.reshape(B, H, n, CHUNK), 2, 0)
            strict = jnp.tril(jnp.ones((CHUNK, CHUNK), bool), -1)
            incl = jnp.tril(jnp.ones((CHUNK, CHUNK), bool))
            eye = jnp.eye(CHUNK, dtype=q.dtype)

            def step(S, inp):
                qi, ki, vi, bi = inp
                kk = jnp.einsum('bhid,bhjd->bhij', ki, ki)
                T = eye + jnp.where(strict, bi[..., :, None] * kk, 0.0)
                rhs = bi[..., None] * (vi - jnp.einsum('bhcd,bhde->bhce', ki, S))
                U = jax.scipy.linalg.solve_triangular(T, rhs, lower=True)
                qk = jnp.einsum('bhid,bhjd->bhij', qi, ki)
                O = jnp.einsum('bhcd,bhde->bhce', qi, S) + jnp.einsum('bhij,bhje->bhie', jnp.where(incl, qk, 0.0), U)
                S_new = S + jnp.einsum('bhcd,bhce->bhde', ki, U)
                return (S_new, O)
            S0 = jnp.zeros((B, H, D, D), q.dtype)
            _, O = jax.lax.scan(step, S0, (qc, kc, vc, bc))
            return jnp.moveaxis(O, 0, 2).reshape(B, H, L, D)
        key = jax.random.key(seed)
        ks = jax.random.split(key, 7)
        B, C, Hh, Ww = (8, 192, 16, 16)
        n_heads = 12
        s = 1.0 / np.sqrt(C)
        x = jax.random.normal(ks[0], (B, C, Hh, Ww), jnp.float32)
        Wq = jax.random.normal(ks[1], (C, C), jnp.float32) * s
        Wk = jax.random.normal(ks[2], (C, C), jnp.float32) * s
        Wv = jax.random.normal(ks[3], (C, C), jnp.float32) * s
        Wb = jax.random.normal(ks[4], (C, n_heads), jnp.float32) * s
        Wo = jax.random.normal(ks[5], (C, C), jnp.float32) * s
        return {'x': x, 'Wq': Wq, 'Wk': Wk, 'Wv': Wv, 'Wb': Wb, 'Wo': Wo}
    _L0_conv_all = _L0_conv_setup()
    _L0_conv_in = {k: v for k, v in _L0_conv_all.items() if k in ('Wq', 'Wk', 'Wv', 'Wb', 'Wo')}
    del _L0_conv_all

    def _L0_ffn_setup():
        import jax, jax.numpy as jnp
        import numpy as np
        N_EMBD = 192
        HIDDEN = 4 * N_EMBD
        N_EXPERTS = 8
        TOP_K = 2
        key = jax.random.key(seed)
        ks = jax.random.split(key, 4)
        B, T, C, E, H = (4, 512, N_EMBD, N_EXPERTS, HIDDEN)
        x = jax.random.normal(ks[0], (B, T, C), dtype=jnp.float32)
        gate_w = jax.random.normal(ks[1], (E, C), dtype=jnp.float32) * 0.02
        gate_b = jnp.zeros((E,), dtype=jnp.float32)
        w_fc = jax.random.normal(ks[2], (E, H, C), dtype=jnp.float32) * 0.02
        b_fc = jnp.zeros((E, H), dtype=jnp.float32)
        w_proj = jax.random.normal(ks[3], (E, C, H), dtype=jnp.float32) * 0.02
        b_proj = jnp.zeros((E, C), dtype=jnp.float32)
        return {'x': x, 'gate_w': gate_w, 'gate_b': gate_b, 'w_fc': w_fc, 'b_fc': b_fc, 'w_proj': w_proj, 'b_proj': b_proj}
    _L0_ffn_all = _L0_ffn_setup()
    _L0_ffn_in = {k: v for k, v in _L0_ffn_all.items() if k in ('gate_w', 'gate_b', 'w_fc', 'b_fc', 'w_proj', 'b_proj')}
    del _L0_ffn_all
    return {'x': x, 'L0_conv_Wq': _L0_conv_in['Wq'], 'L0_conv_Wk': _L0_conv_in['Wk'], 'L0_conv_Wv': _L0_conv_in['Wv'], 'L0_conv_Wb': _L0_conv_in['Wb'], 'L0_conv_Wo': _L0_conv_in['Wo'], 'L0_ffn_gate_w': _L0_ffn_in['gate_w'], 'L0_ffn_gate_b': _L0_ffn_in['gate_b'], 'L0_ffn_w_fc': _L0_ffn_in['w_fc'], 'L0_ffn_b_fc': _L0_ffn_in['b_fc'], 'L0_ffn_w_proj': _L0_ffn_in['w_proj'], 'L0_ffn_b_proj': _L0_ffn_in['b_proj']}

def reference(x, L0_conv_Wq, L0_conv_Wk, L0_conv_Wv, L0_conv_Wb, L0_conv_Wo, L0_ffn_gate_w, L0_ffn_gate_b, L0_ffn_w_fc, L0_ffn_b_fc, L0_ffn_w_proj, L0_ffn_b_proj):
    import jax
    import jax.numpy as jnp

    def _L0_conv_ref(x, Wq, Wk, Wv, Wb, Wo):
        import jax, jax.numpy as jnp
        import numpy as np
        CHUNK = 16

        def l2norm(x, eps=1e-06):
            return x * jax.lax.rsqrt(jnp.sum(x * x, axis=-1, keepdims=True) + eps)

        def delta_rule_chunked(q, k, v, beta):
            B, H, L, D = q.shape
            n = L // CHUNK

            def to_chunks(t):
                return jnp.moveaxis(t.reshape(B, H, n, CHUNK, *(t.shape[4:] if t.ndim > 4 else ())) if False else t.reshape(B, H, n, CHUNK, -1) if t.ndim == 4 else t.reshape(B, H, n, CHUNK), 2, 0)
            qc = jnp.moveaxis(q.reshape(B, H, n, CHUNK, D), 2, 0)
            kc = jnp.moveaxis(k.reshape(B, H, n, CHUNK, D), 2, 0)
            vc = jnp.moveaxis(v.reshape(B, H, n, CHUNK, D), 2, 0)
            bc = jnp.moveaxis(beta.reshape(B, H, n, CHUNK), 2, 0)
            strict = jnp.tril(jnp.ones((CHUNK, CHUNK), bool), -1)
            incl = jnp.tril(jnp.ones((CHUNK, CHUNK), bool))
            eye = jnp.eye(CHUNK, dtype=q.dtype)

            def step(S, inp):
                qi, ki, vi, bi = inp
                kk = jnp.einsum('bhid,bhjd->bhij', ki, ki)
                T = eye + jnp.where(strict, bi[..., :, None] * kk, 0.0)
                rhs = bi[..., None] * (vi - jnp.einsum('bhcd,bhde->bhce', ki, S))
                U = jax.scipy.linalg.solve_triangular(T, rhs, lower=True)
                qk = jnp.einsum('bhid,bhjd->bhij', qi, ki)
                O = jnp.einsum('bhcd,bhde->bhce', qi, S) + jnp.einsum('bhij,bhje->bhie', jnp.where(incl, qk, 0.0), U)
                S_new = S + jnp.einsum('bhcd,bhce->bhde', ki, U)
                return (S_new, O)
            S0 = jnp.zeros((B, H, D, D), q.dtype)
            _, O = jax.lax.scan(step, S0, (qc, kc, vc, bc))
            return jnp.moveaxis(O, 0, 2).reshape(B, H, L, D)
        B, C, Hh, Ww = x.shape
        L = Hh * Ww
        n_heads = Wb.shape[1]
        D = C // n_heads
        t = x.reshape(B, C, L).transpose(0, 2, 1)

        def heads(z):
            return z.reshape(B, L, n_heads, D).transpose(0, 2, 1, 3)
        q = l2norm(heads(jax.nn.silu(t @ Wq)))
        k = l2norm(heads(jax.nn.silu(t @ Wk)))
        v = heads(jax.nn.silu(t @ Wv))
        beta = jax.nn.sigmoid(t @ Wb).transpose(0, 2, 1)
        o = delta_rule_chunked(q, k, v, beta)
        o = o.transpose(0, 2, 1, 3).reshape(B, L, C)
        y = o @ Wo
        out = t + y
        return out.transpose(0, 2, 1).reshape(B, C, Hh, Ww)

    def _L0_ffn_ref(x, gate_w, gate_b, w_fc, b_fc, w_proj, b_proj):
        import jax, jax.numpy as jnp
        import numpy as np
        N_EMBD = 192
        HIDDEN = 4 * N_EMBD
        N_EXPERTS = 8
        TOP_K = 2
        B, T, C = x.shape
        E = gate_b.shape[0]
        xf = x.reshape(-1, C)
        scores = xf @ gate_w.T + gate_b
        top_s, top_i = jax.lax.top_k(scores, TOP_K)
        gates = jax.nn.softmax(top_s, axis=-1)
        comb = jnp.sum(jax.nn.one_hot(top_i, E, dtype=xf.dtype) * gates[..., None], axis=1)
        out = jnp.zeros_like(xf)
        for j in range(E):
            h = jax.nn.gelu(xf @ w_fc[j].T + b_fc[j], approximate=True)
            y = h @ w_proj[j].T + b_proj[j]
            out = out + comb[:, j:j + 1] * y
        return out.reshape(B, T, C)

    def _gn(v, G=32, eps=1e-05):
        B_, C_, H_, W_ = v.shape
        g = v.reshape(B_, G, C_ // G, H_, W_)
        m = jnp.mean(g, axis=(2, 3, 4), keepdims=True)
        s = jnp.var(g, axis=(2, 3, 4), keepdims=True)
        return ((g - m) / jnp.sqrt(s + eps)).reshape(v.shape)

    def _ln_c(v, eps=1e-06):
        m = jnp.mean(v, axis=1, keepdims=True)
        s = jnp.var(v, axis=1, keepdims=True)
        return (v - m) / jnp.sqrt(s + eps)

    def _ln_t(v, eps=1e-05):
        m = jnp.mean(v, axis=-1, keepdims=True)
        s = jnp.var(v, axis=-1, keepdims=True)
        return (v - m) / jnp.sqrt(s + eps)

    def _to_tokens(v):
        B_, C_, H_, W_ = v.shape
        return v.reshape(B_, C_, H_ * W_).transpose(0, 2, 1)

    def _from_tokens(t, like):
        B_, C_, H_, W_ = like.shape
        return t.transpose(0, 2, 1).reshape(B_, C_, H_, W_)
    x = x + _L0_conv_ref(_ln_c(x), L0_conv_Wq, L0_conv_Wk, L0_conv_Wv, L0_conv_Wb, L0_conv_Wo)
    t = _to_tokens(x)
    t = t + _L0_ffn_ref(_ln_t(t), L0_ffn_gate_w, L0_ffn_gate_b, L0_ffn_w_fc, L0_ffn_b_fc, L0_ffn_w_proj, L0_ffn_b_proj)
    x = _from_tokens(t, x)
    return x

_drawn_inputs = setup_inputs


def setup_inputs(seed=0):
    import zlib

    import numpy as np

    out = dict(_drawn_inputs(seed))
    spreads = {'L0_ffn_gate_b': (0.0, 0.273), 'L0_ffn_b_fc': (0.0, 0.765), 'L0_ffn_b_proj': (0.0, 0.1)}
    factors = {}
    for name, (base, spread) in spreads.items():
        noise = np.random.default_rng([zlib.crc32(name.encode()), seed]).standard_normal(out[name].shape)
        drawn = base * np.exp(spread * noise) if base else spread * noise
        out[name] = jnp.asarray(drawn.astype(out[name].dtype))
    for name, factor in factors.items():
        out[name] = (out[name] * factor).astype(out[name].dtype)
    return out
```

```python
from contextlib import ExitStack

import concourse.bass as bass
from concourse import mybir

B, C, L = 8, 192, 256
TP = 128
NT = B * L // TP
H, D, CH = 12, 16, 16
NC = L // CH
HC = C // 2
KVW = 2 * H * D
QBW = H * D + H
E, HID = 8, 768
HB = HID // 128
ID0, MS0, MU0, MP0, BM0, TB0 = 0, 128, 160, 192, 194, 290
CW = TB0 + E
ONE = 1
WSCALE = 64.0


def program(nc, x, consts, wqkvb, wo, gate, wfc, wproj, bproj, out):
    f32, f16 = mybir.dt.float32, mybir.dt.float16
    ALU, ACT, AX = mybir.AluOpType, mybir.ActivationFunctionType, mybir.AxisListType
    ds = bass.ds
    ctx = ExitStack()
    with ctx:
        def sb(name, shape, dt=f32):
            return ctx.enter_context(nc.sbuf_tensor(name, shape, dt))

        semaphores = []

        def sem(name):
            semaphores.append(ctx.enter_context(nc.semaphore(name)))
            return semaphores[-1]

        def sem2(name):
            return [sem(f"{name}{u}") for u in range(2)]

        def dram(name, shape, dt=f32):
            return nc.dram_tensor(name, shape, dt, kind="Internal").ap()

        d_kv = dram("d_kv", (NT, TP, KVW))
        d_khl = dram("d_khl", (B, NC, CH, 2 * C), f16)
        d_n = dram("d_n", (NT, TP, C))
        d_mt = dram("d_mt", (NT, TP, C))
        d_pt = dram("d_pt", (NT, TP, 2 * C))
        d_ub = dram("d_ub", (B, NC, CH, C))
        d_q = dram("d_q", (NT, TP, C))
        d_w = dram("d_w", (NC, HC, B, 4 * CH))
        d_u = dram("d_u", (2, B, NC, CH, C))

        cst = sb("cst", [128, CW])
        ident = cst[:, ID0:ID0 + 128]
        x_sb = sb("x_sb", [128, NT, C])
        r_sb = sb("r_sb", [128, NT, C])
        st_sb = sb("st_sb", [128, NT, 6])
        mean = sb("mean", [128, NT])
        rstd = sb("rstd", [128, NT])
        tmpa = sb("tmpa", [128, NT])
        tmpb = sb("tmpb", [128, NT])
        eps_c = sb("eps_c", [128, 3])
        beta = sb("beta", [128, NT, H])
        wqkvb_sb = sb("wqkvb_sb", [HC, 2, KVW + QBW])
        wo_sb = sb("wo_sb", [HC, 2, C])
        fch = sb("fch", [HC + 1, 2, E, HID], f16)
        fcl = sb("fcl", [HC + 1, 2, E, HID], f16)
        pjh = sb("pjh", [128, E, HB * C], f16)
        pjl = sb("pjl", [128, E, HB * C], f16)
        fcs = sb("fcs", [HC + 1, 2, HID])
        pjs = sb("pjs", [128, HB * C])

        ps = ctx.enter_context(nc.psum_tensor("ps", [128, 8, 512], f32))

        s_x, s_cst, s_w = sem("s_x"), sem("s_cst"), sem("s_w")
        s_bn, s_mv, s_sq, s_rs = sem("s_bn"), sem("s_mv"), sem("s_sq"), sem("s_rs")
        s_dv = sem("s_dv")
        s_eps = sem("s_eps")

        started = [0]

        def start_at_one(eng):
            for s in semaphores[started[0]:]:
                eng.sem_inc(s, ONE)
            started[0] = len(semaphores)

        def by_constant(eng, *values):
            for value in values:
                eng.compute_val(ONE + value)
            eng.wait_ge(s_cst, ONE + 16)

        def norm_statistics(chain, eps_done):
            me, mo = st_sb[:, :, 1], st_sb[:, :, 4]
            chain(nc.vector.tensor_tensor(mean[:, :], me, mo, ALU.add))
            chain(nc.vector.tensor_scalar(mean[:, :], mean[:, :], 0.5, None, ALU.mult))
            chain(nc.vector.tensor_tensor(tmpa[:, :], me, mean[:, :], ALU.subtract))
            chain(nc.vector.tensor_tensor(tmpa[:, :], tmpa[:, :], tmpa[:, :], ALU.mult))
            chain(nc.vector.tensor_tensor(tmpb[:, :], st_sb[:, :, 2], st_sb[:, :, 5], ALU.add))
            nc.vector.scalar_tensor_tensor(tmpa[:, :], tmpb[:, :], 1.0 / C, tmpa[:, :], ALU.mult, ALU.add)\
                .then_inc(eps_done, 1)

        with ExitStack() as mix:
            def sbm(name, shape, dt=f32):
                return mix.enter_context(nc.sbuf_tensor(name, shape, dt))

            tw = [sbm(f"tw{u}", [128, 2, C]) for u in range(2)]
            tT = [sbm(f"tT{u}", [HC, 2, 2, TP]) for u in range(2)]
            kvw = [sbm(f"kvw{u}", [128, 2, H, 2 * D]) for u in range(2)]
            qw = [sbm(f"qw{u}", [128, 2, H, D]) for u in range(2)]
            qn = [sbm(f"qn{u}", [128, 2, H, 2 * D]) for u in range(2)]
            sqw = [sbm(f"sqw{u}", [128, 2, 2 * H, D]) for u in range(2)]
            ssw = [sbm(f"ssw{u}", [128, 2, 2 * H]) for u in range(2)]
            rnw = [sbm(f"rnw{u}", [128, 2, 2 * H]) for u in range(2)]
            khl = [sbm(f"khl{u}", [128, 2, 2, C], f16) for u in range(2)]
            kqT = [sbm(f"kqT{u}", [128, 3, 2, TP]) for u in range(2)]
            gm = sbm("gm", [128, 3, 4, 2 * CH])
            nw = [sbm(f"nw{u}", [128, 3, 4, CH]) for u in range(2)]
            ptw = [sbm(f"ptw{u}", [128, 3, 4, 2 * CH]) for u in range(2)]
            lane_n = sbm("lane_n", [128, CH, H, CH])
            lane_m = sbm("lane_m", [128, CH, H, CH])
            prod = sbm("prod", [128, CH * H * CH // 2])

            NB2 = B // 2
            TB2 = 10
            GB2 = 4
            t_ready, t_added = sem2("t_ready"), sem2("t_added")
            t_filled, t_evicted = sem("t_filled"), sem2("t_evicted")
            kv_done, qb_done, kv_out, qb_out = sem("kv_done"), sem("qb_done"), sem("kv_out"), sem("qb_out")
            sq_done, ss_done, sn_done = sem2("sq_done"), sem2("ss_done"), sem2("sn_done")
            kn_done, khi_done, klo_done = sem2("kn_done"), sem2("khi_done"), sem2("klo_done")
            g_done, g_out, n_ready = sem2("g_done"), sem("g_out"), sem2("n_ready")
            st_kv, st_k, st_n, st_pt, st_q = (sem2("st_kv"), sem2("st_k"), sem2("st_n"), sem2("st_pt"),
                                              sem2("st_q"))
            s_ch2, pads = sem("s_ch2"), sem("pads")
            ln_ld, inv_done, st_m, s_inv = sem("ln_ld"), sem("inv_done"), sem("st_m"), sem("s_inv")

            with nc.Block() as block:

                @block.sync
                def _(sp):
                    start_at_one(sp)
                    sp.dma_start(x_sb[:, :, :], x.rearrange("p (t c) -> p t c", t=NT)).then_inc(s_x, 16)
                    sp.dma_start(cst[:, :], consts).then_inc(s_cst, 16)
                    sp.dma_start(wqkvb_sb[:, :, :], wqkvb.rearrange("p (a n) -> p a n", a=2)).then_inc(s_w, 16)
                    sp.dma_start(wo_sb[:, :, :], wo.rearrange("p (a n) -> p a n", a=2)).then_inc(s_w, 16)
                    with sp.Fori(0, NB2) as r:
                        for u in range(2):
                            b = 2 * r + u
                            sp.wait_ge(kn_done[u], ONE + r + 1)
                            sp.dma_start(d_kv[ds(2 * b, 2), :, :].rearrange("t p c -> p t c"),
                                         kvw[u][:, :, :, :].rearrange("p t h d -> p t (h d)")).then_inc(st_kv[u], 16)
                            sp.wait_ge(khi_done[u], ONE + r + 1)
                            sp.wait_ge(klo_done[u], ONE + r + 1)
                            for j in range(2):
                                sp.dma_start(d_khl[ds(b, 1), 8 * j:8 * j + 8, :, :].rearrange("b c i w -> (b c i) w"),
                                             khl[u][:, j, :, :].rearrange("p s w -> p (s w)")).then_inc(st_k[u], 16)
                            sp.dma_start(d_q[ds(2 * b, 2), :, :].rearrange("t p c -> p t c"),
                                         qw[u][:, :, :, :].rearrange("p t h d -> p t (h d)")).then_inc(st_q[u], 16)
                            for j in range(2):
                                sp.wait_ge(n_ready[j], ONE + 2 * r + u + 1)
                                sp.dma_start(d_n[ds(2 * b + j, 1), :, :].rearrange("t p c -> (t p) c"),
                                             nw[j][:, :, :, :].rearrange("p a r i -> p (a r i)")).then_inc(st_n[j], 16)
                                sp.dma_start(d_pt[ds(2 * b + j, 1), :, :].rearrange("t p c -> (t p) c"),
                                             ptw[j][:, :, :, :].rearrange("p a r i -> p (a r i)")).then_inc(st_pt[j], 16)
                    for j in range(2):
                        sp.wait_ge(st_n[j], ONE + 16 * B)
                    sp.dma_start(lane_n[:, :, :, :].rearrange("p i h j -> p (i h j)"),
                                 d_n.rearrange("t (c i) w -> (t c) (i w)", i=CH)).then_inc(ln_ld, 16)
                    sp.wait_ge(inv_done, ONE + 1)
                    sp.dma_start(d_mt.rearrange("t (c i) w -> (t c) (i w)", i=CH),
                                 lane_m[:, :, :, :].rearrange("p i h j -> p (i h j)")).then_inc(st_m, 16)
                    sp.wait_ge(st_m, ONE + 16)
                    for u in range(2):
                        sp.wait_ge(st_kv[u], ONE + 16 * NB2)
                        sp.wait_ge(st_k[u], ONE + 32 * NB2)
                        sp.wait_ge(st_pt[u], ONE + 16 * B)
                        sp.wait_ge(st_q[u], ONE + 16 * NB2)

                @block.gpsimd
                def _(pool):
                    nc.gpsimd.memset(eps_c[:, 0:1], 1e-6).then_inc(s_eps, 1)
                    nc.gpsimd.memset(eps_c[:, 1:2], 1e-5).then_inc(s_eps, 1)
                    for u in range(2):
                        nc.gpsimd.memset(qn[u][:, :, :, :], 0.0).then_inc(pads, 1)
                    nc.gpsimd.memset(lane_m[:, :, :, :], 0.0).then_inc(pads, 1)
                    pool.wait_ge(pads, ONE + 3)
                    for j in range(CH):
                        nc.gpsimd.memset(lane_m[:, j, :, j], 1.0).then_inc(pads, 1)
                    with pool.Fori(0, NB2) as r:
                        for u in range(2):
                            b = 2 * r + u
                            pool.wait_ge(t_ready[u], ONE + r + 1)
                            nc.gpsimd.tensor_tensor(r_sb[:, ds(2 * b, 2), :], x_sb[:, ds(2 * b, 2), :],
                                                    tw[u][:, :, :], ALU.add).then_inc(t_added[u], 1)
                        for u in range(2):
                            pool.wait_ge(kv_out, ONE + GB2 * r + 2 * u + 2)
                            pool.wait_ge(qb_out, ONE + GB2 * r + 2 * u + 2)
                            pool.wait_ge(ss_done[u], ONE + r)
                            nc.gpsimd.tensor_tensor(sqw[u][:, :, 0:H, :], kvw[u][:, :, :, 0:D],
                                                    kvw[u][:, :, :, 0:D], ALU.mult).then_inc(sq_done[u], 1)
                            nc.gpsimd.tensor_tensor(sqw[u][:, :, H:2 * H, :], qw[u][:, :, :, :],
                                                    qw[u][:, :, :, :], ALU.mult).then_inc(sq_done[u], 1)
                        for u in range(2):
                            pool.wait_ge(kn_done[u], ONE + r + 1)
                            pool.wait_ge(khi_done[u], ONE + r + 1)
                            nc.gpsimd.tensor_tensor(khl[u][:, :, 1, :].rearrange("p t (h d) -> p t h d", h=H),
                                                    kvw[u][:, :, :, 0:D],
                                                    khl[u][:, :, 0, :].rearrange("p t (h d) -> p t h d", h=H),
                                                    ALU.subtract).then_inc(klo_done[u], 1)

                @block.scalar
                def _(act):
                    act.wait_ge(s_eps, ONE + 2)
                    act.wait_ge(s_mv, ONE + 1)
                    nc.scalar.activation(rstd[:, :], tmpa[:, :], ACT.Sqrt, bias=eps_c[:, 0:1]).then_inc(s_sq, 1)
                    with act.Fori(0, NB2) as r:
                        for u in range(2):
                            act.wait_ge(t_filled, ONE + TB2 * r + u + 1)
                            act.wait_ge(qb_done, ONE + GB2 * r)
                            nc.scalar.activation(tT[u][:, :, :, :].rearrange("p a b n -> p (a b n)"),
                                                 ps[0:HC, u, :], ACT.Copy).then_inc(t_evicted[u], 1)
                        for u in range(2):
                            for j in range(2):
                                n = GB2 * r + 2 * u + j
                                act.wait_ge(kv_done, ONE + n + 1)
                                if j == 0:
                                    act.wait_ge(st_kv[u], ONE + 16 * r)
                                    act.wait_ge(klo_done[u], ONE + r)
                                    act.wait_ge(g_done[1], ONE + 2 * r)
                                nc.scalar.activation(kvw[u][:, j, :, :].rearrange("p h d -> p (h d)"),
                                                     ps[:, 2, 0:KVW], ACT.Silu).then_inc(kv_out, 1)
                                act.wait_ge(qb_done, ONE + n + 1)
                                if j == 0:
                                    act.wait_ge(kn_done[u], ONE + r)
                                    act.wait_ge(st_q[u], ONE + 16 * r)
                                nc.scalar.activation(qw[u][:, j, :, :].rearrange("p h d -> p (h d)"),
                                                     ps[:, 3, 0:C], ACT.Silu)
                                nc.scalar.activation(beta[:, ds(n, 1), :].rearrange("p t h -> p (t h)"),
                                                     ps[:, 3, C:QBW], ACT.Tanh, scale=0.5).then_inc(qb_out, 1)
                        for u in range(2):
                            act.wait_ge(ss_done[u], ONE + r + 1)
                            nc.scalar.activation(rnw[u][:, :, :], ssw[u][:, :, :], ACT.Sqrt, bias=eps_c[:, 0:1])\
                                .then_inc(sn_done[u], 1)
                        for u in range(2):
                            act.wait_ge(kn_done[u], ONE + r + 1)
                            act.wait_ge(st_k[u], ONE + 32 * r)
                            nc.scalar.activation(khl[u][:, :, 0, :].rearrange("p t (h d) -> p t h d", h=H),
                                                 kvw[u][:, :, :, 0:D], ACT.Copy).then_inc(khi_done[u], 1)
                            for j in range(2):
                                idx = 2 + 2 * (2 * u + j)
                                act.wait_ge(g_done[j], ONE + 2 * r + u)
                                for k in range(2):
                                    bank = (idx + k) % 2
                                    act.wait_ge(t_filled, ONE + TB2 * r + idx + k + 1)
                                    nc.scalar.activation(kqT[j][:, :, k, :],
                                                         ps[:, bank, 0:3 * TP].rearrange("p (a n) -> p a n", a=3),
                                                         ACT.Copy).then_inc(t_evicted[bank], 1)

                @block.vector
                def _(dve):
                    dve.wait_ge(s_x, ONE + 16)
                    for t in range(NT):
                        last = nc.vector.bn_stats(st_sb[:, t, :], x_sb[:, t, :])
                    last.then_inc(s_bn, 1)
                    dve.wait_ge(s_bn, ONE + 1)
                    count = [0]

                    def chain(ins):
                        count[0] += 1
                        ins.then_inc(s_dv, 1)
                        dve.wait_ge(s_dv, ONE + count[0])

                    norm_statistics(chain, s_mv)
                    dve.wait_ge(s_sq, ONE + 1)
                    nc.vector.reciprocal(rstd[:, :], rstd[:, :]).then_inc(s_rs, 1)
                    dve.wait_ge(s_rs, ONE + 1)
                    dve.wait_ge(s_cst, ONE + 16)
                    dve.wait_ge(pads, ONE + 3 + CH)
                    LINKS = 10
                    with dve.Fori(0, NB2) as r:
                        k = 0

                        for u in range(2):
                            b = 2 * r + u
                            dve.wait_ge(t_filled, ONE + TB2 * r)
                            dve.wait_ge(t_added[u], ONE + r)
                            for j in range(2):
                                last = nc.vector.tensor_scalar(tw[u][:, j, :],
                                                               x_sb[:, ds(2 * b + j, 1), :].rearrange("p t c -> p (t c)"),
                                                               mean[:, ds(2 * b + j, 1)], rstd[:, ds(2 * b + j, 1)],
                                                               ALU.subtract, ALU.mult)
                            last.then_inc(t_ready[u], 1)
                        for u in range(2):
                            b = 2 * r + u
                            dve.wait_ge(sq_done[u], ONE + 2 * r + 2)
                            nc.vector.tensor_reduce(ssw[u][:, :, :], sqw[u][:, :, :, :], AX.X, ALU.add)\
                                .then_inc(ss_done[u], 1)
                            k += 1
                            nc.vector.tensor_scalar(beta[:, ds(2 * b, 2), :], beta[:, ds(2 * b, 2), :], 0.5, 0.5,
                                                    ALU.mult, ALU.add).then_inc(s_ch2, 1)
                            dve.wait_ge(s_ch2, ONE + LINKS * r + k)
                        for u in range(2):
                            dve.wait_ge(sn_done[u], ONE + r + 1)
                            dve.wait_ge(g_done[1], ONE + 2 * r)
                            k += 1
                            nc.vector.reciprocal(rnw[u][:, :, :], rnw[u][:, :, :]).then_inc(s_ch2, 1)
                            dve.wait_ge(s_ch2, ONE + LINKS * r + k)
                            nc.vector.tensor_tensor(kvw[u][:, :, :, 0:D], kvw[u][:, :, :, 0:D],
                                                    rnw[u][:, :, 0:H].unsqueeze(3).broadcast_to([128, 2, H, D]), ALU.mult)
                            nc.vector.tensor_tensor(qw[u][:, :, :, :], qw[u][:, :, :, :],
                                                    rnw[u][:, :, H:2 * H].unsqueeze(3).broadcast_to([128, 2, H, D]), ALU.mult)\
                                .then_inc(s_ch2, 1)
                            k += 1
                            dve.wait_ge(s_ch2, ONE + LINKS * r + k)
                            nc.vector.tensor_copy(qn[u][:, :, :, 0:D], qw[u][:, :, :, :]).then_inc(kn_done[u], 1)
                        for u in range(2):
                            for j in range(2):
                                n = GB2 * r + 2 * u + j
                                m = 2 * r + u
                                scores = ps[:, 4:8, 0:3 * 64].rearrange("p r (a s i) -> p a r s i", a=3, s=2)
                                dve.wait_ge(g_done[j], ONE + m + 1)
                                dve.wait_ge(st_pt[j], ONE + 16 * m)
                                dve.wait_ge(st_n[j], ONE + 16 * m)
                                nc.vector.tensor_tensor(
                                    ptw[j][:, :, :, :], scores[:, :, :, 1, :],
                                    cst[:, MU0:MU0 + 32].unsqueeze(1).unsqueeze(1).broadcast_to([128, 3, 4, 32]), ALU.mult)
                                k += 1
                                nc.vector.tensor_tensor(
                                    gm[:, :, :, :], scores[:, :, :, 0, :],
                                    cst[:, MS0:MS0 + 32].unsqueeze(1).unsqueeze(1).broadcast_to([128, 3, 4, 32]), ALU.mult)\
                                    .then_inc(g_out, 1)
                                dve.wait_ge(g_out, ONE + n + 1)
                                nc.vector.tensor_tensor(nw[j][:, :, :, :], gm[:, :, :, 0:CH], gm[:, :, :, CH:2 * CH], ALU.add)\
                                    .then_inc(s_ch2, 1)
                                dve.wait_ge(s_ch2, ONE + LINKS * r + k)
                                nc.vector.tensor_tensor(
                                    nw[j][:, :, :, :].rearrange("p a r i -> p (a r) i"),
                                    nw[j][:, :, :, :].rearrange("p a r i -> p (a r) i"),
                                    beta[:, ds(n, 1), :].rearrange("p t h -> p (t h)").unsqueeze(2).broadcast_to([128, H, CH]),
                                    ALU.mult).then_inc(n_ready[j], 1)
                        assert k == LINKS
                    dve.wait_ge(ln_ld, ONE + 16)
                    step = 0
                    for m in range(CH - 1):
                        rows, w = CH - 1 - m, m + 1
                        pr = prod[:, 0:rows * H * w].rearrange("p (i h j) -> p i h j", i=rows, h=H)
                        below = lane_m[:, 0:w, :, m + 1:CH].rearrange("p j h i -> p i h j")
                        nc.vector.tensor_tensor(
                            pr, lane_n[:, m + 1:CH, :, m].unsqueeze(3).broadcast_to([128, rows, H, w]),
                            lane_m[:, 0:w, :, m].rearrange("p j h -> p h j").unsqueeze(1).broadcast_to([128, rows, H, w]),
                            ALU.mult).then_inc(s_inv, 1)
                        step += 1
                        dve.wait_ge(s_inv, ONE + step)
                        last = nc.vector.tensor_tensor(below, below, pr, ALU.subtract)
                        if m == CH - 2:
                            last.then_inc(inv_done, 1)
                        else:
                            last.then_inc(s_inv, 1)
                            step += 1
                            dve.wait_ge(s_inv, ONE + step)

                @block.tensor
                def _(pe):
                    pe.wait_ge(s_cst, ONE + 16)
                    pe.wait_ge(s_w, ONE + 32)
                    pe.wait_ge(pads, ONE + 3)
                    with pe.Fori(0, NB2) as r:
                        for u in range(2):
                            pe.wait_ge(t_ready[u], ONE + r + 1)
                            pe.wait_ge(t_evicted[u], ONE + TB2 // 2 * r)
                            for j in range(2):
                                for hf in range(2):
                                    q = 2 * j + hf
                                    last = nc.tensor.transpose(ps[0:HC, u, q * TP:(q + 1) * TP],
                                                               tw[u][:, j, hf * HC:(hf + 1) * HC], ident)
                            last.then_inc(t_filled, 1)
                        for u in range(2):
                            pe.wait_ge(t_evicted[u], ONE + TB2 // 2 * r + 1)
                            for j in range(2):
                                n = GB2 * r + 2 * u + j
                                pe.wait_ge(kv_out, ONE + n)
                                for hf in range(2):
                                    last = nc.tensor.matmul(ps[:, 2, 0:KVW], tT[u][:, j, hf, :], wqkvb_sb[:, hf, 0:KVW],
                                                            start=(hf == 0), stop=(hf == 1))
                                last.then_inc(kv_done, 1)
                                pe.wait_ge(qb_out, ONE + n)
                                for hf in range(2):
                                    last = nc.tensor.matmul(ps[:, 3, 0:QBW], tT[u][:, j, hf, :],
                                                            wqkvb_sb[:, hf, KVW:KVW + QBW],
                                                            start=(hf == 0), stop=(hf == 1))
                                last.then_inc(qb_done, 1)
                        for u in range(2):
                            pe.wait_ge(kn_done[u], ONE + r + 1)
                            for j in range(2):
                                idx = 2 + 2 * (2 * u + j)
                                n = GB2 * r + 2 * u + j
                                for k, src in enumerate((kvw[u], qn[u])):
                                    bank = (idx + k) % 2
                                    pe.wait_ge(t_evicted[bank], ONE + TB2 // 2 * r + (idx + k) // 2)
                                    for a in range(3):
                                        last = nc.tensor.transpose(
                                            ps[:, bank, a * TP:(a + 1) * TP],
                                            src[:, j, 4 * a:4 * a + 4, :].rearrange("p h d -> p (h d)"), ident)
                                    last.then_inc(t_filled, 1)
                                by_constant(pe, TB2 // 2 * r + idx // 2 + 1, TB2 // 2 * r + (idx + 1) // 2 + 1, n)
                                pe.wait_ge(t_evicted[idx % 2], ONE + TB2 // 2 * r + idx // 2 + 1)
                                pe.wait_ge(t_evicted[(idx + 1) % 2], ONE + TB2 // 2 * r + (idx + 1) // 2 + 1)
                                pe.wait_ge(g_out, ONE + n)
                                for a in range(3):
                                    for g in range(4):
                                        for q in range(4):
                                            rows, cols = slice(32 * q, 32 * q + D), slice(32 * g, 32 * g + 32)
                                            last = nc.tensor.matmul(ps[cols, 4 + q, 64 * a:64 * a + 64],
                                                                    kqT[j][rows, a, 0, cols], kqT[j][rows, a, :, cols],
                                                                    start=True, stop=True)
                                last.then_inc(g_done[j], 1)

        with ExitStack() as wy:
            def sbw(name, shape, dt=f32):
                return wy.enter_context(nc.sbuf_tensor(name, shape, dt))

            mtc = [sbw(f"mtc{u}", [128, H, CH]) for u in range(2)]
            mb = [sbw(f"mb{u}", [128, H, 2, CH]) for u in range(2)]
            kvt = [sbw(f"kvt{u}", [128, H, 2 * D]) for u in range(2)]
            ww = [sbw(f"ww{u}", [128, H, D]) for u in range(2)]
            ubw = [sbw(f"ubw{u}", [128, H, D]) for u in range(2)]
            qt = [sbw(f"qt{u}", [128, C]) for u in range(2)]
            wT = [sbw(f"wT{u}", [HC, 8, 4, CH]) for u in range(2)]
            ld_m, ld_kv, mb_done, x_done, x_out = (sem2("ld_m"), sem2("ld_kv"), sem2("mb_done"), sem2("x_done"),
                                                   sem2("x_out"))
            w_t, w_out, st_ub, st_w, m_beta = sem2("w_t"), sem2("w_out"), sem2("st_ub"), sem2("st_w"), sem2("m_beta")

            with nc.Block() as block:

                @block.sync
                def _(sp):
                    start_at_one(sp)
                    with sp.Fori(0, B) as r:
                        for u in range(2):
                            sp.wait_ge(mb_done[u], ONE + r)
                            sp.dma_start(mtc[u][:, :, :].rearrange("p h i -> p (h i)"),
                                         d_mt[ds(2 * r + u, 1), :, :].rearrange("t p c -> (t p) c")).then_inc(ld_m[u], 16)
                            sp.wait_ge(x_done[u], ONE + r)
                            sp.dma_start(kvt[u][:, :, :].rearrange("p h d -> p (h d)"),
                                         d_kv[ds(2 * r + u, 1), :, :].rearrange("t p c -> (t p) c")).then_inc(ld_kv[u], 16)
                            sp.wait_ge(w_t[u], ONE + r)
                            sp.dma_start(qt[u][:, :], d_q[ds(2 * r + u, 1), :, :].rearrange("t p c -> (t p) c"))\
                                .then_inc(ld_kv[u], 16)

                @block.vector
                def _(dve):
                    with dve.Fori(0, B) as r:
                        for u in range(2):
                            dve.wait_ge(ld_m[u], ONE + 16 * r + 16)
                            nc.vector.tensor_tensor(
                                mtc[u][:, :, :], mtc[u][:, :, :],
                                beta[:, ds(2 * r + u, 1), :].rearrange("p t h -> p (t h)").unsqueeze(2)
                                .broadcast_to([128, H, CH]), ALU.mult).then_inc(m_beta[u], 1)
                            dve.wait_ge(m_beta[u], ONE + r + 1)
                            dve.wait_ge(x_done[u], ONE + r)
                            nc.vector.tensor_tensor(
                                mb[u][:, :, :, :], mtc[u][:, :, :].unsqueeze(2).broadcast_to([128, H, 2, CH]),
                                cst[:, MP0:MP0 + 2].unsqueeze(1).unsqueeze(3).broadcast_to([128, H, 2, CH]), ALU.mult)\
                                .then_inc(mb_done[u], 1)
                        for u in range(2):
                            dve.wait_ge(w_t[u], ONE + r + 1)
                            dve.wait_ge(st_w[u], ONE + 16 * r)
                            nc.vector.tensor_copy(
                                wT[u][:, :, :, :],
                                ps[0:HC, 2 + u, :].rearrange("p (q c i) -> p c q i", q=4, i=CH)).then_inc(w_out[u], 1)

                @block.scalar
                def _(act):
                    with act.Fori(0, B) as r:
                        for u in range(2):
                            both = ps[:, u, 0:KVW].rearrange("p (h s d) -> p s h d", h=H, s=2)
                            act.wait_ge(x_done[u], ONE + r + 1)
                            act.wait_ge(w_t[u], ONE + r)
                            nc.scalar.activation(ww[u][:, :, :], both[:, 0, :, :], ACT.Copy)
                            act.wait_ge(st_ub[u], ONE + 16 * r)
                            nc.scalar.activation(ubw[u][:, :, :], both[:, 1, :, :], ACT.Copy).then_inc(x_out[u], 1)
                            act.wait_ge(x_out[u], ONE + r + 1)
                            act.dma_start(d_ub[ds(r, 1), 8 * u:8 * u + 8, :, :].rearrange("b c i w -> (b c i) w"),
                                          ubw[u][:, :, :].rearrange("p h d -> p (h d)")).then_inc(st_ub[u], 16)
                        for u in range(2):
                            act.wait_ge(w_out[u], ONE + r + 1)
                            act.dma_start(d_w[8 * u:8 * u + 8, :, ds(r, 1), :].rearrange("c p b w -> p c (b w)"),
                                          wT[u][:, :, :, :].rearrange("p c q i -> p c (q i)")).then_inc(st_w[u], 16)
                    for u in range(2):
                        act.wait_ge(st_ub[u], ONE + 16 * B)
                        act.wait_ge(st_w[u], ONE + 16 * B)

                @block.tensor
                def _(pe):
                    with pe.Fori(0, B) as r:
                        for u in range(2):
                            by_constant(pe, r + 1, 32 * r + 32, r)
                            pe.wait_ge(mb_done[u], ONE + r + 1)
                            pe.wait_ge(ld_kv[u], ONE + 32 * r + 32)
                            pe.wait_ge(x_out[u], ONE + r)
                            for h in range(H):
                                for g in range(4):
                                    rows = slice(32 * g, 32 * g + 32)
                                    last = nc.tensor.matmul(ps[rows, u, 32 * h:32 * h + 32],
                                                            mb[u][rows, h, :, :].rearrange("p c i -> p (c i)"),
                                                            kvt[u][rows, h, :], start=True, stop=True)
                            last.then_inc(x_done[u], 1)
                        for u in range(2):
                            pe.wait_ge(x_out[u], ONE + r + 1)
                            pe.wait_ge(w_out[u], ONE + r)
                            for hf in range(2):
                                for s, src in enumerate((ww[u][:, :, :].rearrange("p h d -> p (h d)"), qt[u])):
                                    q = 2 * hf + s
                                    last = nc.tensor.transpose(ps[0:HC, 2 + u, q * TP:(q + 1) * TP],
                                                               src[:, hf * HC:(hf + 1) * HC], ident)
                            last.then_inc(w_t[u], 1)

        with ExitStack() as scan:
            def sbs(name, shape, dt=f32):
                return scan.enter_context(nc.sbuf_tensor(name, shape, dt))

            wqs = [sbs(f"wqs{p}", [HC, B * 4 * CH]) for p in range(2)]
            ks = [sbs(f"ks{p}", [128, 2, 2, C], f16) for p in range(2)]
            ub = [sbs(f"ub{p}", [128, 2, C]) for p in range(2)]
            uo = [sbs(f"uo{p}", [128, 2, C]) for p in range(2)]
            uh = [sbs(f"uh{p}", [128, 2, C], f16) for p in range(2)]
            ul = [sbs(f"ul{p}", [128, 2, C], f16) for p in range(2)]
            s_sb = sbs("s_sb", [HC, 4, 4, HC])
            zero = sbs("zero", [HC, 2 * C], f16)
            zu, ub0 = sem("zu"), sem("ub0")
            sc_ld, ws_done, uo_done, uh_done, ul_done, up_done, s_ready = (
                sem2("sc_ld"), sem2("ws_done"), sem2("uo_done"), sem2("uh_done"), sem2("ul_done"), sem2("up_done"),
                sem2("s_ready"))
            st_u = sem2("st_u")
            fs_ld, fs_sc, fs_hi, fs_lo = sem("fs_ld"), sem("fs_sc"), sem("fs_hi"), sem("fs_lo")

            with nc.Block() as block:

                @block.sync
                def _(sp):
                    start_at_one(sp)
                    sp.wait_ge(ub0, ONE + 2)
                    with sp.Fori(0, NC // 2) as r:
                        for p in range(2):
                            c = 2 * r + p
                            for q in range(2):
                                sp.wait_ge(s_ready[q], ONE + c)
                            sp.dma_start(wqs[p][:, :], d_w[ds(c, 1), :, :, :].rearrange("c p b w -> (c p) (b w)"))\
                                .then_inc(sc_ld[p], 16)
                            for bb in range(4):
                                rows = slice(32 * bb, 32 * bb + CH)
                                sp.dma_start(ks[p][rows, :, :, :].rearrange("i g s w -> i g (s w)"),
                                             d_khl[2 * bb:2 * bb + 2, ds(c, 1), :, :].rearrange("g c i w -> i (g c) w"))\
                                    .then_inc(sc_ld[p], 16)
                                sp.dma_start(ub[p][rows, :, :],
                                             d_ub[2 * bb:2 * bb + 2, ds(c, 1), :, :].rearrange("g c i w -> i (g c) w"))\
                                    .then_inc(sc_ld[p], 16)
                        sp.wait_ge(fs_lo, ONE + 2 * r)
                        sp.dma_start(fcs[:, :, :], wfc[ds(r, 1), :, :, :].rearrange("e p a n -> (e p) a n"))\
                            .then_inc(fs_ld, 16)
                        sp.dma_start(pjs[:, :], wproj[ds(r, 1), :, :].rearrange("e p n -> (e p) n")).then_inc(fs_ld, 16)

                @block.gpsimd
                def _(pool):
                    for p in range(2):
                        nc.gpsimd.memset(ub[p][:, :, :], 0.0).then_inc(ub0, 1)
                    nc.gpsimd.memset(zero[:, :], 0.0).then_inc(zu, 1)
                    with pool.Fori(0, NC // 2) as r:
                        by_constant(pool, 32 * r + 32)
                        pool.wait_ge(fs_ld, ONE + 32 * r + 32)
                        nc.gpsimd.tensor_scalar(fcs[:, :, :], fcs[:, :, :], WSCALE / 8, 8.0, ALU.mult, ALU.mult)\
                            .then_inc(fs_sc, 1)
                        nc.gpsimd.tensor_scalar(pjs[:, :], pjs[:, :], WSCALE / 8, 8.0, ALU.mult, ALU.mult)\
                            .then_inc(fs_sc, 1)
                        pool.wait_ge(fs_hi, ONE + 2 * r + 1)
                        nc.gpsimd.tensor_tensor(fcl[:, :, ds(r, 1), :].rearrange("p a e n -> p (a e) n"), fcs[:, :, :],
                                                fch[:, :, ds(r, 1), :].rearrange("p a e n -> p (a e) n"),
                                                ALU.subtract).then_inc(fs_lo, 1)
                        pool.wait_ge(fs_hi, ONE + 2 * r + 2)
                        nc.gpsimd.tensor_tensor(pjl[:, ds(r, 1), :].rearrange("p e n -> p (e n)"), pjs[:, :],
                                                pjh[:, ds(r, 1), :].rearrange("p e n -> p (e n)"),
                                                ALU.subtract).then_inc(fs_lo, 1)

                @block.vector
                def _(dve):
                    nc.vector.memset(s_sb[:, 0:2, :, :], 0.0).then_inc(s_ready[0], 1)
                    nc.vector.memset(s_sb[:, 2:4, :, :], 0.0).then_inc(s_ready[1], 1)
                    with dve.Fori(0, NC // 2) as r:
                        for p in range(2):
                            c = 2 * r + p
                            dve.wait_ge(sc_ld[p], ONE + 16 * 9 * (r + 1))
                            dve.wait_ge(st_u[p], ONE + 16 * 8 * r)
                            for q in range(2):
                                rows = slice(64 * q, 64 * q + 64)
                                dve.wait_ge(ws_done[q], ONE + c + 1)
                                nc.vector.tensor_tensor(uo[p][rows, :, :], ub[p][rows, :, :],
                                                        ps[rows, 0, 0:2 * C].rearrange("p (g w) -> p g w", g=2),
                                                        ALU.subtract).then_inc(uo_done[q], 1)
                            for q in range(2):
                                rows = slice(64 * q, 64 * q + 64)
                                dve.wait_ge(uh_done[q], ONE + c + 1)
                                nc.vector.tensor_tensor(ul[p][rows, :, :], uo[p][rows, :, :], uh[p][rows, :, :],
                                                        ALU.subtract).then_inc(ul_done[q], 1)
                            for q in range(2):
                                dve.wait_ge(up_done[q], ONE + c + 1)
                                nc.vector.tensor_tensor(
                                    s_sb[:, 2 * q:2 * q + 2, :, :],
                                    ps[0:HC, 4 + 2 * q:6 + 2 * q, 0:4 * HC].rearrange("p a (g w) -> p a g w", w=HC),
                                    cst[0:HC, BM0:BM0 + HC].unsqueeze(1).unsqueeze(1).broadcast_to([HC, 2, 4, HC]),
                                    ALU.mult).then_inc(s_ready[q], 1)

                @block.scalar
                def _(act):
                    with act.Fori(0, NC // 2) as r:
                        for p in range(2):
                            for q in range(2):
                                rows = slice(64 * q, 64 * q + 64)
                                act.wait_ge(uo_done[q], ONE + 2 * r + p + 1)
                                nc.scalar.activation(uh[p][rows, :, :], uo[p][rows, :, :], ACT.Copy)\
                                    .then_inc(uh_done[q], 1)
                            for bb in range(4):
                                for s in range(2):
                                    rows = slice(32 * bb + CH * s, 32 * bb + CH * s + CH)
                                    act.dma_start(
                                        d_u[s, 2 * bb:2 * bb + 2, ds(2 * r + p, 1), :, :].rearrange("g c i w -> i (g c) w"),
                                        uo[p][rows, :, :]).then_inc(st_u[p], 16)
                            act.wait_ge(fs_sc, ONE + 2 * r + p + 1)
                            if p == 0:
                                nc.scalar.activation(fch[:, :, ds(r, 1), :].rearrange("p a e n -> p (a e) n"), fcs[:, :, :],
                                                     ACT.Copy).then_inc(fs_hi, 1)
                            else:
                                nc.scalar.activation(pjh[:, ds(r, 1), :].rearrange("p e n -> p (e n)"), pjs[:, :],
                                                     ACT.Copy).then_inc(fs_hi, 1)
                    for p in range(2):
                        act.wait_ge(st_u[p], ONE + 16 * 8 * NC // 2)

                @block.tensor
                def _(pe):
                    pe.wait_ge(zu, ONE + 1)
                    for bb in range(4):
                        nc.tensor.matmul(ps[0:HC, 4 + bb, 0:4 * HC], zero[0:32, 0:HC], zero[0:32, 0:4 * HC],
                                         start=True, stop=False, skip_group_check=True)
                    with pe.Fori(0, NC // 2) as r:
                        for p in range(2):
                            c = 2 * r + p
                            pe.wait_ge(sc_ld[p], ONE + 16 * 9 * (r + 1))
                            for q in range(2):
                                pe.wait_ge(s_ready[q], ONE + c + 1)
                                pe.wait_ge(uo_done[q], ONE + c)
                                for bb in (2 * q, 2 * q + 1):
                                    for g in range(4):
                                        bg, hf = g // 2, g % 2
                                        o = ((2 * bb + bg) * 2 + hf) * 2 * CH
                                        last = nc.tensor.matmul(ps[32 * bb:32 * bb + 32, 0, g * HC:(g + 1) * HC],
                                                                wqs[p][:, o:o + 2 * CH], s_sb[:, bb, g, :],
                                                                start=True, stop=True)
                                last.then_inc(ws_done[q], 1)
                            for q in range(2):
                                pe.wait_ge(ul_done[q], ONE + c + 1)
                                for part in range(3):
                                    for g in range(4):
                                        for bb in (2 * q, 2 * q + 1):
                                            bg, hf = g // 2, g % 2
                                            rows, w = slice(32 * bb, 32 * bb + CH), slice(hf * HC, (hf + 1) * HC)
                                            last = nc.tensor.matmul(ps[0:HC, 4 + bb, g * HC:(g + 1) * HC],
                                                                    ks[p][rows, bg, part // 2, w],
                                                                    (uh, ul, uh)[part][p][rows, bg, w],
                                                                    start=False, stop=False, skip_group_check=True)
                                last.then_inc(up_done[q], 1)

        with ExitStack() as outp:
            def sbo(name, shape, dt=f32):
                return outp.enter_context(nc.sbuf_tensor(name, shape, dt))

            ut = [sbo(f"ut{u}", [128, C]) for u in range(2)]
            qs = [sbo(f"qs{u}", [128, C]) for u in range(2)]
            pt = [sbo(f"pt{u}", [128, H, 2 * CH]) for u in range(2)]
            ow = [sbo(f"ow{u}", [128, C]) for u in range(2)]
            oT = [sbo(f"oT{u}", [HC, 2, TP]) for u in range(2)]
            ld_o, pu_done, o_done, o_t, o_out, y_done, y_out = (
                sem2("ld_o"), sem2("pu_done"), sem2("o_done"), sem2("o_t"), sem2("o_out"), sem2("y_done"), sem2("y_out"))
            bn2, mv2, sq2, s_dv2 = sem("bn2"), sem("mv2"), sem("sq2"), sem("s_dv2")

            with nc.Block() as block:

                @block.sync
                def _(sp):
                    start_at_one(sp)
                    with sp.Fori(0, B) as r:
                        for u in range(2):
                            t = 2 * r + u
                            sp.wait_ge(pu_done[u], ONE + r)
                            sp.wait_ge(o_done[u], ONE + r)
                            for s, dst in enumerate((ut[u], qs[u])):
                                sp.dma_start(dst[:, :], d_u[s, ds(r, 1), 8 * u:8 * u + 8, :, :]
                                             .rearrange("b c i w -> (b c i) w")).then_inc(ld_o[u], 16)
                            sp.dma_start(pt[u][:, :, :].rearrange("p h i -> p (h i)"),
                                         d_pt[ds(t, 1), :, :].rearrange("t p c -> (t p) c")).then_inc(ld_o[u], 16)

                @block.vector
                def _(dve):
                    with dve.Fori(0, B) as r:
                        for u in range(2):
                            dve.wait_ge(pu_done[u], ONE + r + 1)
                            dve.wait_ge(o_t[u], ONE + r)
                            nc.vector.tensor_tensor(ow[u][:, :], ps[:, u, 0:C], qs[u][:, :], ALU.subtract)\
                                .then_inc(o_done[u], 1)
                        for u in range(2):
                            xt = r_sb[:, ds(2 * r + u, 1), :].rearrange("p t c -> p (t c)")
                            dve.wait_ge(y_done[u], ONE + r + 1)
                            nc.vector.tensor_tensor(xt, ps[:, 4 + u, 0:C], xt, ALU.add).then_inc(y_out[u], 1)
                    for u in range(2):
                        dve.wait_ge(y_out[u], ONE + B)
                    for t in range(NT):
                        last = nc.vector.bn_stats(st_sb[:, t, :], r_sb[:, t, :])
                    last.then_inc(bn2, 1)
                    dve.wait_ge(bn2, ONE + 1)
                    count = [0]

                    def chain(ins):
                        count[0] += 1
                        ins.then_inc(s_dv2, 1)
                        dve.wait_ge(s_dv2, ONE + count[0])

                    norm_statistics(chain, mv2)
                    dve.wait_ge(sq2, ONE + 1)
                    chain(nc.vector.reciprocal(rstd[:, :], rstd[:, :]))

                @block.scalar
                def _(act):
                    with act.Fori(0, B) as r:
                        for u in range(2):
                            act.wait_ge(o_t[u], ONE + r + 1)
                            act.wait_ge(y_done[u], ONE + r)
                            nc.scalar.activation(oT[u][:, :, :].rearrange("p a n -> p (a n)"), ps[0:HC, 2 + u, 0:2 * TP],
                                                 ACT.Copy).then_inc(o_out[u], 1)
                    act.wait_ge(mv2, ONE + 1)
                    nc.scalar.activation(rstd[:, :], tmpa[:, :], ACT.Sqrt, bias=eps_c[:, 1:2]).then_inc(sq2, 1)

                @block.tensor
                def _(pe):
                    with pe.Fori(0, B) as r:
                        for u in range(2):
                            by_constant(pe, 48 * (r + 1), r)
                            pe.wait_ge(ld_o[u], ONE + 48 * (r + 1))
                            pe.wait_ge(o_done[u], ONE + r)
                            for h in range(H):
                                for g in range(4):
                                    rows = slice(32 * g, 32 * g + 32)
                                    last = nc.tensor.matmul(ps[rows, u, D * h:D * h + D], pt[u][rows, h, :],
                                                            ut[u][rows, D * h:D * h + D], start=True, stop=True)
                            last.then_inc(pu_done[u], 1)
                        for u in range(2):
                            pe.wait_ge(o_done[u], ONE + r + 1)
                            pe.wait_ge(o_out[u], ONE + r)
                            for hf in range(2):
                                last = nc.tensor.transpose(ps[0:HC, 2 + u, hf * TP:(hf + 1) * TP],
                                                           ow[u][:, hf * HC:(hf + 1) * HC], ident)
                            last.then_inc(o_t[u], 1)
                        for u in range(2):
                            pe.wait_ge(o_out[u], ONE + r + 1)
                            pe.wait_ge(y_out[u], ONE + r)
                            for hf in range(2):
                                last = nc.tensor.matmul(ps[:, 4 + u, 0:C], oT[u][:, hf, :], wo_sb[:, hf, :],
                                                        start=(hf == 0), stop=(hf == 1))
                            last.then_inc(y_done[u], 1)

        xh = sb("xh", [HC + 1, 2, B * L], f16)
        xl = sb("xl", [HC + 1, 2, B * L], f16)
        gth = sb("gth", [HC + 1, 2, E], f16)
        gtl = sb("gtl", [HC + 1, 2, E], f16)
        gts = sb("gts", [HC + 1, 2, E])
        bps = sb("bps", [1, E, C])
        bph = sb("bph", [1, E, C], f16)
        bpl = sb("bpl", [1, E, C], f16)
        ones = sb("ones", [1, TP], f16)
        xw = [sb(f"xw{u}", [128, C]) for u in range(2)]
        sc = sb("sc", [128, NT, E])
        sel = [sb(f"sel{k}", [128, NT, E]) for k in range(2)]
        key = sb("key", [128, NT, E])
        top = [sb(f"top{k}", [128, NT]) for k in range(2)]
        kmax = sb("kmax", [128, NT])
        g1 = sb("g1", [128, NT])
        g2 = sb("g2", [128, NT])
        comb = sb("comb", [128, NT, E])
        s_g, g_split, s_rt, ex_in, ex_done = (sem("s_g"), sem("g_split"), sem("s_rt"),
                                                        sem("ex_in"), sem("ex_done"))
        xw_done, x_t, xh_done, xl_done, sc_done, sc_out = (sem2("xw_done"), sem2("x_t"), sem2("xh_done"),
                                                           sem2("xl_done"), sem2("sc_done"), sem2("sc_out"))

        with nc.Block() as block:

            @block.sync
            def _(sp):
                start_at_one(sp)
                sp.dma_start(gts[:, :, :], gate.rearrange("p (a n) -> p a n", a=2)).then_inc(s_g, 16)
                sp.dma_start(bps[:, :, :], bproj.rearrange("(a e) n -> a e n", a=1)).then_inc(s_g, 16)
                sp.wait_ge(s_g, ONE + 32)

            @block.gpsimd
            def _(pool):
                pool.wait_ge(s_g, ONE + 32)
                done = 0
                for step in (
                    lambda: nc.gpsimd.memset(xh[HC:HC + 1, :, :], 1.0),
                    lambda: nc.gpsimd.memset(xl[HC:HC + 1, :, :], 0.0),
                    lambda: nc.gpsimd.memset(ones[:, :], 1.0),
                    lambda: nc.gpsimd.tensor_copy(gth[:, :, :], gts[:, :, :]),
                    lambda: nc.gpsimd.tensor_tensor(gtl[:, :, :], gts[:, :, :], gth[:, :, :], ALU.subtract),
                    lambda: nc.gpsimd.tensor_scalar(bps[:, :, :], bps[:, :, :], WSCALE / 8, 8.0, ALU.mult, ALU.mult),
                    lambda: nc.gpsimd.tensor_copy(bph[:, :, :], bps[:, :, :]),
                    lambda: nc.gpsimd.tensor_tensor(bpl[:, :, :], bps[:, :, :], bph[:, :, :], ALU.subtract),
                ):
                    step().then_inc(g_split, 1)
                    done += 1
                    pool.wait_ge(g_split, ONE + done)

            @block.vector
            def _(dve):
                with dve.Fori(0, B) as r:
                    for u in range(2):
                        t = 2 * r + u
                        dve.wait_ge(x_t[u], ONE + r)
                        nc.vector.tensor_scalar(xw[u][:, :], r_sb[:, ds(t, 1), :].rearrange("p t c -> p (t c)"),
                                                mean[:, ds(t, 1)], rstd[:, ds(t, 1)], ALU.subtract, ALU.mult)\
                            .then_inc(xw_done[u], 1)
                    for u in range(2):
                        t = 2 * r + u
                        dve.wait_ge(xh_done[u], ONE + r + 1)
                        nc.vector.tensor_tensor(xl[0:HC, :, ds(t * TP, TP)],
                                                ps[0:HC, u, 0:2 * TP].rearrange("p (h n) -> p h n", h=2),
                                                xh[0:HC, :, ds(t * TP, TP)], ALU.subtract).then_inc(xl_done[u], 1)
                    for u in range(2):
                        dve.wait_ge(sc_done[u], ONE + r + 1)
                        nc.vector.tensor_copy(sc[:, ds(2 * r + u, 1), :].rearrange("p t e -> p (t e)"),
                                              ps[:, 2 + u, 0:E]).then_inc(sc_out[u], 1)
                for u in range(2):
                    dve.wait_ge(sc_out[u], ONE + B)
                count = [0]

                def chain(ins):
                    count[0] += 1
                    ins.then_inc(s_rt, 1)
                    dve.wait_ge(s_rt, ONE + count[0])

                def wide(ap):
                    return ap.unsqueeze(2).broadcast_to([128, NT, E])

                first = cst[:, TB0:TB0 + E].unsqueeze(1).broadcast_to([128, NT, E])
                for k in range(2):
                    chain(nc.vector.tensor_reduce(top[k][:, :], sc[:, :, :], AX.X, ALU.max))
                    chain(nc.vector.tensor_tensor(key[:, :, :], sc[:, :, :], wide(top[k][:, :]), ALU.is_equal))
                    chain(nc.vector.tensor_tensor(key[:, :, :], key[:, :, :], first, ALU.mult))
                    chain(nc.vector.tensor_reduce(kmax[:, :], key[:, :, :], AX.X, ALU.max))
                    chain(nc.vector.tensor_tensor(sel[k][:, :, :], key[:, :, :], wide(kmax[:, :]), ALU.is_equal))
                    if k == 0:
                        chain(nc.vector.scalar_tensor_tensor(sc[:, :, :], sel[0][:, :, :], -1e30, sc[:, :, :],
                                                             ALU.mult, ALU.add))
                nc.vector.tensor_tensor(g2[:, :], top[1][:, :], top[0][:, :], ALU.subtract).then_inc(ex_in, 1)
                dve.wait_ge(ex_done, ONE + 1)
                chain(nc.vector.tensor_scalar(g1[:, :], g2[:, :], 1.0, None, ALU.add))
                chain(nc.vector.reciprocal(g1[:, :], g1[:, :]))
                chain(nc.vector.tensor_tensor(g2[:, :], g2[:, :], g1[:, :], ALU.mult))
                chain(nc.vector.tensor_tensor(comb[:, :, :], sel[0][:, :, :], wide(g1[:, :]), ALU.mult))
                chain(nc.vector.tensor_tensor(key[:, :, :], sel[1][:, :, :], wide(g2[:, :]), ALU.mult))
                chain(nc.vector.tensor_tensor(comb[:, :, :], comb[:, :, :], key[:, :, :], ALU.add))
                chain(nc.vector.tensor_scalar(comb[:, :, :], comb[:, :, :], 1.0 / WSCALE, None, ALU.mult))

            @block.scalar
            def _(act):
                with act.Fori(0, B) as r:
                    for u in range(2):
                        act.wait_ge(x_t[u], ONE + r + 1)
                        nc.scalar.activation(xh[0:HC, :, ds((2 * r + u) * TP, TP)],
                                             ps[0:HC, u, 0:2 * TP].rearrange("p (h n) -> p h n", h=2), ACT.Copy)\
                            .then_inc(xh_done[u], 1)
                act.wait_ge(ex_in, ONE + 1)
                nc.scalar.activation(g2[:, :], g2[:, :], ACT.Exp).then_inc(ex_done, 1)

            @block.tensor
            def _(pe):
                pe.wait_ge(g_split, ONE + 5)
                with pe.Fori(0, B) as r:
                    for u in range(2):
                        pe.wait_ge(xw_done[u], ONE + r + 1)
                        pe.wait_ge(xl_done[u], ONE + r)
                        for hf in range(2):
                            last = nc.tensor.transpose(ps[0:HC, u, hf * TP:(hf + 1) * TP],
                                                       xw[u][:, hf * HC:(hf + 1) * HC], ident)
                        last.then_inc(x_t[u], 1)
                    for u in range(2):
                        pe.wait_ge(xl_done[u], ONE + r + 1)
                        pe.wait_ge(sc_out[u], ONE + r)
                        k = 0
                        for hf in range(2):
                            for xs, gs in ((xh, gth), (xh, gtl), (xl, gth)):
                                last = nc.tensor.matmul(ps[:, 2 + u, 0:E], xs[0:HC + hf, hf, ds((2 * r + u) * TP, TP)],
                                                        gs[0:HC + hf, hf, :], start=(k == 0), stop=(k == 5))
                                k += 1
                        last.then_inc(sc_done[u], 1)

        NB = 512
        hw = [sb(f"hw{p}", [128, NB]) for p in range(2)]
        hh = [sb(f"hh{p}", [128, NB], f16) for p in range(2)]
        hl = [sb(f"hl{p}", [128, NB], f16) for p in range(2)]
        h_done, h_out, hh_done, hl_done, pj_done = (sem2("h_done"), sem2("h_out"), sem2("hh_done"), sem2("hl_done"),
                                                    sem2("pj_done"))
        ye_done, ye_out, s_out = sem2("ye_done"), sem2("ye_out"), sem("s_out")
        HP = HB // 2

        with nc.Block() as block:

            @block.tensor
            def _(pe):
                with pe.Fori(0, E) as e:
                    with pe.Fori(0, 2) as n2:
                        for v in range(2):
                            g = 4 * e + 2 * n2 + v

                            def up(m):
                                p = m % 2
                                pe.wait_ge(h_out[p], ONE + HP * g + m // 2)
                                k = 0
                                for hf in range(2):
                                    K = HC + hf
                                    for ws, xs in ((fch, xh), (fch, xl), (fcl, xh)):
                                        last = nc.tensor.matmul(
                                            ps[:, p, :],
                                            ws[0:K, hf, ds(e, 1), m * 128:(m + 1) * 128].rearrange("p e n -> p (e n)"),
                                            xs[0:K, hf, ds((2 * n2 + v) * NB, NB)], start=(k == 0), stop=(k == 5))
                                        k += 1
                                last.then_inc(h_done[p], 1)

                            def down(m):
                                p = m % 2
                                pe.wait_ge(hl_done[p], ONE + HP * g + m // 2 + 1)
                                if m == 0:
                                    pe.wait_ge(ye_out[v], ONE + 2 * e + n2)
                                for s in range(4):
                                    y = ps[:, 2 + 2 * v + s // 2, (s % 2) * C:(s % 2) * C + C]
                                    for k, (hs, ws) in enumerate(((hh, pjh), (hh, pjl), (hl, pjh))):
                                        last = nc.tensor.matmul(
                                            y, hs[p][:, s * TP:(s + 1) * TP],
                                            ws[:, ds(e, 1), m * C:(m + 1) * C].rearrange("p e n -> p (e n)"),
                                            start=(m == 0 and k == 0 and s % 2 == 0), stop=False, skip_group_check=True)
                                last.then_inc(pj_done[p], 1)

                            up(0)
                            for m in range(1, HB):
                                up(m)
                                down(m - 1)
                            down(HB - 1)
                            for s in range(4):
                                for k, bs in enumerate((bph, bpl)):
                                    last = nc.tensor.matmul(
                                        ps[:, 2 + 2 * v + s // 2, (s % 2) * C:(s % 2) * C + C], ones[:, :],
                                        bs[:, ds(e, 1), :].rearrange("p e n -> p (e n)"), start=False,
                                        stop=(k == 1 and s % 2 == 1), skip_group_check=True)
                            last.then_inc(ye_done[v], 1)

            @block.scalar
            def _(act):
                with act.Fori(0, E * 2) as i:
                    for v in range(2):
                        for m in range(HB):
                            p, n = m % 2, HP * (2 * i + v) + m // 2
                            act.wait_ge(h_done[p], ONE + n + 1)
                            act.wait_ge(hl_done[p], ONE + n)
                            nc.scalar.activation(hw[p][:, :], ps[:, p, :], ACT.Gelu_apprx_tanh, scale=1.0 / WSCALE)\
                                .then_inc(h_out[p], 1)

            @block.vector
            def _(dve):
                with dve.Fori(0, E) as e:
                    with dve.Fori(0, 2) as n2:
                        for v in range(2):
                            for m in range(HB):
                                p, n = m % 2, HP * (4 * e + 2 * n2 + v) + m // 2
                                dve.wait_ge(h_out[p], ONE + n + 1)
                                dve.wait_ge(pj_done[p], ONE + n)
                                nc.vector.tensor_copy(hh[p][:, :], hw[p][:, :]).then_inc(hh_done[p], 1)
                                dve.wait_ge(hh_done[p], ONE + n + 1)
                                nc.vector.tensor_tensor(hl[p][:, :], hw[p][:, :], hh[p][:, :], ALU.subtract)\
                                    .then_inc(hl_done[p], 1)
                            dve.wait_ge(ye_done[v], ONE + 2 * e + n2 + 1)
                            for s in range(4):
                                t = 4 * (2 * n2 + v) + s
                                xt = r_sb[:, ds(t, 1), :].rearrange("p t c -> p (t c)")
                                last = nc.vector.scalar_tensor_tensor(
                                    xt, ps[:, 2 + 2 * v + s // 2, (s % 2) * C:(s % 2) * C + C],
                                    comb[:, ds(t, 1), ds(e, 1)].rearrange("p t e -> p (t e)"), xt, ALU.mult, ALU.add)
                            last.then_inc(ye_out[v], 1)

            @block.sync
            def _(sp):
                start_at_one(sp)
                for v in range(2):
                    sp.wait_ge(ye_out[v], ONE + 2 * E)
                sp.dma_start(out.rearrange("p (t c) -> p t c", t=NT), r_sb[:, :, :]).then_inc(s_out, 16)
                sp.wait_ge(s_out, ONE + 16)


def constants():
    import numpy as np
    p = np.arange(128)
    i, par = p % CH, p // CH % 2
    col = np.arange(2 * CH)
    same = par[:, None] == (col // CH)[None]
    t = np.zeros((128, CW), np.float32)
    t[:, ID0:ID0 + 128] = np.eye(128)
    t[:, MS0:MS0 + 32] = same & ((col % CH)[None] < i[:, None])
    t[:, MU0:MU0 + 32] = same & ((col % CH)[None] >= i[:, None])
    t[:, MP0:MP0 + 2] = par[:, None] == np.arange(2)[None]
    t[:, BM0:BM0 + HC] = (p // D)[:, None] == (np.arange(HC) // D)[None]
    t[:, TB0:TB0 + E] = E - np.arange(E)
    return t


def kernel(**inputs):
    import numpy as np
    import concourse.bacc as bacc
    from concourse.bass_utils import run_bass_kernel_spmd

    a = {k: np.asarray(v) for k, v in inputs.items()}

    def halves(w):
        return np.ascontiguousarray(w.reshape(2, HC, -1).transpose(1, 0, 2).reshape(HC, -1))

    def halves_and_bias(w, bias):
        full = np.zeros((HC + 1, 2, w.shape[1]), w.dtype)
        full[:HC] = w.reshape(2, HC, -1).transpose(1, 0, 2)
        full[HC, 1] = bias
        return full

    by_head = lambda w: w.reshape(C, H, D)
    kv = np.concatenate([by_head(a["L0_conv_Wk"]), by_head(a["L0_conv_Wv"])], axis=2).reshape(C, KVW)
    wqkvb = np.concatenate([kv, a["L0_conv_Wq"], a["L0_conv_Wb"]], axis=1)
    tokens = a["x"].reshape(B, C, L).transpose(0, 2, 1).reshape(NT, TP, C)
    fc, pj = a["L0_ffn_w_fc"], a["L0_ffn_w_proj"]
    arrays = {
        "x": tokens.transpose(1, 0, 2).reshape(TP, NT * C),
        "consts": constants(),
        "wqkvb": halves(wqkvb),
        "wo": halves(a["L0_conv_Wo"]),
        "gate": halves_and_bias(a["L0_ffn_gate_w"].T, a["L0_ffn_gate_b"]).reshape(HC + 1, 2 * E),
        "wfc": np.stack([halves_and_bias(fc[e].T, a["L0_ffn_b_fc"][e]) for e in range(E)]),
        "wproj": pj.transpose(0, 2, 1).reshape(E, HB, 128, C).transpose(0, 2, 1, 3).reshape(E, 128, HB * C),
        "bproj": a["L0_ffn_b_proj"],
    }
    arrays = {k: np.ascontiguousarray(v) for k, v in arrays.items()}
    nc = bacc.Bacc("TRN2", target_bir_lowering=False, num_devices=1)
    f32 = mybir.dt.float32
    args = [nc.dram_tensor(k, v.shape, f32, kind="ExternalInput").ap() for k, v in arrays.items()]
    args.append(nc.dram_tensor("out", (TP, NT * C), f32, kind="ExternalOutput").ap())
    program(nc, *args)
    r = run_bass_kernel_spmd(nc, [arrays], core_ids=[0])
    o = r.results[0]["out"].reshape(TP, NT, C).transpose(1, 0, 2).reshape(B, L, C)
    return np.ascontiguousarray(o.transpose(0, 2, 1)).reshape(B, C, 16, 16)
```

```python
from contextlib import ExitStack

import concourse.bass as bass
from concourse import mybir

B, C, L = 8, 192, 256
TP = 128
NT = B * L // TP
H, D, CH = 12, 16, 16
NC = L // CH
HC = C // 2
KVW = 2 * H * D
QBW = H * D + H
E, HID = 8, 768
HB = HID // 128
ID0, MS0, MU0, MP0, BM0, TB0 = 0, 128, 160, 192, 194, 290
ST = 2 * NT + E
RW = C + 2
TR0 = TB0 + E
TS0 = TR0 + TP
EB0 = TS0 + NT
TI0 = EB0 + E * E
DI0 = TI0 + ST
DM0 = DI0 + 2 * NT
CW = DM0 + 2
IDLE_STEPS = 4
ONE = 1
WSCALE = 64.0


def program(nc, x, consts, wqkvb, wo, gate, wfc, wproj, bproj, out):
    f32, f16 = mybir.dt.float32, mybir.dt.float16
    ALU, ACT, AX = mybir.AluOpType, mybir.ActivationFunctionType, mybir.AxisListType
    ds = bass.ds
    ctx = ExitStack()
    with ctx:
        def sb(name, shape, dt=f32):
            return ctx.enter_context(nc.sbuf_tensor(name, shape, dt))

        semaphores = []
        early = ctx.enter_context(ExitStack())
        held_by = [ctx]

        def sem(name):
            semaphores.append(held_by[0].enter_context(nc.semaphore(name)))
            return semaphores[-1]

        s_cst = sem("s_cst")

        def sem2(name):
            return [sem(f"{name}{u}") for u in range(2)]

        def dram(name, shape, dt=f32):
            return nc.dram_tensor(name, shape, dt, kind="Internal").ap()

        d_kv = dram("d_kv", (NT, TP, KVW))
        d_khl = dram("d_khl", (B, NC, CH, 2 * C), f16)
        d_n = dram("d_n", (NT, TP, C))
        d_mt = dram("d_mt", (NT, TP, C))
        d_pt = dram("d_pt", (NT, TP, 2 * C))
        d_ub = dram("d_ub", (B, NC, CH, C))
        d_q = dram("d_q", (NT, TP, C))
        d_w = dram("d_w", (NC, HC, B, 4 * CH))
        d_u = dram("d_u", (2, B, NC, CH, C))

        d_x = dram("d_x", (ST // 2 + 1, 2, TP, RW))
        d_y = dram("d_y", ((2 * NT + 2) * TP, C))

        cst = sb("cst", [128, CW])
        ident = cst[:, ID0:ID0 + 128]
        x_sb = sb("x_sb", [128, NT, C])
        r_sb = sb("r_sb", [128, NT, C])
        st_sb = sb("st_sb", [128, NT, 6])
        mean = sb("mean", [128, NT])
        rstd = sb("rstd", [128, NT])
        tmpa = sb("tmpa", [128, NT])
        tmpb = sb("tmpb", [128, NT])
        eps_c = sb("eps_c", [128, 3])
        beta = sb("beta", [128, NT, H])
        wqkvb_sb = sb("wqkvb_sb", [HC, 2, KVW + QBW])
        wo_sb = sb("wo_sb", [HC, 2, C])
        fch = sb("fch", [HC + 1, 2, E, HID], f16)
        fcl = sb("fcl", [HC + 1, 2, E, HID], f16)
        pjh = sb("pjh", [128, E, HB * C], f16)
        pjl = sb("pjl", [128, E, HB * C], f16)
        fcs = sb("fcs", [HC + 1, 2, HID])
        pjs = sb("pjs", [128, HB * C])

        ps = ctx.enter_context(nc.psum_tensor("ps", [128, 8, 512], f32))

        held_by[0] = early
        s_x, s_w = sem("s_x"), sem("s_w")
        s_bn, s_mv, s_sq, s_rs = sem("s_bn"), sem("s_mv"), sem("s_sq"), sem("s_rs")
        s_dv = sem("s_dv")
        s_eps = sem("s_eps")

        started = [0]

        def start_at_one(eng):
            for s in semaphores[started[0]:]:
                eng.sem_inc(s, ONE)
            started[0] = len(semaphores)

        def by_constant(eng, *values):
            for value in values:
                eng.compute_val(ONE + value)
            eng.wait_ge(s_cst, ONE + 16)

        def norm_statistics(chain, eps_done):
            me, mo = st_sb[:, :, 1], st_sb[:, :, 4]
            chain(nc.vector.tensor_tensor(mean[:, :], me, mo, ALU.add))
            chain(nc.vector.tensor_scalar(mean[:, :], mean[:, :], 0.5, None, ALU.mult))
            chain(nc.vector.tensor_tensor(tmpa[:, :], me, mean[:, :], ALU.subtract))
            chain(nc.vector.tensor_tensor(tmpa[:, :], tmpa[:, :], tmpa[:, :], ALU.mult))
            chain(nc.vector.tensor_tensor(tmpb[:, :], st_sb[:, :, 2], st_sb[:, :, 5], ALU.add))
            nc.vector.scalar_tensor_tensor(tmpa[:, :], tmpb[:, :], 1.0 / C, tmpa[:, :], ALU.mult, ALU.add)\
                .then_inc(eps_done, 1)

        with ExitStack() as mix:
            def sbm(name, shape, dt=f32):
                return mix.enter_context(nc.sbuf_tensor(name, shape, dt))

            tw = [sbm(f"tw{u}", [128, 2, C]) for u in range(2)]
            tT = [sbm(f"tT{u}", [HC, 2, 2, TP]) for u in range(2)]
            kvw = [sbm(f"kvw{u}", [128, 2, H, 2 * D]) for u in range(2)]
            qw = [sbm(f"qw{u}", [128, 2, H, D]) for u in range(2)]
            qn = [sbm(f"qn{u}", [128, 2, H, 2 * D]) for u in range(2)]
            sqw = [sbm(f"sqw{u}", [128, 2, 2 * H, D]) for u in range(2)]
            ssw = [sbm(f"ssw{u}", [128, 2, 2 * H]) for u in range(2)]
            rnw = [sbm(f"rnw{u}", [128, 2, 2 * H]) for u in range(2)]
            khl = [sbm(f"khl{u}", [128, 2, 2, C], f16) for u in range(2)]
            kqT = [sbm(f"kqT{u}", [128, 3, 2, TP]) for u in range(2)]
            gm = sbm("gm", [128, 3, 4, 2 * CH])
            nw = [sbm(f"nw{u}", [128, 3, 4, CH]) for u in range(2)]
            ptw = [sbm(f"ptw{u}", [128, 3, 4, 2 * CH]) for u in range(2)]
            lane_n = sbm("lane_n", [128, CH, H, CH])
            lane_m = sbm("lane_m", [128, CH, H, CH])
            prod = sbm("prod", [128, CH * H * CH // 2])

            NB2 = B // 2
            TB2 = 10
            GB2 = 4
            t_ready, t_added = sem2("t_ready"), sem2("t_added")
            t_filled, t_evicted = sem("t_filled"), sem2("t_evicted")
            kv_done, qb_done, kv_out, qb_out = sem("kv_done"), sem("qb_done"), sem("kv_out"), sem("qb_out")
            sq_done, ss_done, sn_done = sem2("sq_done"), sem2("ss_done"), sem2("sn_done")
            kn_done, khi_done, klo_done = sem2("kn_done"), sem2("khi_done"), sem2("klo_done")
            g_done, g_out, n_ready = sem2("g_done"), sem("g_out"), sem2("n_ready")
            st_kv, st_k, st_n, st_pt, st_q = (sem2("st_kv"), sem2("st_k"), sem2("st_n"), sem2("st_pt"),
                                              sem2("st_q"))
            s_ch2, pads = sem("s_ch2"), sem("pads")
            ln_ld, inv_done, st_m, s_inv = sem("ln_ld"), sem("inv_done"), sem("st_m"), sem("s_inv")

            with nc.Block() as block:

                @block.sync
                def _(sp):
                    start_at_one(sp)
                    sp.dma_start(x_sb[:, :, :], x.rearrange("p (t c) -> p t c", t=NT)).then_inc(s_x, 16)
                    sp.dma_start(cst[:, :], consts).then_inc(s_cst, 16)
                    sp.dma_start(wqkvb_sb[:, :, :], wqkvb.rearrange("p (a n) -> p a n", a=2)).then_inc(s_w, 16)
                    sp.dma_start(wo_sb[:, :, :], wo.rearrange("p (a n) -> p a n", a=2)).then_inc(s_w, 16)
                    with sp.Fori(0, NB2) as r:
                        for u in range(2):
                            b = 2 * r + u
                            sp.wait_ge(kn_done[u], ONE + r + 1)
                            sp.dma_start(d_kv[ds(2 * b, 2), :, :].rearrange("t p c -> p t c"),
                                         kvw[u][:, :, :, :].rearrange("p t h d -> p t (h d)")).then_inc(st_kv[u], 16)
                            sp.wait_ge(khi_done[u], ONE + r + 1)
                            sp.wait_ge(klo_done[u], ONE + r + 1)
                            for j in range(2):
                                sp.dma_start(d_khl[ds(b, 1), 8 * j:8 * j + 8, :, :].rearrange("b c i w -> (b c i) w"),
                                             khl[u][:, j, :, :].rearrange("p s w -> p (s w)")).then_inc(st_k[u], 16)
                            sp.dma_start(d_q[ds(2 * b, 2), :, :].rearrange("t p c -> p t c"),
                                         qw[u][:, :, :, :].rearrange("p t h d -> p t (h d)")).then_inc(st_q[u], 16)
                            for j in range(2):
                                sp.wait_ge(n_ready[j], ONE + 2 * r + u + 1)
                                sp.dma_start(d_n[ds(2 * b + j, 1), :, :].rearrange("t p c -> (t p) c"),
                                             nw[j][:, :, :, :].rearrange("p a r i -> p (a r i)")).then_inc(st_n[j], 16)
                                sp.dma_start(d_pt[ds(2 * b + j, 1), :, :].rearrange("t p c -> (t p) c"),
                                             ptw[j][:, :, :, :].rearrange("p a r i -> p (a r i)")).then_inc(st_pt[j], 16)
                    for j in range(2):
                        sp.wait_ge(st_n[j], ONE + 16 * B)
                    sp.dma_start(lane_n[:, :, :, :].rearrange("p i h j -> p (i h j)"),
                                 d_n.rearrange("t (c i) w -> (t c) (i w)", i=CH)).then_inc(ln_ld, 16)
                    sp.wait_ge(inv_done, ONE + 1)
                    sp.dma_start(d_mt.rearrange("t (c i) w -> (t c) (i w)", i=CH),
                                 lane_m[:, :, :, :].rearrange("p i h j -> p (i h j)")).then_inc(st_m, 16)
                    sp.wait_ge(st_m, ONE + 16)
                    for u in range(2):
                        sp.wait_ge(st_kv[u], ONE + 16 * NB2)
                        sp.wait_ge(st_k[u], ONE + 32 * NB2)
                        sp.wait_ge(st_pt[u], ONE + 16 * B)
                        sp.wait_ge(st_q[u], ONE + 16 * NB2)

                @block.gpsimd
                def _(pool):
                    nc.gpsimd.memset(eps_c[:, 0:1], 1e-6).then_inc(s_eps, 1)
                    nc.gpsimd.memset(eps_c[:, 1:2], 1e-5).then_inc(s_eps, 1)
                    for u in range(2):
                        nc.gpsimd.memset(qn[u][:, :, :, :], 0.0).then_inc(pads, 1)
                    nc.gpsimd.memset(lane_m[:, :, :, :], 0.0).then_inc(pads, 1)
                    pool.wait_ge(pads, ONE + 3)
                    for j in range(CH):
                        nc.gpsimd.memset(lane_m[:, j, :, j], 1.0).then_inc(pads, 1)
                    with pool.Fori(0, NB2) as r:
                        for u in range(2):
                            b = 2 * r + u
                            pool.wait_ge(t_ready[u], ONE + r + 1)
                            nc.gpsimd.tensor_tensor(r_sb[:, ds(2 * b, 2), :], x_sb[:, ds(2 * b, 2), :],
                                                    tw[u][:, :, :], ALU.add).then_inc(t_added[u], 1)
                        for u in range(2):
                            pool.wait_ge(kv_out, ONE + GB2 * r + 2 * u + 2)
                            pool.wait_ge(qb_out, ONE + GB2 * r + 2 * u + 2)
                            pool.wait_ge(ss_done[u], ONE + r)
                            nc.gpsimd.tensor_tensor(sqw[u][:, :, 0:H, :], kvw[u][:, :, :, 0:D],
                                                    kvw[u][:, :, :, 0:D], ALU.mult).then_inc(sq_done[u], 1)
                            nc.gpsimd.tensor_tensor(sqw[u][:, :, H:2 * H, :], qw[u][:, :, :, :],
                                                    qw[u][:, :, :, :], ALU.mult).then_inc(sq_done[u], 1)
                        for u in range(2):
                            pool.wait_ge(kn_done[u], ONE + r + 1)
                            pool.wait_ge(khi_done[u], ONE + r + 1)
                            nc.gpsimd.tensor_tensor(khl[u][:, :, 1, :].rearrange("p t (h d) -> p t h d", h=H),
                                                    kvw[u][:, :, :, 0:D],
                                                    khl[u][:, :, 0, :].rearrange("p t (h d) -> p t h d", h=H),
                                                    ALU.subtract).then_inc(klo_done[u], 1)

                @block.scalar
                def _(act):
                    act.wait_ge(s_eps, ONE + 2)
                    act.wait_ge(s_mv, ONE + 1)
                    nc.scalar.activation(rstd[:, :], tmpa[:, :], ACT.Sqrt, bias=eps_c[:, 0:1]).then_inc(s_sq, 1)
                    with act.Fori(0, NB2) as r:
                        for u in range(2):
                            act.wait_ge(t_filled, ONE + TB2 * r + u + 1)
                            act.wait_ge(qb_done, ONE + GB2 * r)
                            nc.scalar.activation(tT[u][:, :, :, :].rearrange("p a b n -> p (a b n)"),
                                                 ps[0:HC, u, :], ACT.Copy).then_inc(t_evicted[u], 1)
                        for u in range(2):
                            for j in range(2):
                                n = GB2 * r + 2 * u + j
                                act.wait_ge(kv_done, ONE + n + 1)
                                if j == 0:
                                    act.wait_ge(st_kv[u], ONE + 16 * r)
                                    act.wait_ge(klo_done[u], ONE + r)
                                    act.wait_ge(g_done[1], ONE + 2 * r)
                                nc.scalar.activation(kvw[u][:, j, :, :].rearrange("p h d -> p (h d)"),
                                                     ps[:, 2, 0:KVW], ACT.Silu).then_inc(kv_out, 1)
                                act.wait_ge(qb_done, ONE + n + 1)
                                if j == 0:
                                    act.wait_ge(kn_done[u], ONE + r)
                                    act.wait_ge(st_q[u], ONE + 16 * r)
                                nc.scalar.activation(qw[u][:, j, :, :].rearrange("p h d -> p (h d)"),
                                                     ps[:, 3, 0:C], ACT.Silu)
                                nc.scalar.activation(beta[:, ds(n, 1), :].rearrange("p t h -> p (t h)"),
                                                     ps[:, 3, C:QBW], ACT.Tanh, scale=0.5).then_inc(qb_out, 1)
                        for u in range(2):
                            act.wait_ge(ss_done[u], ONE + r + 1)
                            nc.scalar.activation(rnw[u][:, :, :], ssw[u][:, :, :], ACT.Sqrt, bias=eps_c[:, 0:1])\
                                .then_inc(sn_done[u], 1)
                        for u in range(2):
                            act.wait_ge(kn_done[u], ONE + r + 1)
                            act.wait_ge(st_k[u], ONE + 32 * r)
                            nc.scalar.activation(khl[u][:, :, 0, :].rearrange("p t (h d) -> p t h d", h=H),
                                                 kvw[u][:, :, :, 0:D], ACT.Copy).then_inc(khi_done[u], 1)
                            for j in range(2):
                                idx = 2 + 2 * (2 * u + j)
                                act.wait_ge(g_done[j], ONE + 2 * r + u)
                                for k in range(2):
                                    bank = (idx + k) % 2
                                    act.wait_ge(t_filled, ONE + TB2 * r + idx + k + 1)
                                    nc.scalar.activation(kqT[j][:, :, k, :],
                                                         ps[:, bank, 0:3 * TP].rearrange("p (a n) -> p a n", a=3),
                                                         ACT.Copy).then_inc(t_evicted[bank], 1)

                @block.vector
                def _(dve):
                    dve.wait_ge(s_x, ONE + 16)
                    for t in range(NT):
                        last = nc.vector.bn_stats(st_sb[:, t, :], x_sb[:, t, :])
                    last.then_inc(s_bn, 1)
                    dve.wait_ge(s_bn, ONE + 1)
                    count = [0]

                    def chain(ins):
                        count[0] += 1
                        ins.then_inc(s_dv, 1)
                        dve.wait_ge(s_dv, ONE + count[0])

                    norm_statistics(chain, s_mv)
                    dve.wait_ge(s_sq, ONE + 1)
                    nc.vector.reciprocal(rstd[:, :], rstd[:, :]).then_inc(s_rs, 1)
                    dve.wait_ge(s_rs, ONE + 1)
                    dve.wait_ge(s_cst, ONE + 16)
                    dve.wait_ge(pads, ONE + 3 + CH)
                    LINKS = 10
                    with dve.Fori(0, NB2) as r:
                        k = 0

                        for u in range(2):
                            b = 2 * r + u
                            dve.wait_ge(t_filled, ONE + TB2 * r)
                            dve.wait_ge(t_added[u], ONE + r)
                            for j in range(2):
                                last = nc.vector.tensor_scalar(tw[u][:, j, :],
                                                               x_sb[:, ds(2 * b + j, 1), :].rearrange("p t c -> p (t c)"),
                                                               mean[:, ds(2 * b + j, 1)], rstd[:, ds(2 * b + j, 1)],
                                                               ALU.subtract, ALU.mult)
                            last.then_inc(t_ready[u], 1)
                        for u in range(2):
                            b = 2 * r + u
                            dve.wait_ge(sq_done[u], ONE + 2 * r + 2)
                            nc.vector.tensor_reduce(ssw[u][:, :, :], sqw[u][:, :, :, :], AX.X, ALU.add)\
                                .then_inc(ss_done[u], 1)
                            k += 1
                            nc.vector.tensor_scalar(beta[:, ds(2 * b, 2), :], beta[:, ds(2 * b, 2), :], 0.5, 0.5,
                                                    ALU.mult, ALU.add).then_inc(s_ch2, 1)
                            dve.wait_ge(s_ch2, ONE + LINKS * r + k)
                        for u in range(2):
                            dve.wait_ge(sn_done[u], ONE + r + 1)
                            dve.wait_ge(g_done[1], ONE + 2 * r)
                            k += 1
                            nc.vector.reciprocal(rnw[u][:, :, :], rnw[u][:, :, :]).then_inc(s_ch2, 1)
                            dve.wait_ge(s_ch2, ONE + LINKS * r + k)
                            nc.vector.tensor_tensor(kvw[u][:, :, :, 0:D], kvw[u][:, :, :, 0:D],
                                                    rnw[u][:, :, 0:H].unsqueeze(3).broadcast_to([128, 2, H, D]), ALU.mult)
                            nc.vector.tensor_tensor(qw[u][:, :, :, :], qw[u][:, :, :, :],
                                                    rnw[u][:, :, H:2 * H].unsqueeze(3).broadcast_to([128, 2, H, D]), ALU.mult)\
                                .then_inc(s_ch2, 1)
                            k += 1
                            dve.wait_ge(s_ch2, ONE + LINKS * r + k)
                            nc.vector.tensor_copy(qn[u][:, :, :, 0:D], qw[u][:, :, :, :]).then_inc(kn_done[u], 1)
                        for u in range(2):
                            for j in range(2):
                                n = GB2 * r + 2 * u + j
                                m = 2 * r + u
                                scores = ps[:, 4:8, 0:3 * 64].rearrange("p r (a s i) -> p a r s i", a=3, s=2)
                                dve.wait_ge(g_done[j], ONE + m + 1)
                                dve.wait_ge(st_pt[j], ONE + 16 * m)
                                dve.wait_ge(st_n[j], ONE + 16 * m)
                                nc.vector.tensor_tensor(
                                    ptw[j][:, :, :, :], scores[:, :, :, 1, :],
                                    cst[:, MU0:MU0 + 32].unsqueeze(1).unsqueeze(1).broadcast_to([128, 3, 4, 32]), ALU.mult)
                                k += 1
                                nc.vector.tensor_tensor(
                                    gm[:, :, :, :], scores[:, :, :, 0, :],
                                    cst[:, MS0:MS0 + 32].unsqueeze(1).unsqueeze(1).broadcast_to([128, 3, 4, 32]), ALU.mult)\
                                    .then_inc(g_out, 1)
                                dve.wait_ge(g_out, ONE + n + 1)
                                nc.vector.tensor_tensor(nw[j][:, :, :, :], gm[:, :, :, 0:CH], gm[:, :, :, CH:2 * CH], ALU.add)\
                                    .then_inc(s_ch2, 1)
                                dve.wait_ge(s_ch2, ONE + LINKS * r + k)
                                nc.vector.tensor_tensor(
                                    nw[j][:, :, :, :].rearrange("p a r i -> p (a r) i"),
                                    nw[j][:, :, :, :].rearrange("p a r i -> p (a r) i"),
                                    beta[:, ds(n, 1), :].rearrange("p t h -> p (t h)").unsqueeze(2).broadcast_to([128, H, CH]),
                                    ALU.mult).then_inc(n_ready[j], 1)
                        assert k == LINKS
                    dve.wait_ge(ln_ld, ONE + 16)
                    step = 0
                    for m in range(CH - 1):
                        rows, w = CH - 1 - m, m + 1
                        pr = prod[:, 0:rows * H * w].rearrange("p (i h j) -> p i h j", i=rows, h=H)
                        below = lane_m[:, 0:w, :, m + 1:CH].rearrange("p j h i -> p i h j")
                        nc.vector.tensor_tensor(
                            pr, lane_n[:, m + 1:CH, :, m].unsqueeze(3).broadcast_to([128, rows, H, w]),
                            lane_m[:, 0:w, :, m].rearrange("p j h -> p h j").unsqueeze(1).broadcast_to([128, rows, H, w]),
                            ALU.mult).then_inc(s_inv, 1)
                        step += 1
                        dve.wait_ge(s_inv, ONE + step)
                        last = nc.vector.tensor_tensor(below, below, pr, ALU.subtract)
                        if m == CH - 2:
                            last.then_inc(inv_done, 1)
                        else:
                            last.then_inc(s_inv, 1)
                            step += 1
                            dve.wait_ge(s_inv, ONE + step)

                @block.tensor
                def _(pe):
                    pe.wait_ge(s_cst, ONE + 16)
                    pe.wait_ge(s_w, ONE + 32)
                    pe.wait_ge(pads, ONE + 3)
                    with pe.Fori(0, NB2) as r:
                        for u in range(2):
                            pe.wait_ge(t_ready[u], ONE + r + 1)
                            pe.wait_ge(t_evicted[u], ONE + TB2 // 2 * r)
                            for j in range(2):
                                for hf in range(2):
                                    q = 2 * j + hf
                                    last = nc.tensor.transpose(ps[0:HC, u, q * TP:(q + 1) * TP],
                                                               tw[u][:, j, hf * HC:(hf + 1) * HC], ident)
                            last.then_inc(t_filled, 1)
                        for u in range(2):
                            pe.wait_ge(t_evicted[u], ONE + TB2 // 2 * r + 1)
                            for j in range(2):
                                n = GB2 * r + 2 * u + j
                                pe.wait_ge(kv_out, ONE + n)
                                for hf in range(2):
                                    last = nc.tensor.matmul(ps[:, 2, 0:KVW], tT[u][:, j, hf, :], wqkvb_sb[:, hf, 0:KVW],
                                                            start=(hf == 0), stop=(hf == 1))
                                last.then_inc(kv_done, 1)
                                pe.wait_ge(qb_out, ONE + n)
                                for hf in range(2):
                                    last = nc.tensor.matmul(ps[:, 3, 0:QBW], tT[u][:, j, hf, :],
                                                            wqkvb_sb[:, hf, KVW:KVW + QBW],
                                                            start=(hf == 0), stop=(hf == 1))
                                last.then_inc(qb_done, 1)
                        for u in range(2):
                            pe.wait_ge(kn_done[u], ONE + r + 1)
                            for j in range(2):
                                idx = 2 + 2 * (2 * u + j)
                                n = GB2 * r + 2 * u + j
                                for k, src in enumerate((kvw[u], qn[u])):
                                    bank = (idx + k) % 2
                                    pe.wait_ge(t_evicted[bank], ONE + TB2 // 2 * r + (idx + k) // 2)
                                    for a in range(3):
                                        last = nc.tensor.transpose(
                                            ps[:, bank, a * TP:(a + 1) * TP],
                                            src[:, j, 4 * a:4 * a + 4, :].rearrange("p h d -> p (h d)"), ident)
                                    last.then_inc(t_filled, 1)
                                by_constant(pe, TB2 // 2 * r + idx // 2 + 1, TB2 // 2 * r + (idx + 1) // 2 + 1, n)
                                pe.wait_ge(t_evicted[idx % 2], ONE + TB2 // 2 * r + idx // 2 + 1)
                                pe.wait_ge(t_evicted[(idx + 1) % 2], ONE + TB2 // 2 * r + (idx + 1) // 2 + 1)
                                pe.wait_ge(g_out, ONE + n)
                                for a in range(3):
                                    for g in range(4):
                                        for q in range(4):
                                            rows, cols = slice(32 * q, 32 * q + D), slice(32 * g, 32 * g + 32)
                                            last = nc.tensor.matmul(ps[cols, 4 + q, 64 * a:64 * a + 64],
                                                                    kqT[j][rows, a, 0, cols], kqT[j][rows, a, :, cols],
                                                                    start=True, stop=True)
                                last.then_inc(g_done[j], 1)

        with ExitStack() as wy:
            def sbw(name, shape, dt=f32):
                return wy.enter_context(nc.sbuf_tensor(name, shape, dt))

            mtc = [sbw(f"mtc{u}", [128, H, CH]) for u in range(2)]
            mb = [sbw(f"mb{u}", [128, H, 2, CH]) for u in range(2)]
            kvt = [sbw(f"kvt{u}", [128, H, 2 * D]) for u in range(2)]
            ww = [sbw(f"ww{u}", [128, H, D]) for u in range(2)]
            ubw = [sbw(f"ubw{u}", [128, H, D]) for u in range(2)]
            qt = [sbw(f"qt{u}", [128, C]) for u in range(2)]
            wT = [sbw(f"wT{u}", [HC, 8, 4, CH]) for u in range(2)]
            ld_m, ld_kv, mb_done, x_done, x_out = (sem2("ld_m"), sem2("ld_kv"), sem2("mb_done"), sem2("x_done"),
                                                   sem2("x_out"))
            w_t, w_out, st_ub, st_w, m_beta = sem2("w_t"), sem2("w_out"), sem2("st_ub"), sem2("st_w"), sem2("m_beta")

            with nc.Block() as block:

                @block.sync
                def _(sp):
                    start_at_one(sp)
                    with sp.Fori(0, B) as r:
                        for u in range(2):
                            sp.wait_ge(mb_done[u], ONE + r)
                            sp.dma_start(mtc[u][:, :, :].rearrange("p h i -> p (h i)"),
                                         d_mt[ds(2 * r + u, 1), :, :].rearrange("t p c -> (t p) c")).then_inc(ld_m[u], 16)
                            sp.wait_ge(x_done[u], ONE + r)
                            sp.dma_start(kvt[u][:, :, :].rearrange("p h d -> p (h d)"),
                                         d_kv[ds(2 * r + u, 1), :, :].rearrange("t p c -> (t p) c")).then_inc(ld_kv[u], 16)
                            sp.wait_ge(w_t[u], ONE + r)
                            sp.dma_start(qt[u][:, :], d_q[ds(2 * r + u, 1), :, :].rearrange("t p c -> (t p) c"))\
                                .then_inc(ld_kv[u], 16)

                @block.vector
                def _(dve):
                    with dve.Fori(0, B) as r:
                        for u in range(2):
                            dve.wait_ge(ld_m[u], ONE + 16 * r + 16)
                            nc.vector.tensor_tensor(
                                mtc[u][:, :, :], mtc[u][:, :, :],
                                beta[:, ds(2 * r + u, 1), :].rearrange("p t h -> p (t h)").unsqueeze(2)
                                .broadcast_to([128, H, CH]), ALU.mult).then_inc(m_beta[u], 1)
                            dve.wait_ge(m_beta[u], ONE + r + 1)
                            dve.wait_ge(x_done[u], ONE + r)
                            nc.vector.tensor_tensor(
                                mb[u][:, :, :, :], mtc[u][:, :, :].unsqueeze(2).broadcast_to([128, H, 2, CH]),
                                cst[:, MP0:MP0 + 2].unsqueeze(1).unsqueeze(3).broadcast_to([128, H, 2, CH]), ALU.mult)\
                                .then_inc(mb_done[u], 1)
                        for u in range(2):
                            dve.wait_ge(w_t[u], ONE + r + 1)
                            dve.wait_ge(st_w[u], ONE + 16 * r)
                            nc.vector.tensor_copy(
                                wT[u][:, :, :, :],
                                ps[0:HC, 2 + u, :].rearrange("p (q c i) -> p c q i", q=4, i=CH)).then_inc(w_out[u], 1)

                @block.scalar
                def _(act):
                    with act.Fori(0, B) as r:
                        for u in range(2):
                            both = ps[:, u, 0:KVW].rearrange("p (h s d) -> p s h d", h=H, s=2)
                            act.wait_ge(x_done[u], ONE + r + 1)
                            act.wait_ge(w_t[u], ONE + r)
                            nc.scalar.activation(ww[u][:, :, :], both[:, 0, :, :], ACT.Copy)
                            act.wait_ge(st_ub[u], ONE + 16 * r)
                            nc.scalar.activation(ubw[u][:, :, :], both[:, 1, :, :], ACT.Copy).then_inc(x_out[u], 1)
                            act.wait_ge(x_out[u], ONE + r + 1)
                            act.dma_start(d_ub[ds(r, 1), 8 * u:8 * u + 8, :, :].rearrange("b c i w -> (b c i) w"),
                                          ubw[u][:, :, :].rearrange("p h d -> p (h d)")).then_inc(st_ub[u], 16)
                        for u in range(2):
                            act.wait_ge(w_out[u], ONE + r + 1)
                            act.dma_start(d_w[8 * u:8 * u + 8, :, ds(r, 1), :].rearrange("c p b w -> p c (b w)"),
                                          wT[u][:, :, :, :].rearrange("p c q i -> p c (q i)")).then_inc(st_w[u], 16)
                    for u in range(2):
                        act.wait_ge(st_ub[u], ONE + 16 * B)
                        act.wait_ge(st_w[u], ONE + 16 * B)

                @block.tensor
                def _(pe):
                    with pe.Fori(0, B) as r:
                        for u in range(2):
                            by_constant(pe, r + 1, 32 * r + 32, r)
                            pe.wait_ge(mb_done[u], ONE + r + 1)
                            pe.wait_ge(ld_kv[u], ONE + 32 * r + 32)
                            pe.wait_ge(x_out[u], ONE + r)
                            for h in range(H):
                                for g in range(4):
                                    rows = slice(32 * g, 32 * g + 32)
                                    last = nc.tensor.matmul(ps[rows, u, 32 * h:32 * h + 32],
                                                            mb[u][rows, h, :, :].rearrange("p c i -> p (c i)"),
                                                            kvt[u][rows, h, :], start=True, stop=True)
                            last.then_inc(x_done[u], 1)
                        for u in range(2):
                            pe.wait_ge(x_out[u], ONE + r + 1)
                            pe.wait_ge(w_out[u], ONE + r)
                            for hf in range(2):
                                for s, src in enumerate((ww[u][:, :, :].rearrange("p h d -> p (h d)"), qt[u])):
                                    q = 2 * hf + s
                                    last = nc.tensor.transpose(ps[0:HC, 2 + u, q * TP:(q + 1) * TP],
                                                               src[:, hf * HC:(hf + 1) * HC], ident)
                            last.then_inc(w_t[u], 1)

        with nc.Block() as block:

            @block.sync
            def _(sp):
                numbers = sorted(s.num for s in semaphores[1:])
                assert numbers == list(range(numbers[0], numbers[-1] + 1))
                sp.sem_clear(range(numbers[0], numbers[-1] + 1))

        early.close()
        held_by[0] = ctx

        with ExitStack() as scan:
            def sbs(name, shape, dt=f32):
                return scan.enter_context(nc.sbuf_tensor(name, shape, dt))

            wqs = [sbs(f"wqs{p}", [HC, B * 4 * CH]) for p in range(2)]
            ks = [sbs(f"ks{p}", [128, 2, 2, C], f16) for p in range(2)]
            ub = [sbs(f"ub{p}", [128, 2, C]) for p in range(2)]
            uo = [sbs(f"uo{p}", [128, 2, C]) for p in range(2)]
            uh = [sbs(f"uh{p}", [128, 2, C], f16) for p in range(2)]
            ul = [sbs(f"ul{p}", [128, 2, C], f16) for p in range(2)]
            s_sb = sbs("s_sb", [HC, 4, 4, HC])
            zero = sbs("zero", [HC, 2 * C], f16)
            zu, ub0 = sem("zu"), sem("ub0")
            sc_ld, ws_done, uo_done, uh_done, ul_done, up_done, s_ready = (
                sem2("sc_ld"), sem2("ws_done"), sem2("uo_done"), sem2("uh_done"), sem2("ul_done"), sem2("up_done"),
                sem2("s_ready"))
            st_u = sem2("st_u")
            fs_ld, fs_sc, fs_hi, fs_lo = sem("fs_ld"), sem("fs_sc"), sem("fs_hi"), sem("fs_lo")

            with nc.Block() as block:

                @block.sync
                def _(sp):
                    start_at_one(sp)
                    sp.wait_ge(ub0, ONE + 2)
                    with sp.Fori(0, NC // 2) as r:
                        for p in range(2):
                            c = 2 * r + p
                            for q in range(2):
                                sp.wait_ge(s_ready[q], ONE + c)
                            sp.dma_start(wqs[p][:, :], d_w[ds(c, 1), :, :, :].rearrange("c p b w -> (c p) (b w)"))\
                                .then_inc(sc_ld[p], 16)
                            for bb in range(4):
                                rows = slice(32 * bb, 32 * bb + CH)
                                sp.dma_start(ks[p][rows, :, :, :].rearrange("i g s w -> i g (s w)"),
                                             d_khl[2 * bb:2 * bb + 2, ds(c, 1), :, :].rearrange("g c i w -> i (g c) w"))\
                                    .then_inc(sc_ld[p], 16)
                                sp.dma_start(ub[p][rows, :, :],
                                             d_ub[2 * bb:2 * bb + 2, ds(c, 1), :, :].rearrange("g c i w -> i (g c) w"))\
                                    .then_inc(sc_ld[p], 16)
                        sp.wait_ge(fs_lo, ONE + 2 * r)
                        sp.dma_start(fcs[:, :, :], wfc[ds(r, 1), :, :, :].rearrange("e p a n -> (e p) a n"))\
                            .then_inc(fs_ld, 16)
                        sp.dma_start(pjs[:, :], wproj[ds(r, 1), :, :].rearrange("e p n -> (e p) n")).then_inc(fs_ld, 16)

                @block.gpsimd
                def _(pool):
                    for p in range(2):
                        nc.gpsimd.memset(ub[p][:, :, :], 0.0).then_inc(ub0, 1)
                    nc.gpsimd.memset(zero[:, :], 0.0).then_inc(zu, 1)
                    with pool.Fori(0, NC // 2) as r:
                        by_constant(pool, 32 * r + 32)
                        pool.wait_ge(fs_ld, ONE + 32 * r + 32)
                        nc.gpsimd.tensor_scalar(fcs[:, :, :], fcs[:, :, :], WSCALE / 8, 8.0, ALU.mult, ALU.mult)\
                            .then_inc(fs_sc, 1)
                        nc.gpsimd.tensor_scalar(pjs[:, :], pjs[:, :], WSCALE / 8, 8.0, ALU.mult, ALU.mult)\
                            .then_inc(fs_sc, 1)
                        pool.wait_ge(fs_hi, ONE + 2 * r + 1)
                        nc.gpsimd.tensor_tensor(fcl[:, :, ds(r, 1), :].rearrange("p a e n -> p (a e) n"), fcs[:, :, :],
                                                fch[:, :, ds(r, 1), :].rearrange("p a e n -> p (a e) n"),
                                                ALU.subtract).then_inc(fs_lo, 1)
                        pool.wait_ge(fs_hi, ONE + 2 * r + 2)
                        nc.gpsimd.tensor_tensor(pjl[:, ds(r, 1), :].rearrange("p e n -> p (e n)"), pjs[:, :],
                                                pjh[:, ds(r, 1), :].rearrange("p e n -> p (e n)"),
                                                ALU.subtract).then_inc(fs_lo, 1)

                @block.vector
                def _(dve):
                    nc.vector.memset(s_sb[:, 0:2, :, :], 0.0).then_inc(s_ready[0], 1)
                    nc.vector.memset(s_sb[:, 2:4, :, :], 0.0).then_inc(s_ready[1], 1)
                    with dve.Fori(0, NC // 2) as r:
                        for p in range(2):
                            c = 2 * r + p
                            dve.wait_ge(sc_ld[p], ONE + 16 * 9 * (r + 1))
                            dve.wait_ge(st_u[p], ONE + 16 * 8 * r)
                            for q in range(2):
                                rows = slice(64 * q, 64 * q + 64)
                                dve.wait_ge(ws_done[q], ONE + c + 1)
                                nc.vector.tensor_tensor(uo[p][rows, :, :], ub[p][rows, :, :],
                                                        ps[rows, 0, 0:2 * C].rearrange("p (g w) -> p g w", g=2),
                                                        ALU.subtract).then_inc(uo_done[q], 1)
                            for q in range(2):
                                rows = slice(64 * q, 64 * q + 64)
                                dve.wait_ge(uh_done[q], ONE + c + 1)
                                nc.vector.tensor_tensor(ul[p][rows, :, :], uo[p][rows, :, :], uh[p][rows, :, :],
                                                        ALU.subtract).then_inc(ul_done[q], 1)
                            for q in range(2):
                                dve.wait_ge(up_done[q], ONE + c + 1)
                                nc.vector.tensor_tensor(
                                    s_sb[:, 2 * q:2 * q + 2, :, :],
                                    ps[0:HC, 4 + 2 * q:6 + 2 * q, 0:4 * HC].rearrange("p a (g w) -> p a g w", w=HC),
                                    cst[0:HC, BM0:BM0 + HC].unsqueeze(1).unsqueeze(1).broadcast_to([HC, 2, 4, HC]),
                                    ALU.mult).then_inc(s_ready[q], 1)

                @block.scalar
                def _(act):
                    with act.Fori(0, NC // 2) as r:
                        for p in range(2):
                            for q in range(2):
                                rows = slice(64 * q, 64 * q + 64)
                                act.wait_ge(uo_done[q], ONE + 2 * r + p + 1)
                                nc.scalar.activation(uh[p][rows, :, :], uo[p][rows, :, :], ACT.Copy)\
                                    .then_inc(uh_done[q], 1)
                            for bb in range(4):
                                for s in range(2):
                                    rows = slice(32 * bb + CH * s, 32 * bb + CH * s + CH)
                                    act.dma_start(
                                        d_u[s, 2 * bb:2 * bb + 2, ds(2 * r + p, 1), :, :].rearrange("g c i w -> i (g c) w"),
                                        uo[p][rows, :, :]).then_inc(st_u[p], 16)
                            act.wait_ge(fs_sc, ONE + 2 * r + p + 1)
                            if p == 0:
                                nc.scalar.activation(fch[:, :, ds(r, 1), :].rearrange("p a e n -> p (a e) n"), fcs[:, :, :],
                                                     ACT.Copy).then_inc(fs_hi, 1)
                            else:
                                nc.scalar.activation(pjh[:, ds(r, 1), :].rearrange("p e n -> p (e n)"), pjs[:, :],
                                                     ACT.Copy).then_inc(fs_hi, 1)
                    for p in range(2):
                        act.wait_ge(st_u[p], ONE + 16 * 8 * NC // 2)

                @block.tensor
                def _(pe):
                    pe.wait_ge(zu, ONE + 1)
                    for bb in range(4):
                        nc.tensor.matmul(ps[0:HC, 4 + bb, 0:4 * HC], zero[0:32, 0:HC], zero[0:32, 0:4 * HC],
                                         start=True, stop=False, skip_group_check=True)
                    with pe.Fori(0, NC // 2) as r:
                        for p in range(2):
                            c = 2 * r + p
                            pe.wait_ge(sc_ld[p], ONE + 16 * 9 * (r + 1))
                            for q in range(2):
                                pe.wait_ge(s_ready[q], ONE + c + 1)
                                pe.wait_ge(uo_done[q], ONE + c)
                                for bb in (2 * q, 2 * q + 1):
                                    for g in range(4):
                                        bg, hf = g // 2, g % 2
                                        o = ((2 * bb + bg) * 2 + hf) * 2 * CH
                                        last = nc.tensor.matmul(ps[32 * bb:32 * bb + 32, 0, g * HC:(g + 1) * HC],
                                                                wqs[p][:, o:o + 2 * CH], s_sb[:, bb, g, :],
                                                                start=True, stop=True)
                                last.then_inc(ws_done[q], 1)
                            for q in range(2):
                                pe.wait_ge(ul_done[q], ONE + c + 1)
                                for part in range(3):
                                    for g in range(4):
                                        for bb in (2 * q, 2 * q + 1):
                                            bg, hf = g // 2, g % 2
                                            rows, w = slice(32 * bb, 32 * bb + CH), slice(hf * HC, (hf + 1) * HC)
                                            last = nc.tensor.matmul(ps[0:HC, 4 + bb, g * HC:(g + 1) * HC],
                                                                    ks[p][rows, bg, part // 2, w],
                                                                    (uh, ul, uh)[part][p][rows, bg, w],
                                                                    start=False, stop=False, skip_group_check=True)
                                last.then_inc(up_done[q], 1)

        with ExitStack() as outp:
            def sbo(name, shape, dt=f32):
                return outp.enter_context(nc.sbuf_tensor(name, shape, dt))

            ut = [sbo(f"ut{u}", [128, C]) for u in range(2)]
            qs = [sbo(f"qs{u}", [128, C]) for u in range(2)]
            pt = [sbo(f"pt{u}", [128, H, 2 * CH]) for u in range(2)]
            ow = [sbo(f"ow{u}", [128, C]) for u in range(2)]
            oT = [sbo(f"oT{u}", [HC, 2, TP]) for u in range(2)]
            ld_o, pu_done, o_done, o_t, o_out, y_done, y_out = (
                sem2("ld_o"), sem2("pu_done"), sem2("o_done"), sem2("o_t"), sem2("o_out"), sem2("y_done"), sem2("y_out"))
            bn2, mv2, sq2, s_dv2 = sem("bn2"), sem("mv2"), sem("sq2"), sem("s_dv2")

            with nc.Block() as block:

                @block.sync
                def _(sp):
                    start_at_one(sp)
                    with sp.Fori(0, B) as r:
                        for u in range(2):
                            t = 2 * r + u
                            sp.wait_ge(pu_done[u], ONE + r)
                            sp.wait_ge(o_done[u], ONE + r)
                            for s, dst in enumerate((ut[u], qs[u])):
                                sp.dma_start(dst[:, :], d_u[s, ds(r, 1), 8 * u:8 * u + 8, :, :]
                                             .rearrange("b c i w -> (b c i) w")).then_inc(ld_o[u], 16)
                            sp.dma_start(pt[u][:, :, :].rearrange("p h i -> p (h i)"),
                                         d_pt[ds(t, 1), :, :].rearrange("t p c -> (t p) c")).then_inc(ld_o[u], 16)

                @block.vector
                def _(dve):
                    with dve.Fori(0, B) as r:
                        for u in range(2):
                            dve.wait_ge(pu_done[u], ONE + r + 1)
                            dve.wait_ge(o_t[u], ONE + r)
                            nc.vector.tensor_tensor(ow[u][:, :], ps[:, u, 0:C], qs[u][:, :], ALU.subtract)\
                                .then_inc(o_done[u], 1)
                        for u in range(2):
                            xt = r_sb[:, ds(2 * r + u, 1), :].rearrange("p t c -> p (t c)")
                            dve.wait_ge(y_done[u], ONE + r + 1)
                            nc.vector.tensor_tensor(xt, ps[:, 4 + u, 0:C], xt, ALU.add).then_inc(y_out[u], 1)
                    for u in range(2):
                        dve.wait_ge(y_out[u], ONE + B)
                    for t in range(NT):
                        last = nc.vector.bn_stats(st_sb[:, t, :], r_sb[:, t, :])
                    last.then_inc(bn2, 1)
                    dve.wait_ge(bn2, ONE + 1)
                    count = [0]

                    def chain(ins):
                        count[0] += 1
                        ins.then_inc(s_dv2, 1)
                        dve.wait_ge(s_dv2, ONE + count[0])

                    norm_statistics(chain, mv2)
                    dve.wait_ge(sq2, ONE + 1)
                    chain(nc.vector.reciprocal(rstd[:, :], rstd[:, :]))

                @block.scalar
                def _(act):
                    with act.Fori(0, B) as r:
                        for u in range(2):
                            act.wait_ge(o_t[u], ONE + r + 1)
                            act.wait_ge(y_done[u], ONE + r)
                            nc.scalar.activation(oT[u][:, :, :].rearrange("p a n -> p (a n)"), ps[0:HC, 2 + u, 0:2 * TP],
                                                 ACT.Copy).then_inc(o_out[u], 1)
                    act.wait_ge(mv2, ONE + 1)
                    nc.scalar.activation(rstd[:, :], tmpa[:, :], ACT.Sqrt, bias=eps_c[:, 1:2]).then_inc(sq2, 1)

                @block.tensor
                def _(pe):
                    with pe.Fori(0, B) as r:
                        for u in range(2):
                            by_constant(pe, 48 * (r + 1), r)
                            pe.wait_ge(ld_o[u], ONE + 48 * (r + 1))
                            pe.wait_ge(o_done[u], ONE + r)
                            for h in range(H):
                                for g in range(4):
                                    rows = slice(32 * g, 32 * g + 32)
                                    last = nc.tensor.matmul(ps[rows, u, D * h:D * h + D], pt[u][rows, h, :],
                                                            ut[u][rows, D * h:D * h + D], start=True, stop=True)
                            last.then_inc(pu_done[u], 1)
                        for u in range(2):
                            pe.wait_ge(o_done[u], ONE + r + 1)
                            pe.wait_ge(o_out[u], ONE + r)
                            for hf in range(2):
                                last = nc.tensor.transpose(ps[0:HC, 2 + u, hf * TP:(hf + 1) * TP],
                                                           ow[u][:, hf * HC:(hf + 1) * HC], ident)
                            last.then_inc(o_t[u], 1)
                        for u in range(2):
                            pe.wait_ge(o_out[u], ONE + r + 1)
                            pe.wait_ge(y_out[u], ONE + r)
                            for hf in range(2):
                                last = nc.tensor.matmul(ps[:, 4 + u, 0:C], oT[u][:, hf, :], wo_sb[:, hf, :],
                                                        start=(hf == 0), stop=(hf == 1))
                            last.then_inc(y_done[u], 1)

        xh = [sb(f"xh{u}", [HC + 1, 2, TP], f16) for u in range(2)]
        xl = [sb(f"xl{u}", [HC + 1, 2, TP], f16) for u in range(2)]
        rows = [sb(f"rows{k}", [128, NT, RW]) for k in range(2)]
        idle = [sb(f"idle{u}", [128, RW]) for u in range(2)]
        gth = sb("gth", [HC + 1, 2, E], f16)
        gtl = sb("gtl", [HC + 1, 2, E], f16)
        gts = sb("gts", [HC + 1, 2, E])
        bps = sb("bps", [1, E, C])
        bph = sb("bph", [1, E, C], f16)
        bpl = sb("bpl", [1, E, C], f16)
        bpw = sb("bpw", [2, E, C], f16)
        ones = sb("ones", [128, TP], f16)
        tri = sb("tri", [128, TP], f16)
        xw = [sb(f"xw{u}", [128, C]) for u in range(2)]
        sc = sb("sc", [128, NT, E])
        sel = [sb(f"sel{k}", [128, NT, E]) for k in range(2)]
        taken = sb("taken", [128, NT, E], f16)
        key = sb("key", [128, NT, E])
        pos = sb("pos", [128, NT, E])
        top = [sb(f"top{k}", [128, NT]) for k in range(2)]
        kmax = sb("kmax", [128, NT])
        g1 = sb("g1", [128, NT])
        g2 = sb("g2", [128, NT])
        load = sb("load", [128, E])
        more = sb("more", [128, E, NT])
        tiles = sb("tiles", [128, E])
        before = sb("before", [128, E, E])
        base = sb("base", [128, E])
        ends = sb("ends", [128, E])
        past = sb("past", [1, ST, E - 1])
        owner_f = sb("owner_f", [1, ST])
        owner = sb("owner", [1, ST], mybir.dt.int32)
        slot_f = sb("slot_f", [128, NT])
        slot = [sb(f"slot{k}", [128, NT], mybir.dt.uint32) for k in range(2)]
        s_g, g_split, s_rt, ex_in, ex_done, s_fill, s_bp = (
            sem("s_g"), sem("g_split"), sem("s_rt"), sem("ex_in"), sem("ex_done"), sem("s_fill"), sem("s_bp"))
        tk_done, rk_done, slots_done, gate_in = sem("tk_done"), sem("rk_done"), sem("slots_done"), sem("gate_in")
        xw_done, xc_done, x_t, xh_done, xl_done, sc_done, sc_out = (
            sem2("xw_done"), sem2("xc_done"), sem2("x_t"), sem2("xh_done"), sem2("xl_done"), sem2("sc_done"),
            sem2("sc_out"))
        s_sct = ctx.enter_context(nc.semaphore("s_sct"))

        with nc.Block() as block:

            @block.sync
            def _(sp):
                start_at_one(sp)
                sp.dma_start(gts[:, :, :], gate.rearrange("p (a n) -> p a n", a=2)).then_inc(s_g, 16)
                sp.dma_start(bps[:, :, :], bproj.rearrange("(a e) n -> a e n", a=1)).then_inc(s_g, 16)
                sp.wait_ge(g_split, ONE + IDLE_STEPS)
                for u in range(2):
                    sp.dma_start(d_x[:, u, :, :].rearrange("a p c -> p a c"),
                                 idle[u][:, :].unsqueeze(1).broadcast_to([128, (ST + 2) // 2, RW])).then_inc(s_fill, 16)
                sp.wait_ge(g_split, ONE + IDLE_STEPS + 13)
                sp.dma_start(bpw[0:1, :, :], bph[:, :, :]).then_inc(s_bp, 16)
                sp.dma_start(bpw[1:2, :, :], bpl[:, :, :]).then_inc(s_bp, 16)
                sp.wait_ge(s_g, ONE + 32)
                sp.wait_ge(s_bp, ONE + 32)
                sp.wait_ge(s_fill, ONE + 32)

            @block.gpsimd
            def _(pool):
                done = 0
                for step in (
                    lambda: nc.gpsimd.memset(idle[0][:, :], 0.0),
                    lambda: nc.gpsimd.tensor_copy(idle[0][:, C:C + 1], cst[:, DM0:DM0 + 1]),
                    lambda: nc.gpsimd.memset(idle[1][:, :], 0.0),
                    lambda: nc.gpsimd.tensor_copy(idle[1][:, C:C + 1], cst[:, DM0 + 1:DM0 + 2]),
                    lambda: nc.gpsimd.tensor_copy(gth[:, :, :], gts[:, :, :]),
                    lambda: nc.gpsimd.tensor_tensor(gtl[:, :, :], gts[:, :, :], gth[:, :, :], ALU.subtract),
                    lambda: nc.gpsimd.memset(xh[0][HC:HC + 1, :, :], 1.0),
                    lambda: nc.gpsimd.memset(xh[1][HC:HC + 1, :, :], 1.0),
                    lambda: nc.gpsimd.memset(xl[0][HC:HC + 1, :, :], 0.0),
                    lambda: nc.gpsimd.memset(xl[1][HC:HC + 1, :, :], 0.0),
                    lambda: nc.gpsimd.memset(ones[:, :], 1.0),
                    lambda: nc.gpsimd.tensor_copy(tri[:, :], cst[:, TR0:TR0 + TP]),
                    lambda: nc.gpsimd.tensor_copy(rows[0][:, :, C], cst[:, DI0:DI0 + NT]),
                    lambda: nc.gpsimd.tensor_copy(rows[1][:, :, C], cst[:, DI0 + NT:DI0 + 2 * NT]),
                    lambda: nc.gpsimd.tensor_scalar(bps[:, :, :], bps[:, :, :], WSCALE / 8, 8.0, ALU.mult, ALU.mult),
                    lambda: nc.gpsimd.tensor_copy(bph[:, :, :], bps[:, :, :]),
                    lambda: nc.gpsimd.tensor_tensor(bpl[:, :, :], bps[:, :, :], bph[:, :, :], ALU.subtract),
                ):
                    if done == IDLE_STEPS:
                        pool.wait_ge(s_g, ONE + 32)
                    step().then_inc(g_split, 1)
                    done += 1
                    pool.wait_ge(g_split, ONE + done)
                pool.wait_ge(s_fill, ONE + 32)
                pool.wait_ge(slots_done, ONE + 2)
                for u in range(2):
                    pool.wait_ge(xc_done[u], ONE + 2 * B)
                for t in range(NT):
                    for k in range(2):
                        nc.gpsimd.indirect_dma_start(
                            d_x.rearrange("a u p c -> (a u p) c"),
                            bass.IndirectOffsetOnAxis(ap=slot[k][:, t:t + 1], axis=0),
                            rows[k][:, t, :], None).then_inc(s_sct, 16)
                pool.wait_ge(s_sct, 16 * 2 * NT)

            @block.vector
            def _(dve):
                with dve.Fori(0, B) as r:
                    for u in range(2):
                        t = 2 * r + u
                        dve.wait_ge(x_t[u], ONE + r)
                        dve.wait_ge(xc_done[u], ONE + 2 * r)
                        nc.vector.tensor_scalar(xw[u][:, :],
                                                r_sb[:, ds(t, 1), :].rearrange("p t c -> p (t c)"),
                                                mean[:, ds(t, 1)], rstd[:, ds(t, 1)], ALU.subtract, ALU.mult)\
                            .then_inc(xw_done[u], 1)
                    for u in range(2):
                        dve.wait_ge(xh_done[u], ONE + r + 1)
                        nc.vector.tensor_tensor(xl[u][0:HC, :, :],
                                                ps[0:HC, u, 0:2 * TP].rearrange("p (h n) -> p h n", h=2),
                                                xh[u][0:HC, :, :], ALU.subtract).then_inc(xl_done[u], 1)
                    for u in range(2):
                        dve.wait_ge(sc_done[u], ONE + r + 1)
                        nc.vector.tensor_copy(sc[:, ds(2 * r + u, 1), :].rearrange("p t e -> p (t e)"),
                                              ps[:, 2 + u, 0:E]).then_inc(sc_out[u], 1)
                for u in range(2):
                    dve.wait_ge(sc_out[u], ONE + B)
                count = [0]

                def chain(ins):
                    count[0] += 1
                    ins.then_inc(s_rt, 1)
                    dve.wait_ge(s_rt, ONE + count[0])

                def wide(ap):
                    return ap.unsqueeze(2).broadcast_to([128, NT, E])

                first = cst[:, TB0:TB0 + E].unsqueeze(1).broadcast_to([128, NT, E])
                for k in range(2):
                    chain(nc.vector.tensor_reduce(top[k][:, :], sc[:, :, :], AX.X, ALU.max))
                    chain(nc.vector.tensor_tensor(key[:, :, :], sc[:, :, :], wide(top[k][:, :]), ALU.is_equal))
                    chain(nc.vector.tensor_tensor(key[:, :, :], key[:, :, :], first, ALU.mult))
                    chain(nc.vector.tensor_reduce(kmax[:, :], key[:, :, :], AX.X, ALU.max))
                    chain(nc.vector.tensor_tensor(sel[k][:, :, :], key[:, :, :], wide(kmax[:, :]), ALU.is_equal))
                    if k == 0:
                        chain(nc.vector.scalar_tensor_tensor(sc[:, :, :], sel[0][:, :, :], -1e30, sc[:, :, :],
                                                             ALU.mult, ALU.add))
                nc.vector.tensor_tensor(taken[:, :, :], sel[0][:, :, :], sel[1][:, :, :], ALU.add).then_inc(tk_done, 1)
                nc.vector.tensor_tensor(g2[:, :], top[1][:, :], top[0][:, :], ALU.subtract).then_inc(ex_in, 1)
                dve.wait_ge(rk_done, ONE + 1)
                chain(nc.vector.tensor_copy(load[:, :], ps[:, 5, 0:E]))
                chain(nc.vector.tensor_tensor(more[:, :, :], load[:, :].unsqueeze(2).broadcast_to([128, E, NT]),
                                              cst[:, TS0:TS0 + NT].unsqueeze(1).broadcast_to([128, E, NT]), ALU.is_gt))
                chain(nc.vector.tensor_reduce(tiles[:, :], more[:, :, :], AX.X, ALU.add))
                chain(nc.vector.tensor_tensor(before[:, :, :], tiles[:, :].unsqueeze(1).broadcast_to([128, E, E]),
                                              cst[:, EB0:EB0 + E * E].rearrange("p (a b) -> p a b", a=E), ALU.mult))
                chain(nc.vector.tensor_reduce(base[:, :], before[:, :, :], AX.X, ALU.add))
                chain(nc.vector.tensor_tensor(ends[:, :], base[:, :], tiles[:, :], ALU.add))
                chain(nc.vector.tensor_tensor(past[:, :, :], cst[0:1, TI0:TI0 + ST].unsqueeze(2).broadcast_to([1, ST, E - 1]),
                                              ends[0:1, 0:E - 1].unsqueeze(1).broadcast_to([1, ST, E - 1]), ALU.is_ge))
                chain(nc.vector.tensor_reduce(owner_f[:, :], past[:, :, :], AX.X, ALU.add))
                chain(nc.vector.tensor_copy(owner[:, :], owner_f[:, :]))
                chain(nc.vector.tensor_scalar(base[:, :], base[:, :], float(TP), None, ALU.mult))
                chain(nc.vector.tensor_tensor(pos[:, :, :], ps[:, 4, 0:NT * E].rearrange("p (t e) -> p t e", e=E),
                                              base[:, :].unsqueeze(1).broadcast_to([128, NT, E]), ALU.add))
                for k in range(2):
                    chain(nc.vector.tensor_tensor(key[:, :, :], sel[k][:, :, :], pos[:, :, :], ALU.mult))
                    chain(nc.vector.tensor_reduce(slot_f[:, :], key[:, :, :], AX.X, ALU.add))
                    chain(nc.vector.tensor_copy(slot[k][:, :], slot_f[:, :]))
                dve.wait_ge(ex_done, ONE + 1)
                chain(nc.vector.tensor_scalar(g1[:, :], g2[:, :], 1.0, None, ALU.add))
                chain(nc.vector.reciprocal(g1[:, :], g1[:, :]))
                chain(nc.vector.tensor_tensor(g2[:, :], g2[:, :], g1[:, :], ALU.mult))
                for k, g in enumerate((g1, g2)):
                    nc.vector.tensor_scalar(rows[k][:, :, C + 1], g[:, :], 1.0 / WSCALE, None, ALU.mult)\
                        .then_inc(slots_done, 1)

            @block.scalar
            def _(act):
                with act.Fori(0, B) as r:
                    for u in range(2):
                        t = 2 * r + u
                        act.wait_ge(x_t[u], ONE + r + 1)
                        act.wait_ge(sc_done[u], ONE + r)
                        nc.scalar.activation(xh[u][0:HC, :, :],
                                             ps[0:HC, u, 0:2 * TP].rearrange("p (h n) -> p h n", h=2), ACT.Copy)\
                            .then_inc(xh_done[u], 1)
                    for u in range(2):
                        act.wait_ge(xw_done[u], ONE + r + 1)
                        for k in range(2):
                            nc.scalar.activation(rows[k][:, ds(2 * r + u, 1), 0:C].rearrange("p t c -> p (t c)"),
                                                 xw[u][:, :], ACT.Copy).then_inc(xc_done[u], 1)
                act.wait_ge(ex_in, ONE + 1)
                nc.scalar.activation(g2[:, :], g2[:, :], ACT.Exp).then_inc(ex_done, 1)

            @block.tensor
            def _(pe):
                pe.wait_ge(g_split, ONE + IDLE_STEPS + 8)
                with pe.Fori(0, B) as r:
                    for u in range(2):
                        pe.wait_ge(xw_done[u], ONE + r + 1)
                        pe.wait_ge(xl_done[u], ONE + r)
                        for hf in range(2):
                            last = nc.tensor.transpose(ps[0:HC, u, hf * TP:(hf + 1) * TP],
                                                       xw[u][:, hf * HC:(hf + 1) * HC], ident)
                        last.then_inc(x_t[u], 1)
                    for u in range(2):
                        pe.wait_ge(xl_done[u], ONE + r + 1)
                        pe.wait_ge(sc_out[u], ONE + r)
                        k = 0
                        for hf in range(2):
                            for xs, gs in ((xh, gth), (xh, gtl), (xl, gth)):
                                last = nc.tensor.matmul(ps[:, 2 + u, 0:E], xs[u][0:HC + hf, hf, :],
                                                        gs[0:HC + hf, hf, :], start=(k == 0), stop=(k == 5))
                                k += 1
                        last.then_inc(sc_done[u], 1)
                pe.wait_ge(tk_done, ONE + 1)
                flat = taken[:, :, :].rearrange("p t e -> p (t e)")
                nc.tensor.matmul(ps[:, 4, 0:NT * E], tri[:, :], flat, start=True, stop=False, skip_group_check=True)
                for d in range(1, NT):
                    nc.tensor.matmul(ps[:, 4, d * E:NT * E], ones[:, :], flat[:, 0:(NT - d) * E], start=False,
                                     stop=(d == NT - 1), skip_group_check=True)
                for t in range(NT):
                    last = nc.tensor.matmul(ps[:, 5, 0:E], ones[:, :], taken[:, t, :], start=(t == 0),
                                            stop=(t == NT - 1))
                last.then_inc(rk_done, 1)

        HH = HID // 2
        HM = HB // 2
        row = [sb(f"row{u}", [128, RW]) for u in range(2)]
        tag = [sb(f"tag{u}", [128, 2]) for u in range(2)]
        dest = [sb(f"dest{u}", [128, 1], mybir.dt.uint32) for u in range(2)]
        yo = [sb(f"yo{u}", [128, C]) for u in range(2)]
        scrap = sb("scrap", [1, 2])
        hw = [sb(f"hw{u}", [128, 2, HH]) for u in range(2)]
        hh = [sb(f"hh{u}", [128, 2, HH], f16) for u in range(2)]
        hl = [sb(f"hl{u}", [128, 2, HH], f16) for u in range(2)]
        rw_ld, tagged, xs_t, xsh, xsl, up_done, hw_done, hh_done, hl_done, dn_done, y_done, y_free = (
            sem2("rw_ld"), sem2("tagged"), sem2("xs_t"), sem2("xsh"), sem2("xsl"), sem2("fc_done"), sem2("hw_done"),
            sem2("hh_done"), sem2("hl_done"), sem2("dn_done"), sem2("ye_done"), sem2("ye_free"))
        s_ysc = [ctx.enter_context(nc.semaphore(f"s_ysc{u}")) for u in range(2)]

        with nc.Block() as block:

            @block.sync
            def _(sp):
                start_at_one(sp)
                for u in range(2):
                    sp.dma_start(row[u][:, :], d_x[0, u, :, :]).then_inc(rw_ld[u], 16)
                with sp.Fori(0, ST // 2) as r:
                    for u in range(2):
                        sp.wait_ge(tagged[u], ONE + r + 1)
                        sp.dma_start(row[u][:, :], d_x[ds(r + 1, 1), u, :, :].rearrange("a p c -> (a p) c"))\
                            .then_inc(rw_ld[u], 16)

            @block.tensor
            def _(pe):
                def transposes(u):
                    for hf in range(2):
                        last = nc.tensor.transpose(ps[0:HC, 4 + u, hf * TP:(hf + 1) * TP],
                                                   row[u][:, hf * HC:(hf + 1) * HC], ident)
                    last.then_inc(xs_t[u], 1)

                def up(u, e, r):
                    pe.wait_ge(xsl[u], ONE + r + 1)
                    pe.wait_ge(hw_done[u], ONE + 2 * r)
                    for m in range(HB):
                        k = 0
                        for hf in range(2):
                            K = HC + hf
                            for ws, xs in ((fch, xh), (fch, xl), (fcl, xh)):
                                last = nc.tensor.matmul(
                                    ps[:, 2 * u + m // HM, (m % HM) * TP:(m % HM + 1) * TP],
                                    ws[0:K, hf, ds(e, 1), m * 128:(m + 1) * 128].rearrange("p e n -> p (e n)"),
                                    xs[u][0:K, hf, :], start=(k == 0), stop=(k == 5))
                                k += 1
                        if m % HM == HM - 1:
                            last.then_inc(up_done[u], 1)

                def down(u, e, r):
                    pe.wait_ge(y_done[u], ONE + 2 * r)
                    y = ps[:, 6 + u, 0:C]
                    for m in range(HB):
                        if m % HM == 0:
                            pe.wait_ge(hl_done[u], ONE + 2 * r + m // HM + 1)
                        for k, (hs, ws) in enumerate(((hh, pjh), (hh, pjl), (hl, pjh))):
                            nc.tensor.matmul(y, hs[u][:, m // HM, (m % HM) * TP:(m % HM + 1) * TP],
                                             ws[:, ds(e, 1), m * C:(m + 1) * C].rearrange("p e n -> p (e n)"),
                                             start=(m == 0 and k == 0), stop=False)
                    nc.tensor.matmul(y, ones[0:2, :], bpw[:, ds(e, 1), :].rearrange("p e n -> p (e n)"), start=False,
                                     stop=True).then_inc(dn_done[u], 1)

                for u in range(2):
                    pe.wait_ge(rw_ld[u], ONE + 16)
                    transposes(u)
                with pe.Fori(0, ST // 2) as r:
                    e = [pe.value_load(owner[0:1, ds(2 * r + u, 1)], min_val=0, max_val=E - 1) for u in range(2)]
                    for u in range(2):
                        up(u, e[u], r)
                    down(0, e[0], r)
                    for u in range(2):
                        pe.wait_ge(rw_ld[u], ONE + 16 * (r + 2))
                        transposes(u)
                    down(1, e[1], r)

            @block.scalar
            def _(act):
                def high(u):
                    nc.scalar.activation(xh[u][0:HC, :, :],
                                         ps[0:HC, 4 + u, 0:2 * TP].rearrange("p (h n) -> p h n", h=2), ACT.Copy)\
                        .then_inc(xsh[u], 1)

                for u in range(2):
                    act.wait_ge(xs_t[u], ONE + 1)
                    high(u)
                with act.Fori(0, ST // 2) as r:
                    for u in range(2):
                        for i in range(2):
                            act.wait_ge(up_done[u], ONE + 2 * r + i + 1)
                            act.wait_ge(hl_done[u], ONE + 2 * r)
                            nc.scalar.activation(hw[u][:, i, :], ps[:, 2 * u + i, 0:HH], ACT.Gelu_apprx_tanh,
                                                 scale=1.0 / WSCALE).then_inc(hw_done[u], 1)
                    for u in range(2):
                        act.wait_ge(xs_t[u], ONE + r + 2)
                        high(u)

            @block.vector
            def _(dve):
                def low(u):
                    nc.vector.tensor_tensor(xl[u][0:HC, :, :],
                                            ps[0:HC, 4 + u, 0:2 * TP].rearrange("p (h n) -> p h n", h=2),
                                            xh[u][0:HC, :, :], ALU.subtract).then_inc(xsl[u], 1)

                def keep_tag(u):
                    nc.vector.tensor_copy(tag[u][:, :], row[u][:, C:C + 2]).then_inc(tagged[u], 1)

                for u in range(2):
                    dve.wait_ge(rw_ld[u], ONE + 16)
                    dve.wait_ge(xsh[u], ONE + 1)
                    low(u)
                    keep_tag(u)
                with dve.Fori(0, ST // 2) as r:
                    for u in range(2):
                        for i in range(2):
                            dve.wait_ge(hw_done[u], ONE + 2 * r + i + 1)
                            dve.wait_ge(dn_done[u], ONE + r)
                            nc.vector.tensor_copy(hh[u][:, i, :], hw[u][:, i, :]).then_inc(hh_done[u], 1)
                            dve.wait_ge(hh_done[u], ONE + 2 * r + i + 1)
                            nc.vector.tensor_tensor(hl[u][:, i, :], hw[u][:, i, :], hh[u][:, i, :], ALU.subtract)\
                                .then_inc(hl_done[u], 1)
                    for u in range(2):
                        dve.wait_ge(y_free[u], ONE + r)
                        dve.wait_ge(tagged[u], ONE + r + 1)
                        nc.vector.tensor_copy(dest[u][:, :], tag[u][:, 0:1]).then_inc(y_done[u], 1)
                        dve.wait_ge(dn_done[u], ONE + r + 1)
                        nc.vector.tensor_scalar(yo[u][:, :], ps[:, 6 + u, 0:C], tag[u][:, 1:2], None, ALU.mult)\
                            .then_inc(y_done[u], 1)
                        if u == 0:
                            for w in range(2):
                                dve.wait_ge(xsh[w], ONE + r + 2)
                                low(w)
                        dve.wait_ge(y_done[u], ONE + 2 * r + 2)
                        dve.wait_ge(rw_ld[u], ONE + 16 * (r + 2))
                        keep_tag(u)

            @block.gpsimd
            def _(pool):
                with pool.Fori(0, ST // 2) as r:
                    for u in range(2):
                        by_constant(pool, 2 * r + 2)
                        pool.wait_ge(y_done[u], ONE + 2 * r + 2)
                        nc.gpsimd.indirect_dma_start(d_y, bass.IndirectOffsetOnAxis(ap=dest[u][:, :], axis=0),
                                                     yo[u][:, :], None).then_inc(s_ysc[u], 16)
                    for u in range(2):
                        by_constant(pool, 16 * (r + 1) - ONE)
                        pool.wait_ge(s_ysc[u], 16 * (r + 1))
                        nc.gpsimd.memset(scrap[:, u:u + 1], 0.0).then_inc(y_free[u], 1)

        PT = 4
        ya = [rows[k][:, :, 0:C] for k in range(2)]
        ya_ld = [sem(f"ya_ld{i}") for i in range(NT // PT)]
        added, s_add, s_out = sem("added"), sem("s_add"), sem("s_out")

        with nc.Block() as block:

            def loads(eng, k):
                for i in range(NT // PT):
                    eng.dma_start(ya[k][:, i * PT:(i + 1) * PT, :],
                                  d_y[(k * NT + i * PT) * TP:(k * NT + (i + 1) * PT) * TP, :]
                                  .rearrange("(t p) c -> p t c", p=TP)).then_inc(ya_ld[i], 16)

            @block.sync
            def _(sp):
                start_at_one(sp)
                loads(sp, 0)
                for i in range(NT // PT):
                    sp.wait_ge(added, ONE + i + 1)
                    sp.dma_start(out.rearrange("p (t c) -> p t c", t=NT)[:, i * PT:(i + 1) * PT, :],
                                 r_sb[:, i * PT:(i + 1) * PT, :]).then_inc(s_out, 16)
                sp.wait_ge(s_out, ONE + 16 * NT // PT)

            @block.scalar
            def _(act):
                act.wait_ge(ya_ld[0], ONE)
                loads(act, 1)

            @block.vector
            def _(dve):
                for i in range(NT // PT):
                    piece = r_sb[:, i * PT:(i + 1) * PT, :]
                    dve.wait_ge(ya_ld[i], ONE + 32)
                    nc.vector.tensor_tensor(piece, piece, ya[0][:, i * PT:(i + 1) * PT, :], ALU.add).then_inc(s_add, 1)
                    dve.wait_ge(s_add, ONE + i + 1)
                    nc.vector.tensor_tensor(piece, piece, ya[1][:, i * PT:(i + 1) * PT, :], ALU.add).then_inc(added, 1)


def constants():
    import numpy as np
    p = np.arange(128)
    i, par = p % CH, p // CH % 2
    col = np.arange(2 * CH)
    same = par[:, None] == (col // CH)[None]
    t = np.zeros((128, CW), np.float32)
    t[:, ID0:ID0 + 128] = np.eye(128)
    t[:, MS0:MS0 + 32] = same & ((col % CH)[None] < i[:, None])
    t[:, MU0:MU0 + 32] = same & ((col % CH)[None] >= i[:, None])
    t[:, MP0:MP0 + 2] = par[:, None] == np.arange(2)[None]
    t[:, BM0:BM0 + HC] = (p // D)[:, None] == (np.arange(HC) // D)[None]
    t[:, TB0:TB0 + E] = E - np.arange(E)
    t[:, TR0:TR0 + TP] = p[:, None] < np.arange(TP)[None]
    t[:, TS0:TS0 + NT] = TP * np.arange(NT)
    t[:, EB0:EB0 + E * E] = (np.arange(E)[None] < np.arange(E)[:, None]).reshape(-1)
    t[:, TI0:TI0 + ST] = np.arange(ST)
    t[:, DI0:DI0 + 2 * NT] = TP * np.arange(2 * NT)[None] + p[:, None]
    t[:, DM0:DM0 + 2] = 2 * NT * TP + TP * np.arange(2)[None] + p[:, None]
    return t


def kernel(**inputs):
    import numpy as np
    import concourse.bacc as bacc
    from concourse.bass_utils import run_bass_kernel_spmd

    a = {k: np.asarray(v) for k, v in inputs.items()}

    def halves(w):
        return np.ascontiguousarray(w.reshape(2, HC, -1).transpose(1, 0, 2).reshape(HC, -1))

    def halves_and_bias(w, bias):
        full = np.zeros((HC + 1, 2, w.shape[1]), w.dtype)
        full[:HC] = w.reshape(2, HC, -1).transpose(1, 0, 2)
        full[HC, 1] = bias
        return full

    by_head = lambda w: w.reshape(C, H, D)
    kv = np.concatenate([by_head(a["L0_conv_Wk"]), by_head(a["L0_conv_Wv"])], axis=2).reshape(C, KVW)
    wqkvb = np.concatenate([kv, a["L0_conv_Wq"], a["L0_conv_Wb"]], axis=1)
    tokens = a["x"].reshape(B, C, L).transpose(0, 2, 1).reshape(NT, TP, C)
    fc, pj = a["L0_ffn_w_fc"], a["L0_ffn_w_proj"]
    arrays = {
        "x": tokens.transpose(1, 0, 2).reshape(TP, NT * C),
        "consts": constants(),
        "wqkvb": halves(wqkvb),
        "wo": halves(a["L0_conv_Wo"]),
        "gate": halves_and_bias(a["L0_ffn_gate_w"].T, a["L0_ffn_gate_b"]).reshape(HC + 1, 2 * E),
        "wfc": np.stack([halves_and_bias(fc[e].T, a["L0_ffn_b_fc"][e]) for e in range(E)]),
        "wproj": pj.transpose(0, 2, 1).reshape(E, HB, 128, C).transpose(0, 2, 1, 3).reshape(E, 128, HB * C),
        "bproj": a["L0_ffn_b_proj"],
    }
    arrays = {k: np.ascontiguousarray(v) for k, v in arrays.items()}
    nc = bacc.Bacc("TRN2", target_bir_lowering=False, num_devices=1)
    f32 = mybir.dt.float32
    args = [nc.dram_tensor(k, v.shape, f32, kind="ExternalInput").ap() for k, v in arrays.items()]
    args.append(nc.dram_tensor("out", (TP, NT * C), f32, kind="ExternalOutput").ap())
    program(nc, *args)
    r = run_bass_kernel_spmd(nc, [arrays], core_ids=[0])
    o = r.results[0]["out"].reshape(TP, NT, C).transpose(1, 0, 2).reshape(B, L, C)
    return np.ascontiguousarray(o.transpose(0, 2, 1)).reshape(B, C, 16, 16)
```

```python
from contextlib import ExitStack

import concourse.bass as bass
from concourse import mybir

B, C, L = 8, 192, 256
TP = 128
NT = B * L // TP
H, D, CH = 12, 16, 16
NC = L // CH
HC = C // 2
KVW = 2 * H * D
QBW = H * D + H
E, HID = 8, 768
HB = HID // 128
ID0, MS0, MU0, MP0, BM0, TB0 = 0, 128, 160, 192, 194, 290
ST = 2 * NT + E
TR0 = TB0 + E
TS0 = TR0 + TP
EB0 = TS0 + NT
IO0 = EB0 + E * E
DI0 = IO0 + TP
PI0 = DI0 + 2 * NT
DM0 = PI0 + 1
CW = DM0 + ST
PT = 4
ONE = 1
WSCALE = 64.0


def program(nc, x, consts, wqkvb, wo, gate, wfc, wproj, bproj, out):
    f32, f16 = mybir.dt.float32, mybir.dt.float16
    ALU, ACT, AX = mybir.AluOpType, mybir.ActivationFunctionType, mybir.AxisListType
    ds = bass.ds
    ctx = ExitStack()
    with ctx:
        def sb(name, shape, dt=f32):
            return ctx.enter_context(nc.sbuf_tensor(name, shape, dt))

        semaphores = []
        early = ctx.enter_context(ExitStack())
        held_by = [ctx]

        def sem(name):
            semaphores.append(held_by[0].enter_context(nc.semaphore(name)))
            return semaphores[-1]

        s_cst = sem("s_cst")

        def sem2(name):
            return [sem(f"{name}{u}") for u in range(2)]

        def dram(name, shape, dt=f32):
            return nc.dram_tensor(name, shape, dt, kind="Internal").ap()

        d_kv = dram("d_kv", (NT, TP, KVW))
        d_khl = dram("d_khl", (B, NC, CH, 2 * C), f16)
        d_n = dram("d_n", (NT, TP, C))
        d_mt = dram("d_mt", (NT, TP, C))
        d_pt = dram("d_pt", (NT, TP, 2 * C))
        d_ub = dram("d_ub", (B, NC, CH, C))
        d_q = dram("d_q", (NT, TP, C))
        d_w = dram("d_w", (NC, HC, B, 4 * CH))
        d_u = dram("d_u", (NC, 4, 2, CH, 2, C))

        d_x = dram("d_x", (NT, TP, C))
        d_y = dram("d_y", ((2 * NT + 2) * TP, C))

        cst = sb("cst", [128, CW])
        ident = cst[:, ID0:ID0 + 128]
        x_sb = sb("x_sb", [128, NT, C])
        r_sb = sb("r_sb", [128, NT, C])
        st_sb = sb("st_sb", [128, NT, 6])
        mean = sb("mean", [128, NT])
        rstd = sb("rstd", [128, NT])
        tmpa = sb("tmpa", [128, NT])
        tmpb = sb("tmpb", [128, NT])
        eps_c = sb("eps_c", [128, 3])
        beta = sb("beta", [128, NT, H])
        wqkvb_sb = sb("wqkvb_sb", [HC, 2, KVW + QBW])
        wo_sb = sb("wo_sb", [HC, 2, C])
        woh = sb("woh", [HC, 2, C], f16)
        wol = sb("wol", [HC, 2, C], f16)
        fch = sb("fch", [HC + 1, 2, E, HID], f16)
        fcl = sb("fcl", [HC + 1, 2, E, HID], f16)
        pjh = sb("pjh", [128, E, HB * C], f16)
        pjl = sb("pjl", [128, E, HB * C], f16)
        fcs = sb("fcs", [HC + 1, 2, HID])
        pjs = sb("pjs", [128, HB * C])

        ps = ctx.enter_context(nc.psum_tensor("ps", [128, 8, 512], f32))

        held_by[0] = early
        PARTS = ((0, 4), (4, NT))
        s_x, s_w, s_wo = sem2("s_x"), sem("s_w"), sem("s_wo")
        s_bn, s_mv, s_sq, s_rs = sem("s_bn"), sem("s_mv"), sem("s_sq"), sem("s_rs")
        s_dv = sem("s_dv")
        s_eps = sem("s_eps")

        started = [0]

        def start_at_one(eng, end=None):
            end = len(semaphores) if end is None else end
            for s in semaphores[started[0]:end]:
                eng.sem_inc(s, ONE)
            started[0] = end

        def by_constant(eng, *values):
            for value in values:
                eng.compute_val(ONE + value)
            eng.wait_ge(s_cst, ONE + 16)

        def norm_statistics(chain, eps_done, lo, hi):
            me, mo = st_sb[:, lo:hi, 1], st_sb[:, lo:hi, 4]
            mn, ta, tb = mean[:, lo:hi], tmpa[:, lo:hi], tmpb[:, lo:hi]
            chain(nc.vector.tensor_tensor(mn, me, mo, ALU.add))
            chain(nc.vector.tensor_scalar(mn, mn, 0.5, None, ALU.mult))
            chain(nc.vector.tensor_tensor(ta, me, mn, ALU.subtract))
            chain(nc.vector.tensor_tensor(ta, ta, ta, ALU.mult))
            chain(nc.vector.tensor_tensor(tb, st_sb[:, lo:hi, 2], st_sb[:, lo:hi, 5], ALU.add))
            nc.vector.scalar_tensor_tensor(ta, tb, 1.0 / C, ta, ALU.mult, ALU.add).then_inc(eps_done, 1)

        with ExitStack() as mix:
            def sbm(name, shape, dt=f32):
                return mix.enter_context(nc.sbuf_tensor(name, shape, dt))

            tw = [sbm(f"tw{u}", [128, 2, C]) for u in range(2)]
            tTh = [sbm(f"tTh{u}", [HC, 2, 2, TP], f16) for u in range(2)]
            tTl = [sbm(f"tTl{u}", [HC, 2, 2, TP], f16) for u in range(2)]
            wqh = sbm("wqh", [HC, 2, KVW + QBW], f16)
            wql = sbm("wql", [HC, 2, KVW + QBW], f16)
            kvw = [sbm(f"kvw{u}", [128, 2, H, 2 * D]) for u in range(2)]
            qw = [sbm(f"qw{u}", [128, 2, H, D]) for u in range(2)]
            qn = [sbm(f"qn{u}", [128, 2, H, 2 * D]) for u in range(2)]
            sqw = [sbm(f"sqw{u}", [128, 2, 2 * H, D]) for u in range(2)]
            ssw = [sbm(f"ssw{u}", [128, 2, 2 * H]) for u in range(2)]
            rnw = [sbm(f"rnw{u}", [128, 2, 2 * H]) for u in range(2)]
            khl = [sbm(f"khl{u}", [128, 2, 2, C], f16) for u in range(2)]
            kqT = [sbm(f"kqT{u}", [128, 3, 2, TP]) for u in range(2)]
            early_s = sbm("early_s", [1, 4])
            gm = sbm("gm", [128, 3, 4, 2 * CH])
            nw = [sbm(f"nw{u}", [128, 3, 4, CH]) for u in range(2)]
            ptw = [sbm(f"ptw{u}", [128, 3, 4, 2 * CH]) for u in range(2)]
            lane_n = sbm("lane_n", [128, CH, H, CH])
            lane_m = sbm("lane_m", [128, CH, H, CH])
            prod = sbm("prod", [128, H * CH * CH // 4])

            t_ready, t_added, tT_filled, tT_out = sem("t_ready"), sem("t_added"), sem("tT_filled"), sem("tT_out")
            tT_high, wq_high, wq_low = sem("tT_high"), sem("wq_high"), sem("wq_low")
            kv_done, qb_done, kv_out, qb_out = sem("kv_done"), sem("qb_done"), sem("kv_out"), sem("qb_out")
            sn_done = sem("sn_done")
            sq_done, ss_done, bt_done, rn_done, qn_in = (sem("sq_done"), sem("ss_done"), sem("bt_done"),
                                                         sem("rn_done"), sem("qn_in"))
            kn_done, khi_done, klo_done = sem("kn_done"), sem("khi_done"), sem2("klo_done")
            kT_filled, qT_filled, kT_out, qT_out = (sem("kT_filled"), sem("qT_filled"), sem("kT_out"),
                                                    sem("qT_out"))
            g_done, g_out, nb_in, n_ready = sem2("g_done"), sem("g_out"), sem("nb_in"), sem2("n_ready")
            st_kv, st_k, st_n, st_pt, st_q = (sem2("st_kv"), sem2("st_k"), sem2("st_n"), sem2("st_pt"),
                                              sem2("st_q"))
            pads = sem("pads")

            def first_use(b):
                return isinstance(b, int) and b < 2

            def batch_steps(eng, step, before_last_two=None):
                with eng.Fori(0, B // 2 - 1) as r:
                    step(2 * r, 0, r, 2)
                    step(2 * r + 1, 1, r, 2)
                if before_last_two:
                    before_last_two()
                step(B - 2, 0, B // 2 - 1, 1)
                step(B - 1, 1, B // 2 - 1, 0)

            inv_done, s_inv = sem("inv_done"), sem("s_inv")
            ln_ld = sem2("ln_ld")
            st_m = [sem(f"st_m{q}") for q in range(4)]

            with nc.Block() as block:

                @block.sync
                def _(sp):
                    start_at_one(sp)
                    for part, (lo, hi) in enumerate(PARTS):
                        sp.dma_start(x_sb[:, lo:hi, :], x.rearrange("p (t c) -> p t c", t=NT)[:, lo:hi, :])\
                            .then_inc(s_x[part], 16)
                        if part == 0:
                            sp.dma_start(wqkvb_sb[:, :, :], wqkvb.rearrange("p (a n) -> p a n", a=2)).then_inc(s_w, 16)
                            sp.dma_start(cst[:, :], consts).then_inc(s_cst, 16)
                    sp.dma_start(wo_sb[:, :, :], wo.rearrange("p (a n) -> p a n", a=2)).then_inc(s_wo, 16)

                    def store_kvq(b, u, n):
                        by_constant(sp, b + 1, n + 1)
                        sp.wait_ge(kn_done, ONE + b + 1)
                        sp.dma_start(d_kv[ds(2 * b, 2), :, :].rearrange("t p c -> p t c"),
                                     kvw[u][:, :, :, :].rearrange("p t h d -> p t (h d)")).then_inc(st_kv[u], 16)
                        sp.dma_start(d_q[ds(2 * b, 2), :, :].rearrange("t p c -> p t c"),
                                     qw[u][:, :, :, :].rearrange("p t h d -> p t (h d)")).then_inc(st_q[u], 16)
                        sp.wait_ge(khi_done, ONE + b + 1)
                        sp.wait_ge(klo_done[u], ONE + n + 1)
                        for j in range(2):
                            sp.dma_start(d_khl[ds(b, 1), 8 * j:8 * j + 8, :, :].rearrange("b c i w -> (b c i) w"),
                                         khl[u][:, j, :, :].rearrange("p s w -> p (s w)")).then_inc(st_k[u], 16)

                    def step(b, u, n, ahead):
                        if ahead:
                            store_kvq(b + 1, 1 - u, n + u)
                        for j in range(2):
                            by_constant(sp, b + 1)
                            sp.wait_ge(n_ready[j], ONE + b + 1)
                            sp.dma_start(d_n[ds(2 * b + j, 1), :, :].rearrange("t p c -> (t p) c"),
                                         nw[j][:, :, :, :].rearrange("p a r i -> p (a r i)")).then_inc(st_n[j], 16)
                            sp.dma_start(d_pt[ds(2 * b + j, 1), :, :].rearrange("t p c -> (t p) c"),
                                         ptw[j][:, :, :, :].rearrange("p a r i -> p (a r i)")).then_inc(st_pt[j], 16)

                    store_kvq(0, 0, 0)
                    def load_lanes(part, lo, hi):
                        for j in range(2):
                            sp.wait_ge(st_n[j], ONE + 16 * hi)
                        sp.dma_start(lane_n[lo * NC:hi * NC, :, :, :].rearrange("p i h j -> p (i h j)"),
                                     d_n[2 * lo:2 * hi, :, :].rearrange("t (c i) w -> (t c) (i w)", i=CH))\
                            .then_inc(ln_ld[part], 16)

                    batch_steps(sp, step, lambda: load_lanes(0, 0, B - 2))
                    load_lanes(1, B - 2, B)
                    sp.wait_ge(s_wo, ONE + 16)
                    sp.wait_ge(inv_done, ONE + 1)
                    for q in range(4):
                        sp.dma_start(d_mt[4 * q:4 * q + 4, :, :].rearrange("t (c i) w -> (t c) (i w)", i=CH),
                                     lane_m[32 * q:32 * q + 32, :, :, :].rearrange("p i h j -> p (i h j)"))\
                            .then_inc(st_m[q], 16)
                    for u in range(2):
                        sp.wait_ge(st_kv[u], ONE + 16 * (B // 2))
                        sp.wait_ge(st_k[u], ONE + 32 * (B // 2))
                        sp.wait_ge(st_pt[u], ONE + 16 * B)
                        sp.wait_ge(st_q[u], ONE + 16 * (B // 2))

                @block.gpsimd
                def _(pool):
                    nc.gpsimd.memset(eps_c[:, 0:1], 1e-6).then_inc(s_eps, 1)
                    nc.gpsimd.memset(eps_c[:, 1:2], 1e-5).then_inc(s_eps, 1)
                    for u in range(2):
                        nc.gpsimd.memset(qn[u][:, :, :, :], 0.0).then_inc(pads, 1)
                    nc.gpsimd.memset(lane_m[:, :, :, :], 0.0).then_inc(pads, 1)
                    pool.wait_ge(pads, ONE + 3)
                    for j in range(CH):
                        nc.gpsimd.memset(lane_m[:, j, :, j], 1.0).then_inc(pads, 1)

                    def residual(b, u):
                        pool.wait_ge(t_ready, ONE + b + 1)
                        nc.gpsimd.tensor_tensor(r_sb[:, ds(2 * b, 2), :], x_sb[:, ds(2 * b, 2), :],
                                                tw[u][:, :, :], ALU.add).then_inc(t_added, 1)

                    def squares(b, u):
                        pool.wait_ge(kv_out, ONE + 2 * b + 2)
                        pool.wait_ge(qb_out, ONE + 2 * b + 2)
                        pool.wait_ge(ss_done, ONE + b)
                        nc.gpsimd.tensor_tensor(sqw[u][:, :, 0:H, :], kvw[u][:, :, :, 0:D],
                                                kvw[u][:, :, :, 0:D], ALU.mult).then_inc(sq_done, 1)
                        nc.gpsimd.tensor_tensor(sqw[u][:, :, H:2 * H, :], qw[u][:, :, :, :],
                                                qw[u][:, :, :, :], ALU.mult).then_inc(sq_done, 1)

                    def low_k(b, u):
                        pool.wait_ge(kn_done, ONE + b + 1)
                        pool.wait_ge(khi_done, ONE + b + 1)
                        nc.gpsimd.tensor_tensor(khl[u][:, :, 1, :].rearrange("p t (h d) -> p t h d", h=H),
                                                kvw[u][:, :, :, 0:D],
                                                khl[u][:, :, 0, :].rearrange("p t (h d) -> p t h d", h=H),
                                                ALU.subtract).then_inc(klo_done[u], 1)

                    def step(b, u, n, ahead):
                        if ahead == 2:
                            residual(b + 2, u)
                        if ahead:
                            squares(b + 1, 1 - u)
                            low_k(b + 1, 1 - u)

                    residual(0, 0)
                    residual(1, 1)
                    squares(0, 0)
                    low_k(0, 0)
                    batch_steps(pool, step)

                @block.scalar
                def _(act):
                    act.wait_ge(s_eps, ONE + 2)

                    def deviation(part):
                        lo, hi = PARTS[part]
                        act.wait_ge(s_mv, ONE + part + 1)
                        nc.scalar.activation(rstd[:, lo:hi], tmpa[:, lo:hi], ACT.Sqrt, bias=eps_c[:, 0:1])\
                            .then_inc(s_sq, 1)

                    nc.scalar.activation(early_s[:, 0:1], eps_c[0:1, 0:1], ACT.Sqrt)
                    act.wait_ge(s_w, ONE + 16)
                    nc.scalar.activation(wqh[:, :, :], wqkvb_sb[:, :, :], ACT.Copy, scale=WSCALE)
                    nc.scalar.activation(wqkvb_sb[:, :, :], wqkvb_sb[:, :, :], ACT.Copy, scale=WSCALE).then_inc(wq_high, 1)
                    deviation(0)
                    nc.scalar.activation(early_s[:, 1:2], eps_c[0:1, 0:1], ACT.Silu)

                    def out_tT(b, u):
                        act.wait_ge(tT_filled, ONE + b + 1)
                        if not first_use(b):
                            act.wait_ge(qb_done, ONE + 2 * b - 2)
                        nc.scalar.activation(tTh[u][:, :, :, :].rearrange("p a b n -> p (a b n)"),
                                             ps[0:HC, 0, :], ACT.Copy).then_inc(tT_high, 1)

                    def out_kvq(b, u, n):
                        for j in range(2):
                            act.wait_ge(kv_done, ONE + 2 * b + j + 1)
                            if j == 0 and b is not u:
                                act.wait_ge(st_kv[u], ONE + 16 * n)
                                act.wait_ge(klo_done[u], ONE + n)
                                act.wait_ge(kT_filled, ONE + 2 * b - 2)
                            nc.scalar.activation(kvw[u][:, j, :, :].rearrange("p h d -> p (h d)"),
                                                 ps[:, 2, 0:KVW], ACT.Silu, scale=1.0 / WSCALE).then_inc(kv_out, 1)
                            act.wait_ge(qb_done, ONE + 2 * b + j + 1)
                            if j == 0 and b is not u:
                                act.wait_ge(kn_done, ONE + b - 1)
                                act.wait_ge(st_q[u], ONE + 16 * n)
                            nc.scalar.activation(qw[u][:, j, :, :].rearrange("p h d -> p (h d)"),
                                                 ps[:, 3, 0:C], ACT.Silu, scale=1.0 / WSCALE)
                            nc.scalar.activation(beta[:, ds(2 * b + j, 1), :].rearrange("p t h -> p (t h)"),
                                                 ps[:, 3, C:QBW], ACT.Tanh, scale=0.5 / WSCALE).then_inc(qb_out, 1)

                    def lengths(b, u):
                        act.wait_ge(ss_done, ONE + b + 1)
                        if not first_use(b):
                            act.wait_ge(rn_done, ONE + b - 1)
                        nc.scalar.activation(rnw[u][:, :, :], ssw[u][:, :, :], ACT.Sqrt, bias=eps_c[:, 0:1])\
                            .then_inc(sn_done, 1)

                    def high_k(b, u, n):
                        act.wait_ge(kn_done, ONE + b + 1)
                        act.wait_ge(st_k[u], ONE + 32 * n)
                        nc.scalar.activation(khl[u][:, :, 0, :].rearrange("p t (h d) -> p t h d", h=H),
                                             kvw[u][:, :, :, 0:D], ACT.Copy).then_inc(khi_done, 1)

                    def step(b, u, n, ahead):
                        if ahead:
                            out_kvq(b + 1, 1 - u, n + u)
                        for j in range(2):
                            act.wait_ge(g_done[j], ONE + b)
                            for k, (filled, taken) in enumerate(((kT_filled, kT_out), (qT_filled, qT_out))):
                                act.wait_ge(filled, ONE + 2 * b + j + 1)
                                nc.scalar.activation(kqT[j][:, :, k, :],
                                                     ps[:, 1 - k, 0:3 * TP].rearrange("p (a n) -> p a n", a=3),
                                                     ACT.Copy).then_inc(taken, 1)
                        if ahead:
                            lengths(b + 1, 1 - u)
                        if ahead == 2:
                            out_tT(b + 2, u)
                        if ahead:
                            high_k(b + 1, 1 - u, n + u)
                            nc.scalar.activation(early_s[:, 2:3], eps_c[0:1, 0:1], ACT.Silu)

                    out_tT(0, 0)
                    out_kvq(0, 0, 0)
                    out_tT(1, 1)
                    lengths(0, 0)
                    deviation(1)
                    high_k(0, 0, 0)
                    nc.scalar.activation(early_s[:, 3:4], eps_c[0:1, 0:1], ACT.Silu)
                    batch_steps(act, step)

                @block.vector
                def _(dve):
                    count = [0]

                    def chain(ins):
                        count[0] += 1
                        ins.then_inc(s_dv, 1)
                        dve.wait_ge(s_dv, ONE + count[0])

                    def moments(part):
                        lo, hi = PARTS[part]
                        dve.wait_ge(s_x[part], ONE + 16)
                        for t in range(lo, hi):
                            last = nc.vector.bn_stats(st_sb[:, t, :], x_sb[:, t, :])
                        last.then_inc(s_bn, 1)
                        dve.wait_ge(s_bn, ONE + part + 1)
                        norm_statistics(chain, s_mv, lo, hi)

                    def inverse_deviation(part):
                        lo, hi = PARTS[part]
                        dve.wait_ge(s_sq, ONE + part + 1)
                        nc.vector.reciprocal(rstd[:, lo:hi], rstd[:, lo:hi]).then_inc(s_rs, 1)
                        dve.wait_ge(s_rs, ONE + part + 1)

                    moments(0)
                    dve.wait_ge(wq_high, ONE + 1)
                    nc.vector.tensor_tensor(wql[:, :, :], wqkvb_sb[:, :, :], wqh[:, :, :], ALU.subtract).then_inc(wq_low, 1)
                    inverse_deviation(0)
                    dve.wait_ge(s_cst, ONE + 16)

                    def tokens(b, u):
                        if not first_use(b):
                            dve.wait_ge(tT_filled, ONE + b - 1)
                            dve.wait_ge(t_added, ONE + b - 1)
                        for j in range(2):
                            last = nc.vector.tensor_scalar(tw[u][:, j, :],
                                                           x_sb[:, ds(2 * b + j, 1), :].rearrange("p t c -> p (t c)"),
                                                           mean[:, ds(2 * b + j, 1)], rstd[:, ds(2 * b + j, 1)],
                                                           ALU.subtract, ALU.mult)
                        last.then_inc(t_ready, 1)

                    def low_t(b, u):
                        dve.wait_ge(tT_high, ONE + b + 1)
                        if not first_use(b):
                            dve.wait_ge(qb_done, ONE + 2 * b - 2)
                        nc.vector.tensor_tensor(tTl[u][:, :, :, :].rearrange("p a b n -> p (a b n)"), ps[0:HC, 0, :],
                                                tTh[u][:, :, :, :].rearrange("p a b n -> p (a b n)"), ALU.subtract)\
                            .then_inc(tT_out, 1)

                    def sums(b, u):
                        dve.wait_ge(sq_done, ONE + 2 * b + 2)
                        nc.vector.tensor_reduce(ssw[u][:, :, :], sqw[u][:, :, :, :], AX.X, ALU.add).then_inc(ss_done, 1)
                        nc.vector.tensor_scalar(beta[:, ds(2 * b, 2), :], beta[:, ds(2 * b, 2), :], 0.5, 0.5,
                                                ALU.mult, ALU.add).then_inc(bt_done, 1)

                    def norm(b, u):
                        dve.wait_ge(sn_done, ONE + b + 1)
                        nc.vector.reciprocal(rnw[u][:, :, :], rnw[u][:, :, :]).then_inc(rn_done, 1)
                        dve.wait_ge(rn_done, ONE + b + 1)
                        nc.vector.tensor_tensor(kvw[u][:, :, :, 0:D], kvw[u][:, :, :, 0:D],
                                                rnw[u][:, :, 0:H].unsqueeze(3).broadcast_to([128, 2, H, D]), ALU.mult)
                        nc.vector.tensor_tensor(qw[u][:, :, :, :], qw[u][:, :, :, :],
                                                rnw[u][:, :, H:2 * H].unsqueeze(3).broadcast_to([128, 2, H, D]), ALU.mult)\
                            .then_inc(qn_in, 1)
                        dve.wait_ge(qn_in, ONE + b + 1)
                        if not first_use(b):
                            dve.wait_ge(qT_filled, ONE + 2 * b - 2)
                        nc.vector.tensor_copy(qn[u][:, :, :, 0:D], qw[u][:, :, :, :]).then_inc(kn_done, 1)

                    def scores_out(b, j):
                        scores = ps[:, 4:8, 0:3 * 64].rearrange("p r (a s i) -> p a r s i", a=3, s=2)
                        dve.wait_ge(g_done[j], ONE + b + 1)
                        dve.wait_ge(st_pt[j], ONE + 16 * b)
                        dve.wait_ge(st_n[j], ONE + 16 * b)
                        nc.vector.tensor_tensor(
                            ptw[j][:, :, :, :], scores[:, :, :, 1, :],
                            cst[:, MU0:MU0 + 32].unsqueeze(1).unsqueeze(1).broadcast_to([128, 3, 4, 32]), ALU.mult)
                        nc.vector.tensor_tensor(
                            gm[:, :, :, :], scores[:, :, :, 0, :],
                            cst[:, MS0:MS0 + 32].unsqueeze(1).unsqueeze(1).broadcast_to([128, 3, 4, 32]), ALU.mult)\
                            .then_inc(g_out, 1)
                        dve.wait_ge(g_out, ONE + 2 * b + j + 1)
                        nc.vector.tensor_tensor(nw[j][:, :, :, :], gm[:, :, :, 0:CH], gm[:, :, :, CH:2 * CH], ALU.add)\
                            .then_inc(nb_in, 1)
                        dve.wait_ge(nb_in, ONE + 2 * b + j + 1)
                        nc.vector.tensor_tensor(
                            nw[j][:, :, :, :].rearrange("p a r i -> p (a r) i"),
                            nw[j][:, :, :, :].rearrange("p a r i -> p (a r) i"),
                            beta[:, ds(2 * b + j, 1), :].rearrange("p t h -> p (t h)").unsqueeze(2)
                            .broadcast_to([128, H, CH]), ALU.mult).then_inc(n_ready[j], 1)

                    def step(b, u, n, ahead):
                        if ahead == 2:
                            tokens(b + 2, u)
                        if ahead:
                            sums(b + 1, 1 - u)
                        dve.wait_ge(bt_done, ONE + b + 1)
                        scores_out(b, 0)
                        if ahead == 2:
                            low_t(b + 2, u)
                        if ahead:
                            norm(b + 1, 1 - u)
                        scores_out(b, 1)

                    tokens(0, 0)
                    tokens(1, 1)
                    low_t(0, 0)
                    moments(1)
                    sums(0, 0)
                    dve.wait_ge(pads, ONE + 3 + CH)
                    norm(0, 0)
                    low_t(1, 1)
                    inverse_deviation(1)
                    batch_steps(dve, step)
                    for part in range(2):
                        dve.wait_ge(ln_ld[part], ONE + 16)
                    step = 0
                    for m in range(CH - 1):
                        rows, w = CH - 1 - m, m + 1
                        pr = prod[:, 0:rows * H * w].rearrange("p (i h j) -> p i h j", i=rows, h=H)
                        below = lane_m[:, 0:w, :, m + 1:CH].rearrange("p j h i -> p i h j")
                        nc.vector.tensor_tensor(
                            pr, lane_n[:, m + 1:CH, :, m].unsqueeze(3).broadcast_to([128, rows, H, w]),
                            lane_m[:, 0:w, :, m].rearrange("p j h -> p h j").unsqueeze(1).broadcast_to([128, rows, H, w]),
                            ALU.mult).then_inc(s_inv, 1)
                        step += 1
                        dve.wait_ge(s_inv, ONE + step)
                        last = nc.vector.tensor_tensor(below, below, pr, ALU.subtract)
                        if m == CH - 2:
                            last.then_inc(inv_done, 1)
                        else:
                            last.then_inc(s_inv, 1)
                            step += 1
                            dve.wait_ge(s_inv, ONE + step)

                @block.tensor
                def _(pe):
                    pe.wait_ge(s_cst, ONE + 16)

                    def token_transposes(b, u):
                        pe.wait_ge(t_ready, ONE + b + 1)
                        if not first_use(b):
                            pe.wait_ge(tT_out, ONE + b)
                            pe.wait_ge(qT_out, ONE + 2 * b - 2)
                        elif b == 1:
                            pe.wait_ge(tT_out, ONE + 1)
                        for j in range(2):
                            for hf in range(2):
                                q = 2 * j + hf
                                last = nc.tensor.transpose(ps[0:HC, 0, q * TP:(q + 1) * TP],
                                                           tw[u][:, j, hf * HC:(hf + 1) * HC], ident)
                        last.then_inc(tT_filled, 1)

                    def products(bank, j, u, first, width):
                        k = 0
                        for hf in range(2):
                            for ts, ws in ((tTh, wqh), (tTl, wqh), (tTh, wql)):
                                last = nc.tensor.matmul(ps[:, bank, 0:width], ts[u][:, j, hf, :],
                                                        ws[:, hf, first:first + width], start=(k == 0), stop=(k == 5))
                                k += 1
                        return last

                    def project(b, u):
                        pe.wait_ge(tT_out, ONE + b + 1)
                        for j in range(2):
                            pe.wait_ge(kv_out, ONE + 2 * b + j)
                            products(2, j, u, 0, KVW).then_inc(kv_done, 1)
                            pe.wait_ge(qb_out, ONE + 2 * b + j)
                            products(3, j, u, KVW, QBW).then_inc(qb_done, 1)

                    def step(b, u, n, ahead):
                        if ahead:
                            project(b + 1, 1 - u)
                        pe.wait_ge(kn_done, ONE + b + 1)
                        for j in range(2):
                            for k, (src, filled, taken) in enumerate(((kvw[u], kT_filled, kT_out),
                                                                      (qn[u], qT_filled, qT_out))):
                                pe.wait_ge(taken, ONE + 2 * b + j)
                                if j == 0 and k == 1:
                                    pe.wait_ge(tT_out, ONE + b + 1 + (ahead > 0))
                                for a in range(3):
                                    last = nc.tensor.transpose(
                                        ps[:, 1 - k, a * TP:(a + 1) * TP],
                                        src[:, j, 4 * a:4 * a + 4, :].rearrange("p h d -> p (h d)"), ident)
                                last.then_inc(filled, 1)
                        for j in range(2):
                            by_constant(pe, 2 * b + j + 1, 2 * b + j)
                            pe.wait_ge(kT_out, ONE + 2 * b + j + 1)
                            pe.wait_ge(qT_out, ONE + 2 * b + j + 1)
                            pe.wait_ge(g_out, ONE + 2 * b + j)
                            for a in range(3):
                                for g in range(4):
                                    for q in range(4):
                                        rows, cols = slice(32 * q, 32 * q + D), slice(32 * g, 32 * g + 32)
                                        last = nc.tensor.matmul(ps[cols, 4 + q, 64 * a:64 * a + 64],
                                                                kqT[j][rows, a, 0, cols], kqT[j][rows, a, :, cols],
                                                                start=True, stop=True)
                            last.then_inc(g_done[j], 1)
                            if j == 0 and ahead == 2:
                                token_transposes(b + 2, u)

                    token_transposes(0, 0)
                    pe.wait_ge(wq_low, ONE + 1)
                    project(0, 0)
                    token_transposes(1, 1)
                    batch_steps(pe, step)

        over_scan = ctx.enter_context(ExitStack())
        ub = over_scan.enter_context(nc.sbuf_tensor("ub", [128, NC, 2, C], f32))

        with ExitStack() as wy:
            def sbw(name, shape, dt=f32):
                return wy.enter_context(nc.sbuf_tensor(name, shape, dt))

            mtc = [sbw(f"mtc{u}", [128, H, CH]) for u in range(2)]
            mb = [sbw(f"mb{u}", [128, H, 2, CH]) for u in range(2)]
            kvt = [sbw(f"kvt{u}", [128, H, 2 * D]) for u in range(2)]
            ww = [sbw(f"ww{u}", [128, H, D]) for u in range(2)]
            ubw = [sbw(f"ubw{u}", [128, H, D]) for u in range(2)]
            qt = [sbw(f"qt{u}", [128, C]) for u in range(2)]
            wT = [sbw(f"wT{u}", [HC, 8, 4, CH]) for u in range(2)]
            ld_q, ub0, ub_early, wo_high = sem2("ld_q"), sem("ub0"), sem("ub_early"), sem("wo_high")
            ld_m, ld_kv, mb_done, x_done, x_out = (sem2("ld_m"), sem2("ld_kv"), sem2("mb_done"), sem2("x_done"),
                                                   sem2("x_out"))
            w_t, w_out, st_ub, st_w, m_beta = sem2("w_t"), sem2("w_out"), sem2("st_ub"), sem2("st_w"), sem2("m_beta")

            with nc.Block() as block:

                @block.sync
                def _(sp):
                    start_at_one(sp)
                    for q in range(4):
                        sp.wait_ge(st_m[q], ONE + 16)
                        with sp.Fori(2 * q, 2 * q + 2) as r:
                            for u in range(2):
                                sp.wait_ge(mb_done[u], ONE + r)
                                sp.dma_start(mtc[u][:, :, :].rearrange("p h i -> p (h i)"),
                                             d_mt[ds(2 * r + u, 1), :, :].rearrange("t p c -> (t p) c")).then_inc(ld_m[u], 16)
                                sp.wait_ge(x_done[u], ONE + r)
                                sp.dma_start(kvt[u][:, :, :].rearrange("p h d -> p (h d)"),
                                             d_kv[ds(2 * r + u, 1), :, :].rearrange("t p c -> (t p) c")).then_inc(ld_kv[u], 16)
                            for u in range(2):
                                sp.wait_ge(w_t[u], ONE + r)
                                sp.dma_start(qt[u][:, :], d_q[ds(2 * r + u, 1), :, :].rearrange("t p c -> (t p) c"))\
                                    .then_inc(ld_q[u], 16)
                    sp.wait_ge(ub0, ONE + 1)
                    for u in range(2):
                        sp.wait_ge(st_ub[u], ONE + 16 * (B - 2))
                    for b in range(B - 2):
                        rows = slice(32 * (b // 2), 32 * (b // 2) + CH)
                        sp.dma_start(ub[rows, :, b % 2, :], d_ub[b, :, :, :].rearrange("c i w -> i c w"))\
                            .then_inc(ub_early, 16)
                    sp.wait_ge(ub_early, ONE + 16 * (B - 2))

                @block.vector
                def _(dve):
                    with dve.Fori(0, B) as r:
                        for u in range(2):
                            dve.wait_ge(ld_m[u], ONE + 16 * r + 16)
                            nc.vector.tensor_tensor(
                                mtc[u][:, :, :], mtc[u][:, :, :],
                                beta[:, ds(2 * r + u, 1), :].rearrange("p t h -> p (t h)").unsqueeze(2)
                                .broadcast_to([128, H, CH]), ALU.mult).then_inc(m_beta[u], 1)
                            dve.wait_ge(m_beta[u], ONE + r + 1)
                            dve.wait_ge(x_done[u], ONE + r)
                            nc.vector.tensor_tensor(
                                mb[u][:, :, :, :], mtc[u][:, :, :].unsqueeze(2).broadcast_to([128, H, 2, CH]),
                                cst[:, MP0:MP0 + 2].unsqueeze(1).unsqueeze(3).broadcast_to([128, H, 2, CH]), ALU.mult)\
                                .then_inc(mb_done[u], 1)

                @block.gpsimd
                def _(pool):
                    nc.gpsimd.memset(ub[:, :, :, :], 0.0).then_inc(ub0, 1)
                    pool.wait_ge(wo_high, ONE + 1)
                    nc.gpsimd.tensor_tensor(wol[:, :, :], wo_sb[:, :, :], woh[:, :, :], ALU.subtract).then_inc(ub0, 1)
                    pool.wait_ge(ub0, ONE + 2)

                @block.scalar
                def _(act):
                    nc.scalar.activation(woh[:, :, :], wo_sb[:, :, :], ACT.Copy, scale=WSCALE)
                    nc.scalar.activation(wo_sb[:, :, :], wo_sb[:, :, :], ACT.Copy, scale=WSCALE).then_inc(wo_high, 1)
                    with act.Fori(0, B) as r:
                        for u in range(2):
                            both = ps[:, u, 0:KVW].rearrange("p (h s d) -> p s h d", h=H, s=2)
                            act.wait_ge(x_done[u], ONE + r + 1)
                            act.wait_ge(w_t[u], ONE + r)
                            nc.scalar.activation(ww[u][:, :, :], both[:, 0, :, :], ACT.Copy)
                            act.wait_ge(st_ub[u], ONE + 16 * r)
                            nc.scalar.activation(ubw[u][:, :, :], both[:, 1, :, :], ACT.Copy).then_inc(x_out[u], 1)
                            act.wait_ge(x_out[u], ONE + r + 1)
                            act.dma_start(d_ub[ds(r, 1), 8 * u:8 * u + 8, :, :].rearrange("b c i w -> (b c i) w"),
                                          ubw[u][:, :, :].rearrange("p h d -> p (h d)")).then_inc(st_ub[u], 16)
                        for u in range(2):
                            act.wait_ge(w_t[u], ONE + r + 1)
                            act.wait_ge(st_w[u], ONE + 16 * r)
                            nc.scalar.activation(
                                wT[u][:, :, :, :],
                                ps[0:HC, 2 + u, :].rearrange("p (q c i) -> p c q i", q=4, i=CH), ACT.Copy)\
                                .then_inc(w_out[u], 1)
                            act.wait_ge(w_out[u], ONE + r + 1)
                            act.dma_start(d_w[8 * u:8 * u + 8, :, ds(r, 1), :].rearrange("c p b w -> p c (b w)"),
                                          wT[u][:, :, :, :].rearrange("p c q i -> p c (q i)")).then_inc(st_w[u], 16)
                    for u in range(2):
                        act.wait_ge(st_ub[u], ONE + 16 * B)
                        act.wait_ge(st_w[u], ONE + 16 * B)

                @block.tensor
                def _(pe):
                    with pe.Fori(0, B) as r:
                        for u in range(2):
                            by_constant(pe, r + 1, 16 * r + 16, r)
                            pe.wait_ge(mb_done[u], ONE + r + 1)
                            pe.wait_ge(ld_kv[u], ONE + 16 * r + 16)
                            pe.wait_ge(x_out[u], ONE + r)
                            for h in range(H):
                                for g in range(4):
                                    rows = slice(32 * g, 32 * g + 32)
                                    last = nc.tensor.matmul(ps[rows, u, 32 * h:32 * h + 32],
                                                            mb[u][rows, h, :, :].rearrange("p c i -> p (c i)"),
                                                            kvt[u][rows, h, :], start=True, stop=True)
                            last.then_inc(x_done[u], 1)
                        for u in range(2):
                            pe.wait_ge(x_out[u], ONE + r + 1)
                            pe.wait_ge(ld_q[u], ONE + 16 * r + 16)
                            pe.wait_ge(w_out[u], ONE + r)
                            for hf in range(2):
                                for s, src in enumerate((ww[u][:, :, :].rearrange("p h d -> p (h d)"), qt[u])):
                                    q = 2 * hf + s
                                    last = nc.tensor.transpose(ps[0:HC, 2 + u, q * TP:(q + 1) * TP],
                                                               src[:, hf * HC:(hf + 1) * HC], ident)
                            last.then_inc(w_t[u], 1)

        with nc.Block() as block:

            @block.sync
            def _(sp):
                numbers = sorted(s.num for s in semaphores[1:])
                assert numbers == list(range(numbers[0], numbers[-1] + 1))
                sp.sem_clear(range(numbers[0], numbers[-1] + 1))

        early.close()
        held_by[0] = ctx

        with ExitStack() as scan:
            def sbs(name, shape, dt=f32):
                return scan.enter_context(nc.sbuf_tensor(name, shape, dt))

            wqs = [sbs(f"wqs{p}", [HC, B * 4 * CH]) for p in range(2)]
            ks = [sbs(f"ks{p}", [128, 2, 2, C], f16) for p in range(2)]
            uo = [sbs(f"uo{p}", [128, 2, C]) for p in range(2)]
            uh = [sbs(f"uh{p}", [128, 2, C], f16) for p in range(2)]
            ul = [sbs(f"ul{p}", [128, 2, C], f16) for p in range(2)]
            s_sb = sbs("s_sb", [HC, 4, 4, HC])
            zero = sbs("zero", [HC, 2 * C], f16)
            zu = sem("zu")
            sc_ld, ws_done, uo_done, uh_done, ul_done, up_done, s_ready = (
                sem2("sc_ld"), sem2("ws_done"), sem2("uo_done"), sem2("uh_done"), sem2("ul_done"), sem2("up_done"),
                sem2("s_ready"))
            st_u = sem2("st_u")
            ub_ld = sem("ub_ld")
            fs_ld, fs_sc, fs_hi, fs_lo = sem("fs_ld"), sem("fs_sc"), sem("fs_hi"), sem("fs_lo")

            of_scan = len(semaphores)
            st_x = [sem(f"st_x{u}") for u in range(4)]
            s_g, g_split, s_rt, ex_in, ex_done, s_bp = (
                sem("s_g"), sem("g_split"), sem("s_rt"), sem("ex_in"), sem("ex_done"), sem("s_bp"))
            tk_done, rk_done, hot, met_part = sem("tk_done"), sem("rk_done"), sem("hot"), sem("met_part")
            xw_done, x_t, xh_done, xl_done, sc_done, sc_out = (
                [sem(f"{name}{u}") for u in range(4)]
                for name in ("xw_done", "x_t", "xh_done", "xl_done", "sc_done", "sc_out"))
            ld_o = [sem(f"ld_o{k}") for k in range(4)]
            o_done = [sem(f"o_done{k}") for k in range(4)]
            o_high = sem2("o_high")
            pu_done, o_t, o_out, y_done, y_out = (
                sem2("pu_done"), sem2("o_t"), sem2("o_out"), sem2("y_done"), sem2("y_out"))
            bn2, mv2, sq2, s_dv2 = sem("bn2"), sem("mv2"), sem("sq2"), sem("s_dv2")
            src_in, xs_t, xsh, xsl, fc_done, hw_done, hh_done, hl_done, dn_done, ye_done, y_free = (
                sem2("src_in"), sem2("xs_t"), sem2("xsh"), sem2("xsl"), sem2("fc_done"), sem2("hw_done"),
                sem2("hh_done"), sem2("hl_done"), sem2("dn_done"), sem2("ye_done"), sem2("ye_free"))
            ya_ld = [sem(f"ya_ld{i}") for i in range(NT // PT)]
            s_add, s_out = sem("s_add"), sem("s_out")

            with nc.Block() as block:

                @block.sync
                def _(sp):
                    start_at_one(sp, of_scan)
                    with sp.Fori(0, NC // 2) as r:
                        for p in range(2):
                            c = 2 * r + p
                            for q in range(2):
                                sp.wait_ge(s_ready[q], ONE + c)
                            sp.dma_start(wqs[p][:, :], d_w[ds(c, 1), :, :, :].rearrange("c p b w -> (c p) (b w)"))\
                                .then_inc(sc_ld[p], 16)
                            for bb in range(4):
                                rows = slice(32 * bb, 32 * bb + CH)
                                sp.dma_start(ks[p][rows, :, :, :].rearrange("i g s w -> i g (s w)"),
                                             d_khl[2 * bb:2 * bb + 2, ds(c, 1), :, :].rearrange("g c i w -> i (g c) w"))\
                                    .then_inc(sc_ld[p], 16)
                        sp.wait_ge(fs_lo, ONE + 2 * r)
                        sp.dma_start(fcs[:, :, :], wfc[ds(r, 1), :, :, :].rearrange("e p a n -> (e p) a n"))\
                            .then_inc(fs_ld, 16)
                        sp.dma_start(pjs[:, :], wproj[ds(r, 1), :, :].rearrange("e p n -> (e p) n")).then_inc(fs_ld, 16)
                    start_at_one(sp)

                @block.gpsimd
                def _(pool):
                    nc.gpsimd.memset(zero[:, :], 0.0).then_inc(zu, 1)
                    with pool.Fori(0, NC // 2) as r:
                        by_constant(pool, 32 * r + 32)
                        pool.wait_ge(fs_ld, ONE + 32 * r + 32)
                        nc.gpsimd.tensor_scalar(fcs[:, :, :], fcs[:, :, :], WSCALE / 8, 8.0, ALU.mult, ALU.mult)\
                            .then_inc(fs_sc, 1)
                        nc.gpsimd.tensor_scalar(pjs[:, :], pjs[:, :], WSCALE / 8, 8.0, ALU.mult, ALU.mult)\
                            .then_inc(fs_sc, 1)
                        pool.wait_ge(fs_hi, ONE + 2 * r + 1)
                        nc.gpsimd.tensor_tensor(fcl[:, :, ds(r, 1), :].rearrange("p a e n -> p (a e) n"), fcs[:, :, :],
                                                fch[:, :, ds(r, 1), :].rearrange("p a e n -> p (a e) n"),
                                                ALU.subtract).then_inc(fs_lo, 1)

                @block.vector
                def _(dve):
                    nc.vector.memset(s_sb[:, 0:2, :, :], 0.0).then_inc(s_ready[0], 1)
                    nc.vector.memset(s_sb[:, 2:4, :, :], 0.0).then_inc(s_ready[1], 1)
                    dve.wait_ge(ub_ld, ONE + 32)
                    with dve.Fori(0, NC // 2) as r:
                        for p in range(2):
                            c = 2 * r + p
                            dve.wait_ge(st_u[p], ONE + 16 * r)
                            for q in range(2):
                                rows = slice(64 * q, 64 * q + 64)
                                dve.wait_ge(ws_done[q], ONE + c + 1)
                                nc.vector.tensor_tensor(uo[p][rows, :, :], ub[rows, ds(c, 1), :, :].rearrange("p c g w -> p (c g) w"),
                                                        ps[rows, 0, 0:2 * C].rearrange("p (g w) -> p g w", g=2),
                                                        ALU.subtract).then_inc(uo_done[q], 1)
                            for q in range(2):
                                rows = slice(64 * q, 64 * q + 64)
                                dve.wait_ge(uh_done[q], ONE + c + 1)
                                nc.vector.tensor_tensor(ul[p][rows, :, :], uo[p][rows, :, :], uh[p][rows, :, :],
                                                        ALU.subtract).then_inc(ul_done[q], 1)
                            for q in range(2):
                                dve.wait_ge(up_done[q], ONE + c + 1)
                                nc.vector.tensor_tensor(
                                    s_sb[:, 2 * q:2 * q + 2, :, :],
                                    ps[0:HC, 4 + 2 * q:6 + 2 * q, 0:4 * HC].rearrange("p a (g w) -> p a g w", w=HC),
                                    cst[0:HC, BM0:BM0 + HC].unsqueeze(1).unsqueeze(1).broadcast_to([HC, 2, 4, HC]),
                                    ALU.mult).then_inc(s_ready[q], 1)
                        dve.wait_ge(fs_hi, ONE + 2 * r + 2)
                        nc.vector.tensor_tensor(pjl[:, ds(r, 1), :].rearrange("p e n -> p (e n)"), pjs[:, :],
                                                pjh[:, ds(r, 1), :].rearrange("p e n -> p (e n)"),
                                                ALU.subtract).then_inc(fs_lo, 1)

                @block.scalar
                def _(act):
                    act.wait_ge(ub_ld, ONE)
                    for b in range(B - 2, B):
                        rows = slice(32 * (b // 2), 32 * (b // 2) + CH)
                        act.dma_start(ub[rows, :, b % 2, :], d_ub[b, :, :, :].rearrange("c i w -> i c w"))\
                            .then_inc(ub_ld, 16)
                    with act.Fori(0, NC // 2) as r:
                        for p in range(2):
                            for q in range(2):
                                rows = slice(64 * q, 64 * q + 64)
                                act.wait_ge(uo_done[q], ONE + 2 * r + p + 1)
                                nc.scalar.activation(uh[p][rows, :, :], uo[p][rows, :, :], ACT.Copy)\
                                    .then_inc(uh_done[q], 1)
                            act.dma_start(d_u[ds(2 * r + p, 1), :, :, :, :, :].rearrange("c a s i g w -> (c a s i) g w"),
                                          uo[p][:, :, :]).then_inc(st_u[p], 16)
                        act.wait_ge(fs_sc, ONE + 2 * r + 2)
                        nc.scalar.activation(fch[:, :, ds(r, 1), :].rearrange("p a e n -> p (a e) n"), fcs[:, :, :],
                                             ACT.Copy).then_inc(fs_hi, 1)
                        nc.scalar.activation(pjh[:, ds(r, 1), :].rearrange("p e n -> p (e n)"), pjs[:, :],
                                             ACT.Copy).then_inc(fs_hi, 1)
                    for p in range(2):
                        act.wait_ge(st_u[p], ONE + 16 * NC // 2)

                @block.tensor
                def _(pe):
                    pe.wait_ge(zu, ONE + 1)
                    for bb in range(4):
                        nc.tensor.matmul(ps[0:HC, 4 + bb, 0:4 * HC], zero[0:32, 0:HC], zero[0:32, 0:4 * HC],
                                         start=True, stop=False, skip_group_check=True)
                    with pe.Fori(0, NC // 2) as r:
                        for p in range(2):
                            c = 2 * r + p
                            pe.wait_ge(sc_ld[p], ONE + 16 * 5 * (r + 1))
                            for q in range(2):
                                pe.wait_ge(s_ready[q], ONE + c + 1)
                                pe.wait_ge(uo_done[q], ONE + c)
                                for bb in (2 * q, 2 * q + 1):
                                    for g in range(4):
                                        bg, hf = g // 2, g % 2
                                        o = ((2 * bb + bg) * 2 + hf) * 2 * CH
                                        last = nc.tensor.matmul(ps[32 * bb:32 * bb + 32, 0, g * HC:(g + 1) * HC],
                                                                wqs[p][:, o:o + 2 * CH], s_sb[:, bb, g, :],
                                                                start=True, stop=True)
                                last.then_inc(ws_done[q], 1)
                            for q in range(2):
                                pe.wait_ge(ul_done[q], ONE + c + 1)
                                for part in range(3):
                                    for g in range(4):
                                        for bb in (2 * q, 2 * q + 1):
                                            bg, hf = g // 2, g % 2
                                            rows, w = slice(32 * bb, 32 * bb + CH), slice(hf * HC, (hf + 1) * HC)
                                            last = nc.tensor.matmul(ps[0:HC, 4 + bb, g * HC:(g + 1) * HC],
                                                                    ks[p][rows, bg, part // 2, w],
                                                                    (uh, ul, uh)[part][p][rows, bg, w],
                                                                    start=False, stop=False, skip_group_check=True)
                                last.then_inc(up_done[q], 1)

        over_scan.close()

        xh = [sb(f"xh{u}", [HC + 1, 2, TP], f16) for u in range(4)]
        xl = [sb(f"xl{u}", [HC + 1, 2, TP], f16) for u in range(4)]
        u32 = mybir.dt.uint32
        CK, CT, CP = 0, 1, 2
        in_tile = [sb(f"in_tile{k}", [128, NT, TP], f16) for k in range(2)]
        of_tile = [sb(f"of_tile{k}", [128, NT, 3, ST], f16) for k in range(2)]
        low = sb("low", [128, NT], f16)
        high = sb("high", [128, NT], f16)
        count16 = sb("count16", [128, TP], f16)
        tile16 = sb("tile16", [128, 2 * NT], f16)
        part_u = sb("part_u", [128, NT], u32)
        met = sb("met", [128, 3, ST])
        ans = sb("ans", [128, ST])
        over = sb("over", [128, ST])
        free = sb("free", [128, ST])
        take = sb("take", [128, ST + 2], u32)
        give = sb("give", [128, ST], u32)
        gth = sb("gth", [HC + 1, 2, E], f16)
        gtl = sb("gtl", [HC + 1, 2, E], f16)
        gts = sb("gts", [HC + 1, 2, E])
        bps = sb("bps", [1, E, C])
        bph = sb("bph", [1, E, C], f16)
        bpl = sb("bpl", [1, E, C], f16)
        bpw = sb("bpw", [2, E, C], f16)
        ones = sb("ones", [128, TP], f16)
        tri = sb("tri", [128, TP], f16)
        xw = [sb(f"xw{u}", [128, C]) for u in range(4)]
        sc = sb("sc", [128, NT, E])
        sel = [sb(f"sel{k}", [128, NT, E]) for k in range(2)]
        taken = sb("taken", [128, NT, E], f16)
        key = sb("key", [128, NT, E])
        pos = sb("pos", [128, NT, E])
        top = [sb(f"top{k}", [128, NT]) for k in range(2)]
        kmax = sb("kmax", [128, NT])
        g1 = sb("g1", [128, NT])
        g2 = sb("g2", [128, NT])
        load = sb("load", [128, E])
        more = sb("more", [128, E, NT])
        tiles = sb("tiles", [128, E])
        before = sb("before", [128, E, E])
        base = sb("base", [128, E])
        ends = sb("ends", [128, E])
        past = sb("past", [1, ST, E - 1])
        owner_f = sb("owner_f", [1, ST])
        owner = sb("owner", [1, ST], mybir.dt.int32)
        slot_f = sb("slot_f", [128, NT])
        slot = [sb(f"slot{k}", [128, NT], u32) for k in range(2)]

        with ExitStack() as outp:
            def sbo(name, shape, dt=f32):
                return outp.enter_context(nc.sbuf_tensor(name, shape, dt))

            ut = [sbo(f"ut{k}", [128, C]) for k in range(4)]
            qs = [sbo(f"qs{k}", [128, C]) for k in range(4)]
            pt = [sbo(f"pt{k}", [128, H, 2 * CH]) for k in range(4)]
            ow = [sbo(f"ow{u}", [128, C]) for u in range(2)]
            oTh = [sbo(f"oTh{u}", [HC, 2, TP], f16) for u in range(2)]
            oTl = [sbo(f"oTl{u}", [HC, 2, TP], f16) for u in range(2)]

            with nc.Block() as block:

                @block.sync
                def _(sp):
                    with sp.Fori(0, B // 2) as a:
                        for k in range(4):
                            g, u = k // 2, k % 2
                            sp.wait_ge(o_done[k], ONE + a)
                            for s, dst in enumerate((ut[k], qs[k])):
                                sp.dma_start(dst[:, :], d_u[8 * u:8 * u + 8, ds(a, 1), s, :, g, :]
                                             .rearrange("c a i w -> c (a i) w")).then_inc(ld_o[k], 16)
                            sp.dma_start(pt[k][:, :, :].rearrange("p h i -> p (h i)"),
                                         d_pt[ds(4 * a + k, 1), :, :].rearrange("t p c -> (t p) c")).then_inc(ld_o[k], 16)
                    sp.dma_start(gts[:, :, :], gate.rearrange("p (a n) -> p a n", a=2)).then_inc(s_g, 16)
                    sp.dma_start(bps[:, :, :], bproj.rearrange("(a e) n -> a e n", a=1)).then_inc(s_g, 16)

                @block.gpsimd
                def _(pool):
                    done = [0]

                    def chain(ins):
                        done[0] += 1
                        ins.then_inc(g_split, 1)
                        pool.wait_ge(g_split, ONE + done[0])

                    pool.wait_ge(s_g, ONE + 32)
                    chain(nc.gpsimd.tensor_copy(gth[:, :, :], gts[:, :, :]))
                    chain(nc.gpsimd.tensor_tensor(gtl[:, :, :], gts[:, :, :], gth[:, :, :], ALU.subtract))
                    for u in range(4):
                        chain(nc.gpsimd.memset(xh[u][HC:HC + 1, :, :], 1.0))
                        chain(nc.gpsimd.memset(xl[u][HC:HC + 1, :, :], 0.0))
                    chain(nc.gpsimd.memset(ones[:, :], 1.0))
                    chain(nc.gpsimd.tensor_copy(tri[:, :], cst[:, TR0:TR0 + TP]))
                    chain(nc.gpsimd.tensor_copy(count16[:, :], cst[:, IO0:IO0 + TP]))
                    chain(nc.gpsimd.tensor_copy(tile16[:, :], cst[:, DI0:DI0 + 2 * NT]))
                    chain(nc.gpsimd.tensor_scalar(bps[:, :, :], bps[:, :, :], WSCALE / 8, 8.0, ALU.mult, ALU.mult))
                    chain(nc.gpsimd.tensor_copy(bph[:, :, :], bps[:, :, :]))
                    chain(nc.gpsimd.tensor_tensor(bpl[:, :, :], bps[:, :, :], bph[:, :, :], ALU.subtract))

                @block.vector
                def _(dve):
                    with dve.Fori(0, B // 2) as a:
                        for g in range(2):
                            r = 2 * a + g
                            for u in range(2):
                                dve.wait_ge(pu_done[u], ONE + r + 1)
                                dve.wait_ge(o_t[u], ONE + r)
                                nc.vector.tensor_tensor(ow[u][:, :], ps[:, u, 0:C], qs[2 * g + u][:, :], ALU.subtract)\
                                    .then_inc(o_done[2 * g + u], 1)
                            for u in range(2):
                                dve.wait_ge(o_high[u], ONE + r + 1)
                                nc.vector.tensor_tensor(oTl[u][:, :, :].rearrange("p a n -> p (a n)"),
                                                        ps[0:HC, 2 + u, 0:2 * TP],
                                                        oTh[u][:, :, :].rearrange("p a n -> p (a n)"), ALU.subtract)\
                                    .then_inc(o_out[u], 1)
                            for u in range(2):
                                xt = r_sb[:, ds(2 * r + u, 1), :].rearrange("p t c -> p (t c)")
                                dve.wait_ge(y_done[u], ONE + r + 1)
                                nc.vector.scalar_tensor_tensor(xt, ps[:, 4 + u, 0:C], 1.0 / WSCALE, xt, ALU.mult, ALU.add)\
                                    .then_inc(y_out[u], 1)
                            for u in range(2):
                                dve.wait_ge(y_out[u], ONE + r + 1)
                                nc.vector.bn_stats(st_sb[:, ds(2 * r + u, 1), :].rearrange("p t c -> p (t c)"),
                                                   r_sb[:, ds(2 * r + u, 1), :].rearrange("p t c -> p (t c)"))\
                                    .then_inc(bn2, 1)
                    dve.wait_ge(bn2, ONE + NT)
                    count = [0]

                    def chain(ins):
                        count[0] += 1
                        ins.then_inc(s_dv2, 1)
                        dve.wait_ge(s_dv2, ONE + count[0])

                    norm_statistics(chain, mv2, 0, NT)
                    dve.wait_ge(sq2, ONE + 1)
                    chain(nc.vector.reciprocal(rstd[:, :], rstd[:, :]))

                @block.scalar
                def _(act):
                    with act.Fori(0, B // 2) as a:
                        for g in range(2):
                            r = 2 * a + g
                            for u in range(2):
                                act.wait_ge(o_t[u], ONE + r + 1)
                                act.wait_ge(y_done[u], ONE + r)
                                nc.scalar.activation(oTh[u][:, :, :].rearrange("p a n -> p (a n)"), ps[0:HC, 2 + u, 0:2 * TP],
                                                     ACT.Copy).then_inc(o_high[u], 1)
                    act.wait_ge(mv2, ONE + 1)
                    nc.scalar.activation(rstd[:, :], tmpa[:, :], ACT.Sqrt, bias=eps_c[:, 1:2]).then_inc(sq2, 1)

                @block.tensor
                def _(pe):
                    with pe.Fori(0, B // 2) as a:
                        for g in range(2):
                            r = 2 * a + g
                            for u in range(2):
                                by_constant(pe, 48 * (a + 1), a + g)
                                pe.wait_ge(ld_o[2 * g + u], ONE + 48 * (a + 1))
                                pe.wait_ge(o_done[2 * (1 - g) + u], ONE + a + g)
                                for h in range(H):
                                    for w in range(4):
                                        rows = slice(32 * w, 32 * w + 32)
                                        last = nc.tensor.matmul(ps[rows, u, D * h:D * h + D], pt[2 * g + u][rows, h, :],
                                                                ut[2 * g + u][rows, D * h:D * h + D], start=True, stop=True)
                                last.then_inc(pu_done[u], 1)
                            for u in range(2):
                                pe.wait_ge(o_done[2 * g + u], ONE + a + 1)
                                pe.wait_ge(o_out[u], ONE + r)
                                for hf in range(2):
                                    last = nc.tensor.transpose(ps[0:HC, 2 + u, hf * TP:(hf + 1) * TP],
                                                               ow[u][:, hf * HC:(hf + 1) * HC], ident)
                                last.then_inc(o_t[u], 1)
                            for u in range(2):
                                pe.wait_ge(o_out[u], ONE + r + 1)
                                pe.wait_ge(y_out[u], ONE + r)
                                k = 0
                                for hf in range(2):
                                    for os, ws in ((oTh, woh), (oTl, woh), (oTh, wol)):
                                        last = nc.tensor.matmul(ps[:, 4 + u, 0:C], os[u][:, hf, :], ws[:, hf, :],
                                                                start=(k == 0), stop=(k == 5))
                                        k += 1
                                last.then_inc(y_done[u], 1)


        with nc.Block() as block:

            @block.sync
            def _(sp):
                with sp.Fori(0, B // 2) as r:
                    for u in range(4):
                        by_constant(sp, r + 1)
                        sp.wait_ge(xw_done[u], ONE + r + 1)
                        sp.dma_start(d_x[ds(4 * r + u, 1), :, :].rearrange("t p c -> (t p) c"), xw[u][:, :])\
                            .then_inc(st_x[u], 16)
                sp.dma_start(bpw[0:1, :, :], bph[:, :, :]).then_inc(s_bp, 16)
                sp.dma_start(bpw[1:2, :, :], bpl[:, :, :]).then_inc(s_bp, 16)
                sp.wait_ge(s_bp, ONE + 32)
                for u in range(4):
                    sp.wait_ge(st_x[u], ONE + 16 * (B // 2))

            @block.vector
            def _(dve):
                with dve.Fori(0, B // 2) as r:
                    for u in range(4):
                        t = 4 * r + u
                        dve.wait_ge(x_t[u], ONE + r)
                        dve.wait_ge(st_x[u], ONE + 16 * r)
                        nc.vector.tensor_scalar(xw[u][:, :],
                                                r_sb[:, ds(t, 1), :].rearrange("p t c -> p (t c)"),
                                                mean[:, ds(t, 1)], rstd[:, ds(t, 1)], ALU.subtract, ALU.mult)\
                            .then_inc(xw_done[u], 1)
                    for u in range(4):
                        dve.wait_ge(xh_done[u], ONE + r + 1)
                        nc.vector.tensor_tensor(xl[u][0:HC, :, :],
                                                ps[0:HC, u, 0:2 * TP].rearrange("p (h n) -> p h n", h=2),
                                                xh[u][0:HC, :, :], ALU.subtract).then_inc(xl_done[u], 1)
                    for u in range(4):
                        dve.wait_ge(sc_done[u], ONE + r + 1)
                        nc.vector.tensor_copy(sc[:, ds(4 * r + u, 1), :].rearrange("p t e -> p (t e)"),
                                              ps[:, 4 + u, 0:E]).then_inc(sc_out[u], 1)
                for u in range(4):
                    dve.wait_ge(sc_out[u], ONE + B // 2)
                count = [0]

                def chain(ins):
                    count[0] += 1
                    ins.then_inc(s_rt, 1)
                    dve.wait_ge(s_rt, ONE + count[0])

                def wide(ap):
                    return ap.unsqueeze(2).broadcast_to([128, NT, E])

                first = cst[:, TB0:TB0 + E].unsqueeze(1).broadcast_to([128, NT, E])
                for k in range(2):
                    chain(nc.vector.tensor_reduce(top[k][:, :], sc[:, :, :], AX.X, ALU.max))
                    chain(nc.vector.tensor_tensor(key[:, :, :], sc[:, :, :], wide(top[k][:, :]), ALU.is_equal))
                    chain(nc.vector.tensor_tensor(key[:, :, :], key[:, :, :], first, ALU.mult))
                    chain(nc.vector.tensor_reduce(kmax[:, :], key[:, :, :], AX.X, ALU.max))
                    chain(nc.vector.tensor_tensor(sel[k][:, :, :], key[:, :, :], wide(kmax[:, :]), ALU.is_equal))
                    if k == 0:
                        chain(nc.vector.scalar_tensor_tensor(sc[:, :, :], sel[0][:, :, :], -1e30, sc[:, :, :],
                                                             ALU.mult, ALU.add))
                nc.vector.tensor_tensor(taken[:, :, :], sel[0][:, :, :], sel[1][:, :, :], ALU.add).then_inc(tk_done, 1)
                nc.vector.tensor_tensor(g2[:, :], top[1][:, :], top[0][:, :], ALU.subtract).then_inc(ex_in, 1)
                dve.wait_ge(rk_done, ONE + 1)
                chain(nc.vector.tensor_copy(load[:, :], ps[:, 5, 0:E]))
                chain(nc.vector.tensor_tensor(more[:, :, :], load[:, :].unsqueeze(2).broadcast_to([128, E, NT]),
                                              cst[:, TS0:TS0 + NT].unsqueeze(1).broadcast_to([128, E, NT]), ALU.is_gt))
                chain(nc.vector.tensor_reduce(tiles[:, :], more[:, :, :], AX.X, ALU.add))
                chain(nc.vector.tensor_tensor(before[:, :, :], tiles[:, :].unsqueeze(1).broadcast_to([128, E, E]),
                                              cst[:, EB0:EB0 + E * E].rearrange("p (a b) -> p a b", a=E), ALU.mult))
                chain(nc.vector.tensor_reduce(base[:, :], before[:, :, :], AX.X, ALU.add))
                chain(nc.vector.tensor_tensor(ends[:, :], base[:, :], tiles[:, :], ALU.add))
                chain(nc.vector.tensor_tensor(past[:, :, :], cst[0:1, IO0:IO0 + ST].unsqueeze(2).broadcast_to([1, ST, E - 1]),
                                              ends[0:1, 0:E - 1].unsqueeze(1).broadcast_to([1, ST, E - 1]), ALU.is_ge))
                chain(nc.vector.tensor_reduce(owner_f[:, :], past[:, :, :], AX.X, ALU.add))
                chain(nc.vector.tensor_copy(owner[:, :], owner_f[:, :]))
                chain(nc.vector.tensor_scalar(base[:, :], base[:, :], float(TP), None, ALU.mult))
                chain(nc.vector.tensor_tensor(pos[:, :, :], ps[:, 4, 0:NT * E].rearrange("p (t e) -> p t e", e=E),
                                              base[:, :].unsqueeze(1).broadcast_to([128, NT, E]), ALU.add))
                for k in range(2):
                    chain(nc.vector.tensor_tensor(key[:, :, :], sel[k][:, :, :], pos[:, :, :], ALU.mult))
                    chain(nc.vector.tensor_reduce(slot_f[:, :], key[:, :, :], AX.X, ALU.add))
                    chain(nc.vector.tensor_copy(slot[k][:, :], slot_f[:, :]))
                dve.wait_ge(ex_done, ONE + 1)
                chain(nc.vector.tensor_scalar(g1[:, :], g2[:, :], 1.0, None, ALU.add))
                chain(nc.vector.reciprocal(g1[:, :], g1[:, :]))
                chain(nc.vector.tensor_tensor(g2[:, :], g2[:, :], g1[:, :], ALU.mult))
                for g in (g1, g2):
                    chain(nc.vector.tensor_scalar(g[:, :], g[:, :], 1.0 / WSCALE, None, ALU.mult))

                for k in range(2):
                    for out, op, v in ((low, ALU.bitwise_and, TP - 1), (high, ALU.logical_shift_right, 7)):
                        chain(nc.vector.tensor_scalar(part_u[:, :], slot[k][:, :], v, None, op))
                        chain(nc.vector.tensor_copy(out[:, :], part_u[:, :]))
                    nc.vector.tensor_tensor(in_tile[k][:, :, :], count16[:, :].unsqueeze(1).broadcast_to([128, NT, TP]),
                                            low[:, :].unsqueeze(2).broadcast_to([128, NT, TP]), ALU.is_equal)\
                        .then_inc(hot, 1)
                    chain(nc.vector.tensor_tensor(of_tile[k][:, :, CK, :],
                                                  count16[:, 0:ST].unsqueeze(1).broadcast_to([128, NT, ST]),
                                                  high[:, :].unsqueeze(2).broadcast_to([128, NT, ST]), ALU.is_equal))
                    nc.vector.tensor_tensor(of_tile[k][:, :, CT, :], of_tile[k][:, :, CK, :],
                                            tile16[:, k * NT:(k + 1) * NT].unsqueeze(2).broadcast_to([128, NT, ST]),
                                            ALU.mult).then_inc(hot, 1)
                    nc.vector.tensor_scalar(of_tile[k][:, :, CP, :], of_tile[k][:, :, CK, :], cst[:, PI0:PI0 + 1], None,
                                            ALU.mult).then_inc(hot, 1)
                dve.wait_ge(met_part, ONE + 2)
                chain(nc.vector.tensor_copy(met[:, :, :], ps[:, 6, 0:3 * ST].rearrange("p (a i) -> p a i", a=3)))
                chain(nc.vector.scalar_tensor_tensor(ans[:, :], met[:, CT, :], float(TP), met[:, CP, :], ALU.mult, ALU.add))
                chain(nc.vector.tensor_scalar(over[:, :], ans[:, :], float(B * L), float(B * L), ALU.is_ge, ALU.mult))
                chain(nc.vector.tensor_tensor(over[:, :], ans[:, :], over[:, :], ALU.subtract))
                chain(nc.vector.memset(take[:, ST:ST + 2], 0))
                chain(nc.vector.tensor_copy(take[:, 0:ST], over[:, :]))
                chain(nc.vector.tensor_scalar(free[:, :], met[:, CK, :], -1.0, 1.0, ALU.mult, ALU.add))
                chain(nc.vector.tensor_tensor(free[:, :], free[:, :], cst[:, DM0:DM0 + ST], ALU.mult))
                chain(nc.vector.tensor_tensor(ans[:, :], ans[:, :], free[:, :], ALU.add))
                chain(nc.vector.tensor_copy(give[:, :], ans[:, :]))

            @block.scalar
            def _(act):
                with act.Fori(0, B // 2) as r:
                    for u in range(4):
                        t = 4 * r + u
                        act.wait_ge(x_t[u], ONE + r + 1)
                        act.wait_ge(sc_done[u], ONE + r)
                        nc.scalar.activation(xh[u][0:HC, :, :],
                                             ps[0:HC, u, 0:2 * TP].rearrange("p (h n) -> p h n", h=2), ACT.Copy)\
                            .then_inc(xh_done[u], 1)
                act.wait_ge(ex_in, ONE + 1)
                nc.scalar.activation(g2[:, :], g2[:, :], ACT.Exp).then_inc(ex_done, 1)

            @block.tensor
            def _(pe):
                with pe.Fori(0, B // 2) as r:
                    for u in range(4):
                        pe.wait_ge(xw_done[u], ONE + r + 1)
                        pe.wait_ge(xl_done[u], ONE + r)
                        for hf in range(2):
                            last = nc.tensor.transpose(ps[0:HC, u, hf * TP:(hf + 1) * TP],
                                                       xw[u][:, hf * HC:(hf + 1) * HC], ident)
                        last.then_inc(x_t[u], 1)
                    for u in range(4):
                        pe.wait_ge(xl_done[u], ONE + r + 1)
                        pe.wait_ge(sc_out[u], ONE + r)
                        k = 0
                        for hf in range(2):
                            for xs, gs in ((xh, gth), (xh, gtl), (xl, gth)):
                                last = nc.tensor.matmul(ps[:, 4 + u, 0:E], xs[u][0:HC + hf, hf, :],
                                                        gs[0:HC + hf, hf, :], start=(k == 0), stop=(k == 5))
                                k += 1
                        last.then_inc(sc_done[u], 1)
                pe.wait_ge(tk_done, ONE + 1)
                flat = taken[:, :, :].rearrange("p t e -> p (t e)")
                nc.tensor.matmul(ps[:, 4, 0:NT * E], tri[:, :], flat, start=True, stop=False, skip_group_check=True)
                for d in range(1, NT):
                    nc.tensor.matmul(ps[:, 4, d * E:NT * E], ones[:, :], flat[:, 0:(NT - d) * E], start=False,
                                     stop=(d == NT - 1), skip_group_check=True)
                for t in range(NT):
                    last = nc.tensor.matmul(ps[:, 5, 0:E], ones[:, :], taken[:, t, :], start=(t == 0),
                                            stop=(t == NT - 1))
                last.then_inc(rk_done, 1)
                for k in range(2):
                    pe.wait_ge(hot, ONE + 3 * k + 3)
                    for t in range(NT):
                        last = nc.tensor.matmul(ps[:, 6, 0:3 * ST], in_tile[k][:, t, :],
                                                of_tile[k][:, t, :, :].rearrange("p a i -> p (a i)"),
                                                start=(k == 0 and t == 0), stop=(k == 1 and t == NT - 1),
                                                skip_group_check=True)
                    last.then_inc(met_part, 1)

        HH = HID // 2
        HM = HB // 2
        row = [sb(f"row{u}", [128, C]) for u in range(2)]
        source = [sb(f"source{u}", [128, 1], u32) for u in range(2)]
        dest = [sb(f"dest{u}", [128, 1], u32) for u in range(2)]
        yo = [sb(f"yo{u}", [128, C]) for u in range(2)]
        scrap = sb("scrap", [1, 2])
        early_g = sb("early_g", [1, 1])
        hw = [sb(f"hw{u}", [128, 2, HH]) for u in range(2)]
        hh = [sb(f"hh{u}", [128, 2, HH], f16) for u in range(2)]
        hl = [sb(f"hl{u}", [128, 2, HH], f16) for u in range(2)]
        rw_ld = [ctx.enter_context(nc.semaphore(f"rw_ld{u}")) for u in range(2)]
        s_ysc = [ctx.enter_context(nc.semaphore(f"s_ysc{u}")) for u in range(2)]

        with nc.Block() as block:

            @block.tensor
            def _(pe):
                def transposes(u):
                    for hf in range(2):
                        last = nc.tensor.transpose(ps[0:HC, 4 + u, hf * TP:(hf + 1) * TP],
                                                   row[u][:, hf * HC:(hf + 1) * HC], ident)
                    last.then_inc(xs_t[u], 1)

                def expert(e):
                    return ([w[:, :, ds(e, 1), :].rearrange("p a e n -> p (a e) n") for w in (fch, fcl)],
                            [w[:, ds(e, 1), :].rearrange("p e n -> p (e n)") for w in (pjh, pjl, bpw)])

                def up(u, e, r):
                    wh, wl = e[0]
                    pe.wait_ge(xsl[u], ONE + r + 1)
                    pe.wait_ge(hw_done[u], ONE + 2 * r)
                    for m in range(HB):
                        k = 0
                        for hf in range(2):
                            K = HC + hf
                            for ws, xs in ((wh, xh), (wh, xl), (wl, xh)):
                                last = nc.tensor.matmul(
                                    ps[:, 2 * u + m // HM, (m % HM) * TP:(m % HM + 1) * TP],
                                    ws[0:K, hf, m * 128:(m + 1) * 128], xs[u][0:K, hf, :], start=(k == 0), stop=(k == 5))
                                k += 1
                        if m % HM == HM - 1:
                            last.then_inc(fc_done[u], 1)

                def down(u, e, r):
                    ph, pl, bias = e[1]
                    pe.wait_ge(ye_done[u], ONE + 2 * r)
                    y = ps[:, 6 + u, 0:C]
                    for m in range(HB):
                        if m % HM == 0:
                            pe.wait_ge(hl_done[u], ONE + 2 * r + m // HM + 1)
                        for k, (hs, ws) in enumerate(((hh, ph), (hh, pl), (hl, ph))):
                            nc.tensor.matmul(y, hs[u][:, m // HM, (m % HM) * TP:(m % HM + 1) * TP],
                                             ws[:, m * C:(m + 1) * C], start=(m == 0 and k == 0), stop=False)
                    nc.tensor.matmul(y, ones[0:2, :], bias, start=False,
                                     stop=True).then_inc(dn_done[u], 1)

                for u in range(2):
                    pe.wait_ge(rw_ld[u], 16)
                    transposes(u)
                with pe.Fori(0, ST // 4) as a:
                    for r in (2 * a, 2 * a + 1):
                        e = [pe.value_load(owner[0:1, ds(2 * r + u, 1)], min_val=0, max_val=E - 1) for u in range(2)]
                        e = [expert(i) for i in e]
                        for u in range(2):
                            up(u, e[u], r)
                        down(0, e[0], r)
                        for u in range(2):
                            pe.wait_ge(rw_ld[u], 16 * (r + 2))
                            transposes(u)
                        down(1, e[1], r)

            @block.scalar
            def _(act):
                def high(u):
                    nc.scalar.activation(xh[u][0:HC, :, :],
                                         ps[0:HC, 4 + u, 0:2 * TP].rearrange("p (h n) -> p h n", h=2), ACT.Copy)\
                        .then_inc(xsh[u], 1)

                nc.scalar.activation(early_g[:, :], eps_c[0:1, 0:1], ACT.Gelu_apprx_tanh)
                for u in range(2):
                    act.wait_ge(xs_t[u], ONE + 1)
                    high(u)
                with act.Fori(0, ST // 4) as a:
                    for r in (2 * a, 2 * a + 1):
                        for u in range(2):
                            for i in range(2):
                                act.wait_ge(fc_done[u], ONE + 2 * r + i + 1)
                                act.wait_ge(hl_done[u], ONE + 2 * r)
                                nc.scalar.activation(hw[u][:, i, :], ps[:, 2 * u + i, 0:HH], ACT.Gelu_apprx_tanh,
                                                     scale=1.0 / WSCALE).then_inc(hw_done[u], 1)
                        for u in range(2):
                            act.wait_ge(xs_t[u], ONE + r + 2)
                            high(u)

            @block.vector
            def _(dve):
                def low_x(u):
                    nc.vector.tensor_tensor(xl[u][0:HC, :, :],
                                            ps[0:HC, 4 + u, 0:2 * TP].rearrange("p (h n) -> p h n", h=2),
                                            xh[u][0:HC, :, :], ALU.subtract).then_inc(xsl[u], 1)

                for u in range(2):
                    nc.vector.tensor_copy(source[u][:, :], take[:, u:u + 1]).then_inc(src_in[u], 1)
                for u in range(2):
                    dve.wait_ge(xsh[u], ONE + 1)
                    low_x(u)
                with dve.Fori(0, ST // 4) as a:
                    for r in (2 * a, 2 * a + 1):
                        for u in range(2):
                            dve.wait_ge(rw_ld[u], 16 * (r + 1))
                            nc.vector.tensor_copy(source[u][:, :], take[:, ds(2 * (r + 1) + u, 1)])\
                                .then_inc(src_in[u], 1)
                        for u in range(2):
                            for i in range(2):
                                dve.wait_ge(hw_done[u], ONE + 2 * r + i + 1)
                                dve.wait_ge(dn_done[u], ONE + r)
                                nc.vector.tensor_copy(hh[u][:, i, :], hw[u][:, i, :]).then_inc(hh_done[u], 1)
                                dve.wait_ge(hh_done[u], ONE + 2 * r + i + 1)
                                nc.vector.tensor_tensor(hl[u][:, i, :], hw[u][:, i, :], hh[u][:, i, :], ALU.subtract)\
                                    .then_inc(hl_done[u], 1)
                        for u in range(2):
                            dve.wait_ge(y_free[u], ONE + r)
                            nc.vector.tensor_copy(dest[u][:, :], give[:, ds(2 * r + u, 1)]).then_inc(ye_done[u], 1)
                            dve.wait_ge(dn_done[u], ONE + r + 1)
                            nc.vector.tensor_copy(yo[u][:, :], ps[:, 6 + u, 0:C]).then_inc(ye_done[u], 1)
                            if u == 0:
                                for w in range(2):
                                    dve.wait_ge(xsh[w], ONE + r + 2)
                                    low_x(w)

            @block.gpsimd
            def _(pool):
                def gather(u):
                    nc.gpsimd.indirect_dma_start(row[u][:, :], None, d_x.rearrange("t p c -> (t p) c"),
                                                 bass.IndirectOffsetOnAxis(ap=source[u][:, :], axis=0))\
                        .then_inc(rw_ld[u], 16)

                for u in range(2):
                    pool.wait_ge(src_in[u], ONE + 1)
                    gather(u)
                with pool.Fori(0, ST // 2) as r:
                    for u in range(2):
                        by_constant(pool, r + 2, r + 1)
                        pool.wait_ge(src_in[u], ONE + r + 2)
                        pool.wait_ge(xs_t[u], ONE + r + 1)
                        gather(u)
                    for u in range(2):
                        by_constant(pool, 2 * r + 2)
                        pool.wait_ge(ye_done[u], ONE + 2 * r + 2)
                        nc.gpsimd.indirect_dma_start(d_y, bass.IndirectOffsetOnAxis(ap=dest[u][:, :], axis=0),
                                                     yo[u][:, :], None).then_inc(s_ysc[u], 16)
                    for u in range(2):
                        by_constant(pool, 16 * (r + 1) - ONE)
                        pool.wait_ge(s_ysc[u], 16 * (r + 1))
                        nc.gpsimd.memset(scrap[:, u:u + 1], 0.0).then_inc(y_free[u], 1)

        ya = [x_sb, sb("ya1", [128, NT, C])]

        with nc.Block() as block:

            def loads(eng, k):
                for i in range(NT // PT):
                    eng.dma_start(ya[k][:, i * PT:(i + 1) * PT, :],
                                  d_y[(k * NT + i * PT) * TP:(k * NT + (i + 1) * PT) * TP, :]
                                  .rearrange("(t p) c -> p t c", p=TP)).then_inc(ya_ld[i], 16)

            @block.sync
            def _(sp):
                loads(sp, 0)
                for i in range(NT // PT):
                    sp.wait_ge(s_add, ONE + 2 * i + 2)
                    sp.dma_start(out.rearrange("p (t c) -> p t c", t=NT)[:, i * PT:(i + 1) * PT, :],
                                 r_sb[:, i * PT:(i + 1) * PT, :]).then_inc(s_out, 16)
                sp.wait_ge(s_out, ONE + 16 * NT // PT)

            @block.scalar
            def _(act):
                loads(act, 1)

            @block.vector
            def _(dve):
                for i in range(NT // PT):
                    dve.wait_ge(ya_ld[i], ONE + 32)
                    for k, g in enumerate((g1, g2)):
                        dve.wait_ge(s_add, ONE + 2 * i + k)
                        for t in range(i * PT, (i + 1) * PT):
                            last = nc.vector.scalar_tensor_tensor(r_sb[:, t, :], ya[k][:, t, :], g[:, t:t + 1],
                                                                  r_sb[:, t, :], ALU.mult, ALU.add)
                        last.then_inc(s_add, 1)


def constants():
    import numpy as np
    p = np.arange(128)
    i, par = p % CH, p // CH % 2
    col = np.arange(2 * CH)
    same = par[:, None] == (col // CH)[None]
    t = np.zeros((128, CW), np.float32)
    t[:, ID0:ID0 + 128] = np.eye(128)
    t[:, MS0:MS0 + 32] = same & ((col % CH)[None] < i[:, None])
    t[:, MU0:MU0 + 32] = same & ((col % CH)[None] >= i[:, None])
    t[:, MP0:MP0 + 2] = par[:, None] == np.arange(2)[None]
    t[:, BM0:BM0 + HC] = (p // D)[:, None] == (np.arange(HC) // D)[None]
    t[:, TB0:TB0 + E] = E - np.arange(E)
    t[:, TR0:TR0 + TP] = p[:, None] < np.arange(TP)[None]
    t[:, TS0:TS0 + NT] = TP * np.arange(NT)
    t[:, EB0:EB0 + E * E] = (np.arange(E)[None] < np.arange(E)[:, None]).reshape(-1)
    t[:, IO0:IO0 + TP] = np.arange(TP)
    t[:, DI0:DI0 + 2 * NT] = np.arange(2 * NT)
    t[:, PI0] = p
    t[:, DM0:DM0 + ST] = 2 * NT * TP + TP * (np.arange(ST)[None] % 2) + p[:, None]
    return t


def kernel(**inputs):
    import numpy as np
    import concourse.bacc as bacc
    from concourse.bass_utils import run_bass_kernel_spmd

    a = {k: np.asarray(v) for k, v in inputs.items()}

    def halves(w):
        return np.ascontiguousarray(w.reshape(2, HC, -1).transpose(1, 0, 2).reshape(HC, -1))

    def halves_and_bias(w, bias):
        full = np.zeros((HC + 1, 2, w.shape[1]), w.dtype)
        full[:HC] = w.reshape(2, HC, -1).transpose(1, 0, 2)
        full[HC, 1] = bias
        return full

    by_head = lambda w: w.reshape(C, H, D)
    kv = np.concatenate([by_head(a["L0_conv_Wk"]), by_head(a["L0_conv_Wv"])], axis=2).reshape(C, KVW)
    wqkvb = np.concatenate([kv, a["L0_conv_Wq"], a["L0_conv_Wb"]], axis=1)
    tokens = a["x"].reshape(B, C, L).transpose(0, 2, 1).reshape(NT, TP, C)
    fc, pj = a["L0_ffn_w_fc"], a["L0_ffn_w_proj"]
    arrays = {
        "x": tokens.transpose(1, 0, 2).reshape(TP, NT * C),
        "consts": constants(),
        "wqkvb": halves(wqkvb),
        "wo": halves(a["L0_conv_Wo"]),
        "gate": halves_and_bias(a["L0_ffn_gate_w"].T, a["L0_ffn_gate_b"]).reshape(HC + 1, 2 * E),
        "wfc": np.stack([halves_and_bias(fc[e].T, a["L0_ffn_b_fc"][e]) for e in range(E)]),
        "wproj": pj.transpose(0, 2, 1).reshape(E, HB, 128, C).transpose(0, 2, 1, 3).reshape(E, 128, HB * C),
        "bproj": a["L0_ffn_b_proj"],
    }
    arrays = {k: np.ascontiguousarray(v) for k, v in arrays.items()}
    nc = bacc.Bacc("TRN2", target_bir_lowering=False, num_devices=1)
    f32 = mybir.dt.float32
    args = [nc.dram_tensor(k, v.shape, f32, kind="ExternalInput").ap() for k, v in arrays.items()]
    args.append(nc.dram_tensor("out", (TP, NT * C), f32, kind="ExternalOutput").ap())
    program(nc, *args)
    r = run_bass_kernel_spmd(nc, [arrays], core_ids=[0])
    o = r.results[0]["out"].reshape(TP, NT, C).transpose(1, 0, 2).reshape(B, L, C)
    return np.ascontiguousarray(o.transpose(0, 2, 1)).reshape(B, C, 16, 16)
```
